# Optimizing a Trainium2 kernel written in Bass

```python
import numpy as np
import jax
import jax.numpy as jnp

def _softmax(x, axis=-1):
    return jax.nn.softmax(x, axis=axis)

def _gelu(x):
    return jax.nn.gelu(x, approximate=True)

def _silu(x):
    return jax.nn.silu(x)

def _sigmoid(x):
    return jax.nn.sigmoid(x)

def _layernorm(x, axis=-1, eps=1e-05):
    m = jnp.mean(x, axis=axis, keepdims=True)
    v = jnp.var(x, axis=axis, keepdims=True)
    return (x - m) / jnp.sqrt(v + eps)

def _scatter_add(tgt, idx, src, axis=0):
    return tgt.at[idx].add(src)

def _segment_sum(src, seg, n):
    return jax.ops.segment_sum(src, seg, n)
kernel_name = 'mk_seq_preln_d1_jaxref_r8_029e04'

def setup_inputs(seed: int=0):
    np.random.seed(seed)
    _w = jnp.asarray

    def _L0_attn_setup():
        import jax, jax.numpy as jnp
        import numpy as np
        from jax import lax
        B, T, HID = (4, 128, 128)
        H, DK, DV = (8, 128, 128)
        KCONV = 4
        EPS = 1e-06
        KEY_DIM = H * DK
        VAL_DIM = H * DV
        CONV_DIM = 2 * KEY_DIM + VAL_DIM
        key = jax.random.key(seed)
        ks = jax.random.split(key, 11)
        s = 0.02
        return {'hidden_states': jax.random.normal(ks[0], (B, T, HID), jnp.float32), 'qkv_w': jax.random.normal(ks[1], (CONV_DIM, HID), jnp.float32) * s, 'z_w': jax.random.normal(ks[2], (VAL_DIM, HID), jnp.float32) * s, 'b_w': jax.random.normal(ks[3], (H, HID), jnp.float32) * s, 'a_w': jax.random.normal(ks[4], (H, HID), jnp.float32) * s, 'conv_w': jax.random.normal(ks[5], (CONV_DIM, 1, KCONV), jnp.float32) * 0.2, 'dt_bias': jnp.ones((H,), jnp.float32), 'A_log': jnp.log(jax.random.uniform(ks[6], (H,), jnp.float32, 0.001, 16.0)), 'norm_w': jnp.ones((DV,), jnp.float32), 'out_w': jax.random.normal(ks[7], (HID, VAL_DIM), jnp.float32) * s}
    _L0_attn_in = _L0_attn_setup()

    def _L0_ffn_setup():
        import jax, jax.numpy as jnp
        import numpy as np
        N_EMBD = 128
        NUM_EXPERTS = 8
        TOP_K = 2
        D_FF = 4 * N_EMBD
        B, S = (4, 256)
        key = jax.random.key(seed)
        ks = jax.random.split(key, 7)
        scale = lambda fan_in: 1.0 / np.sqrt(fan_in)
        x = jax.random.normal(ks[0], (B, S, N_EMBD), dtype=jnp.float32)
        W_router = jax.random.normal(ks[1], (N_EMBD, NUM_EXPERTS), dtype=jnp.float32) * scale(N_EMBD)
        b_router = jnp.zeros((NUM_EXPERTS,), dtype=jnp.float32)
        W1 = jax.random.normal(ks[2], (NUM_EXPERTS, N_EMBD, D_FF), dtype=jnp.float32) * scale(N_EMBD)
        b1 = jnp.zeros((NUM_EXPERTS, D_FF), dtype=jnp.float32)
        W2 = jax.random.normal(ks[3], (NUM_EXPERTS, D_FF, N_EMBD), dtype=jnp.float32) * scale(D_FF)
        b2 = jnpp = jnp.zeros((NUM_EXPERTS, N_EMBD), dtype=jnp.float32)
        return {'x': x, 'W_router': W_router, 'b_router': b_router, 'W1': W1, 'b1': b1, 'W2': W2, 'b2': b2}
    _L0_ffn_in = _L0_ffn_setup()
    _d = {'L0_attn_hidden_states': _L0_attn_in['hidden_states'], 'L0_attn_qkv_w': _L0_attn_in['qkv_w'], 'L0_attn_z_w': _L0_attn_in['z_w'], 'L0_attn_b_w': _L0_attn_in['b_w'], 'L0_attn_a_w': _L0_attn_in['a_w'], 'L0_attn_conv_w': _L0_attn_in['conv_w'], 'L0_attn_dt_bias': _L0_attn_in['dt_bias'], 'L0_attn_A_log': _L0_attn_in['A_log'], 'L0_attn_norm_w': _L0_attn_in['norm_w'], 'L0_attn_out_w': _L0_attn_in['out_w'], 'L0_ffn_W_router': _L0_ffn_in['W_router'], 'L0_ffn_b_router': _L0_ffn_in['b_router'], 'L0_ffn_W1': _L0_ffn_in['W1'], 'L0_ffn_b1': _L0_ffn_in['b1'], 'L0_ffn_W2': _L0_ffn_in['W2'], 'L0_ffn_b2': _L0_ffn_in['b2']}
    _x0 = _d['L0_attn_hidden_states']
    _d['L0_attn_hidden_states'] = jax.random.normal(jax.random.fold_in(jax.random.key(seed), 1), (2, 2048, 128), dtype=_x0.dtype)
    del _x0
    return _d

def reference(L0_attn_hidden_states, L0_attn_qkv_w, L0_attn_z_w, L0_attn_b_w, L0_attn_a_w, L0_attn_conv_w, L0_attn_dt_bias, L0_attn_A_log, L0_attn_norm_w, L0_attn_out_w, L0_ffn_W_router, L0_ffn_b_router, L0_ffn_W1, L0_ffn_b1, L0_ffn_W2, L0_ffn_b2):

    def _L0_attn_ref(hidden_states, qkv_w, z_w, b_w, a_w, conv_w, dt_bias, A_log, norm_w, out_w):
        import jax, jax.numpy as jnp
        import numpy as np
        from jax import lax
        B, T, HID = (4, 128, 128)
        H, DK, DV = (8, 128, 128)
        KCONV = 4
        EPS = 1e-06
        KEY_DIM = H * DK
        VAL_DIM = H * DV
        CONV_DIM = 2 * KEY_DIM + VAL_DIM
        b_, t_, _ = hidden_states.shape
        mixed = jnp.einsum('bth,ch->btc', hidden_states, qkv_w)
        x = mixed.transpose(0, 2, 1)
        x = lax.conv_general_dilated(x, conv_w, window_strides=(1,), padding=[(KCONV - 1, 0)], feature_group_count=CONV_DIM, dimension_numbers=('NCH', 'OIH', 'NCH'))
        mixed = x.transpose(0, 2, 1)
        z = jnp.einsum('bth,vh->btv', hidden_states, z_w).reshape(b_, t_, H, DV)
        bb = jnp.einsum('bth,nh->btn', hidden_states, b_w)
        aa = jnp.einsum('bth,nh->btn', hidden_states, a_w)
        q, k, v = jnp.split(mixed, 3, axis=-1)
        q = q.reshape(b_, t_, H, DK)
        k = k.reshape(b_, t_, H, DK)
        v = v.reshape(b_, t_, H, DV)
        beta = jax.nn.sigmoid(bb)
        g = -jnp.exp(A_log) * jax.nn.softplus(aa + dt_bias)
        alpha = jnp.exp(g)

        def step(S, inp):
            q_t, k_t, v_t, beta_t, alpha_t = inp
            S = S * alpha_t[..., None, None]
            kv = jnp.einsum('bhk,bhkv->bhv', k_t, S)
            S = S + jnp.einsum('bhk,bhv->bhkv', k_t, (v_t - kv) * beta_t[..., None])
            o_t = jnp.einsum('bhk,bhkv->bhv', q_t, S)
            return (S, o_t)
        qt = q.transpose(1, 0, 2, 3)
        kt = k.transpose(1, 0, 2, 3)
        vt = v.transpose(1, 0, 2, 3)
        bt = beta.transpose(1, 0, 2)
        at = alpha.transpose(1, 0, 2)
        S0 = jnp.zeros((b_, H, DK, DV), hidden_states.dtype)
        _, o = lax.scan(step, S0, (qt, kt, vt, bt, at))
        o = o.transpose(1, 0, 2, 3)
        var = jnp.mean(jnp.square(o), axis=-1, keepdims=True)
        o = o * lax.rsqrt(var + EPS) * norm_w
        o = o * (z * jax.nn.sigmoid(z))
        out = jnp.einsum('btv,hv->bth', o.reshape(b_, t_, VAL_DIM), out_w)
        return out

    def _L0_ffn_ref(x, W_router, b_router, W1, b1, W2, b2):
        import jax, jax.numpy as jnp
        import numpy as np
        N_EMBD = 128
        NUM_EXPERTS = 8
        TOP_K = 2
        D_FF = 4 * N_EMBD
        B, S = (4, 256)
        Bv, Sv, D = x.shape
        flat_x = x.reshape(-1, D)
        T = flat_x.shape[0]
        logits = flat_x @ W_router + b_router
        top_vals, top_idx = jax.lax.top_k(logits, TOP_K)
        neg_inf = jnp.full_like(logits, -jnp.inf)
        sparse_logits = neg_inf.at[jnp.arange(T)[:, None], top_idx].set(top_vals)
        router_weights = jax.nn.softmax(sparse_logits, axis=-1)
        final_output = jnp.zeros_like(flat_x)
        for e in range(NUM_EXPERTS):
            expert_mask = jnp.any(top_idx == e, axis=-1)
            h = jax.nn.relu(flat_x @ W1[e] + b1[e])
            y = h @ W2[e] + b2[e]
            w = router_weights[:, e] * expert_mask.astype(x.dtype)
            final_output = final_output + y * w[:, None]
        return final_output.reshape(Bv, Sv, D)
    x = L0_attn_hidden_states
    x = x + _L0_attn_ref(_layernorm(x, axis=-1), L0_attn_qkv_w, L0_attn_z_w, L0_attn_b_w, L0_attn_a_w, L0_attn_conv_w, L0_attn_dt_bias, L0_attn_A_log, L0_attn_norm_w, L0_attn_out_w)
    x = x + _L0_ffn_ref(_layernorm(x, axis=-1), L0_ffn_W_router, L0_ffn_b_router, L0_ffn_W1, L0_ffn_b1, L0_ffn_W2, L0_ffn_b2)
    return x

_drawn_inputs = setup_inputs


def setup_inputs(seed=0):
    import zlib

    import numpy as np

    out = dict(_drawn_inputs(seed))
    spreads = {'L0_attn_dt_bias': (1.0, 0.6),
     'L0_attn_norm_w': (1.0, 0.2),
     'L0_ffn_b_router': (0.0, 0.1),
     'L0_ffn_b1': (0.0, 0.1),
     'L0_ffn_b2': (0.0, 0.1)}
    factors = {'L0_attn_b_w': 4.75, 'L0_attn_a_w': 7.888, 'L0_attn_A_log': 5.937}
    for name, (base, spread) in spreads.items():
        noise = np.random.default_rng([zlib.crc32(name.encode()), seed]).standard_normal(out[name].shape)
        drawn = base * np.exp(spread * noise) if base else spread * noise
        out[name] = jnp.asarray(drawn.astype(out[name].dtype))
    for name, factor in factors.items():
        out[name] = (out[name] * factor).astype(out[name].dtype)
    return out
```

```python
import concourse.bass as bass
from concourse import mybir
from contextlib import ExitStack
import numpy as np


def preln_delta_moe_kernel(nc, x_in, qkv_t, z_t, ab_t, conv_w, dt_bias, a_log, norm_w, out_t,
                           router_w, router_b, w1, b1, w2, b2, eye, parity_eye, low_tri, keep_in, out):
    F32, F16, I32 = mybir.dt.float32, mybir.dt.float16, mybir.dt.int32
    ALU, ACT, AX = mybir.AluOpType, mybir.ActivationFunctionType, mybir.AxisListType
    ds = bass.ds

    B, T, D = x_in.shape
    H = ab_t.shape[1] // 2
    C = 128
    NCH = B * T // C
    GC = 2
    GT = GC * C
    NG = NCH // GC
    NT = qkv_t.shape[1] // 128
    TAPS = conv_w.shape[2]
    PAD = TAPS - 1
    W = GT + PAD
    U = 2
    HU = H // U
    BLK = 32
    NB = C // BLK
    NE = router_w.shape[1]
    FF = w1.shape[2]
    NF = FF // 128
    TW = 4
    WSCALE = 64.0
    RING = 4

    ctx = ExitStack()
    with ctx:
        ctx.enter_context(nc.allow_non_contiguous_dma("layout of blocks"))

        def sb(name, shape, dt=F32):
            return ctx.enter_context(nc.sbuf_tensor(name, shape, dt))

        def sem(name):
            return ctx.enter_context(nc.semaphore(name))

        x_sb = sb("x_sb", [128, NCH, D])
        xn_hi = sb("xn_hi", [128, B, PAD + T], F16)
        xn_lo = sb("xn_lo", [128, B, PAD + T], F16)
        wq_hi = sb("wq_hi", [128, NT * 128], F16)
        wq_lo = sb("wq_lo", [128, NT * 128], F16)
        wz_hi = sb("wz_hi", [128, H * 128], F16)
        wz_lo = sb("wz_lo", [128, H * 128], F16)
        wab_hi = sb("wab_hi", [128, 2 * H], F16)
        wab_lo = sb("wab_lo", [128, 2 * H], F16)
        ow = sb("ow", [128, H, D])
        ident = sb("ident", [128, 128])
        par_eye = sb("par_eye", [128, BLK // 2, BLK])
        tri = sb("tri", [128, NE, NE])
        keep = sb("keep", [128, NG])
        taps = sb("taps", [128, NT, TAPS])
        nw = sb("nw", [128, 1])
        dtb = sb("dtb", [128, H])
        alog = sb("alog", [128, H])
        nexp_a = sb("nexp_a", [128, H])
        beta = sb("beta", [128, NCH, H])
        neg_acum = sb("neg_acum", [128, NCH, H])
        kT = sb("kT", [128, H, GT])
        qT = sb("qT", [128, H, GT])
        vT = sb("vT", [128, H, GT])
        raw = sb("raw", [128, RING, 260])
        tapA = sb("tapA", [128, RING, GT])
        tapB = sb("tapB", [128, RING, GT])
        area = [sb(f"area{i}", [128, 2 * GC * H * C]) for i in range(4)]

        def part(i, k):
            n = GC * H * C
            return area[i][:, n * k:n * k + n].rearrange("p (g h c) -> p g h c", g=GC, h=H)
        alpha_b, acum_b = part(0, 0), part(0, 1)
        Nm, AT = part(1, 0), part(1, 1)
        kd, V = part(2, 0), part(2, 1)
        R, zg = part(3, 0), part(3, 1)
        beta_d = sb("beta_d", [128, H, C])
        decay = sb("decay", [128, GC, H, C])
        kd_scale = sb("kd_scale", [128, GC, H])
        a_end = sb("a_end", [128, GC, H])
        blkN = sb("blkN", [128, BLK, BLK])
        blkT = sb("blkT", [128, BLK // 2, BLK])
        T64 = sb("T64", [128, GC, H, 2 * BLK])
        T32 = T64[:, :, :, 0:BLK]
        Y32 = sb("Y32", [128, H, BLK])
        Y64 = sb("Y64", [128, H, 2 * BLK])
        prod = Y64[:, :, :].rearrange("p a b -> p (a b)").rearrange("p (a b) -> p a b", b=BLK)
        S = sb("S", [128, 2, H, 128])
        rhs = sb("rhs", [128, H, C])
        Us = sb("Us", [128, H, C])
        G = sb("G", [128, H, C])
        GTs = sb("GTs", [128, H, C])

        ssq = sb("ssq", [128, H])
        nac = sb("nac", [128, GC, H])
        rs = sb("rs", [128, 4, 32])
        bst_t = sb("bst_t", [128, TW, 6])
        mv_t = sb("mv_t", [128, TW, 2])
        ssq4 = GTs[:, 6, :].rearrange("p (a b) -> p a b", a=4)
        mx = sb("mx", [128, 2, TW])
        cmp = beta_d[:, 0:4, :].rearrange("p a b -> p (a b)").rearrange("p (k a b c) -> p k a b c", k=2, a=TW, b=NE)
        wts = GTs[:, 7, 0:TW * NE].rearrange("p (a b) -> p a b", b=NE)
        rw = sb("rw", [128, NE])
        rb = sb("rb", [128, NE])
        b1_sb = GTs[:, 5, 0:NE * NF].rearrange("p (a b) -> p a b", b=NF)
        b2_sb = GTs[:, 4, :]
        kflat = kT[:, :, :].rearrange("p a b -> p (a b)")
        qflat = qT[:, :, :].rearrange("p a b -> p (a b)")
        vflat = vT[:, :, :].rearrange("p a b -> p (a b)")
        ab = vflat[:, 1024:1024 + NCH * 2 * H].rearrange("p (c k) -> p c k", c=NCH)
        rows = AT[:, 0, 0:2, :]
        rows0 = AT[:, 0, 2:4, :]
        crow = AT[:, 0, 4:6, :]
        zrow = AT[:, 0, 6, :]
        alpha_t = kd[:, 0, 0:2, :].rearrange("p a b -> p (a b)")
        tmp = [kd[:, 1, 2 * i:2 * i + 2, :].rearrange("p a b -> p (a b)") for i in range(4)]
        xn = V[:, 0, 0:TW, :]
        bst = bst_t[:, :, :]
        mv = mv_t[:, :, :]

        pj = [ctx.enter_context(nc.psum_tensor(f"pj{i}", [128, 512], F32)) for i in range(2)]
        kx = [ctx.enter_context(nc.psum_tensor(f"kx{i}", [128, 512], F32)) for i in range(2)]
        rc = [ctx.enter_context(nc.psum_tensor(f"rc{i}", [128, 512], F32)) for i in range(2)]
        ob = [ctx.enter_context(nc.psum_tensor(f"ob{i}", [128, 512], F32)) for i in range(2)]

        def heads(bank):
            return bank[:, :].rearrange("p (h c) -> p h c", h=HU)

        scr_alpha = nc.dram_tensor("scr_alpha", (B, 128, C), F32, kind="Internal").ap()
        scr_acum = nc.dram_tensor("scr_acum", (B, 128, C), F32, kind="Internal").ap()
        scr_n = nc.dram_tensor("scr_n", (GC * NB * H, BLK, BLK), F32, kind="Internal").ap()
        scr_t = nc.dram_tensor("scr_t", (GC * NB * H, BLK, BLK), F32, kind="Internal").ap()
        alpha_rows = scr_alpha.rearrange("b (c h) t -> (b c) (h t)", h=H)
        acum_rows = scr_acum.rearrange("b (c h) t -> (b c) (h t)", h=H)

        def sems(names):
            return [sem(n) for n in names.split()]
        (s_const, s_x, s_wraw, s_whi, s_wsplit, s_zero, s_xn, s_xt, s_xhi, s_xlo, s_ab, s_abc, s_chain, s_nexp,
         s_gate_e, s_gate_u, s_g, s_alpha, s_arow, s_arow_sb, s_crow, s_ccol, s_ncum, s_scr) = sems(
            "s_const s_x s_wraw s_whi s_wsplit s_zero s_xn s_xt s_xhi s_xlo s_ab s_abc s_chain s_nexp "
            "s_gate_e s_gate_u s_g s_alpha s_arow s_arow_sb s_crow s_ccol s_ncum s_scr")
        proj_ready, raw_ready, prod_ready, sum_ready, conv_mid, conv_done = sems(
            "proj_ready raw_ready prod_ready sum_ready conv_mid conv_done")
        alpha_in, acum_in = sems("alpha_in0 alpha_in1"), sems("acum_in0 acum_in1")
        (diag_ready, decay_done, kk_ready, n_ready, ktr_ready, kd_ready, scale_ready, kq_ready, at_ready, aq_ready,
         vtr_ready, v_ready, z_mm, z_tanh, zg_ready) = sems(
            "diag_ready decay_done kk_ready n_ready ktr_ready kd_ready scale_ready kq_ready at_ready aq_ready "
            "vtr_ready v_ready z_mm z_tanh zg_ready")
        (n_out, blk_in, inv_step, inv_done, t_out, t_in, rdiag, y32_mm, y32_sb, r32_mm, r32_sb, y64_mm, y64_sb,
         r64_mm, R_ready) = sems(
            "n_out blk_in inv_step inv_done t_out t_in rdiag y32_mm y32_sb r32_mm r32_sb y64_mm y64_sb r64_mm R_ready")
        (ks_mm, rhs_ready, u_mm, u_ready, sd_mm, S_ready, o_mm, sq_done, rms_step, g_ready, gtr_mm, gt_ready, out_mm,
         x2_ready) = sems(
            "ks_mm rhs_ready u_mm u_ready sd_mm S_ready o_mm sq_done rms_step g_ready gtr_mm gt_ready out_mm x2_ready")
        (f_w1raw, f_w2, f_small, f_whi, f_wlo, f_chain, f_xt, f_xhi, f_xlo, f_lg, f_sub, f_exp, f_wt, f_wtsb, f_b2,
         f_acc, f_h_mm, f_relu, f_y_mm, f_y, f_out) = sems(
            "f_w1raw f_w2 f_small f_whi f_wlo f_chain f_xt f_xhi f_xlo f_lg f_sub f_exp f_wt f_wtsb f_b2 "
            "f_acc f_h_mm f_relu f_y_mm f_y f_out")

        block = ctx.enter_context(nc.Block())

        def rsqrt(dve, step, v, y, t):
            step(nc.vector.tensor_single_scalar(t.bitcast(I32), v.bitcast(I32), 1, ALU.arith_shift_right))
            step(nc.vector.tensor_scalar(y.bitcast(I32), t.bitcast(I32), -1.0, float(0x5F3759DF), ALU.mult, ALU.add))
            for _ in range(4):
                step(nc.vector.tensor_tensor(t, y, y, ALU.mult))
                step(nc.vector.scalar_tensor_tensor(out=t, in0=t, scalar=-0.5, in1=v, op0=ALU.mult, op1=ALU.mult))
                step(nc.vector.scalar_tensor_tensor(out=y, in0=t, scalar=1.5, in1=y, op0=ALU.add, op1=ALU.mult))
        RSQ = 14

        KX = {}
        for kind in ("kk", "ktr", "kq", "vtr", "gtr"):
            for c in range(GC):
                for u in range(U):
                    KX[kind, c, u] = len(KX)
        KX_ORDER = list(KX)
        KX_TAKEN = {"kk": n_ready, "ktr": kd_ready, "kq": at_ready, "vtr": v_ready, "gtr": gt_ready}
        HALVES = GC * U

        def kx_bank(kind, c, u):
            return kx[KX[kind, c, u] % 2]

        def wait_kx(pe, g, kind, c, u):
            n = KX[kind, c, u]
            if n >= 2:
                k0, c0, u0 = KX_ORDER[n - 2]
                pe.wait_ge(KX_TAKEN[k0], g * HALVES + U * c0 + u0 + 1)
            else:
                pe.wait_ge(gt_ready, g * HALVES + U * (GC - 1) + n + 1)

        order = [H + h for h in range(H)] + list(range(H)) + [2 * H + h for h in range(H)]
        conv_out = [(kT, h) for h in range(H)] + [(qT, h) for h in range(H)] + [(vT, h) for h in range(H)]
        KK_AT = {12: 0, 16: 1}
        SCAN_AT = {6: 0, 9: 1}
        INV_STEPS = 2 + 2 * (BLK - 1)
        RMS_STEPS = 1 + RSQ
        f32n = lambda v: float(np.float32(v))
        ATANH = [f32n(1.0 / (2 * k + 1)) for k in range(9)]

        def column(g, c):
            return g * GT + (g // (NG // B)) * PAD + PAD + C * c

        def xflat(t):
            return t[:, :, :].rearrange("p b t -> p (b t)")

        def xtile(t, i):
            return xflat(t)[:, ds(i * (TW * C) + (i // (T // (TW * C))) * PAD + PAD, TW * C)]

        def bc(ap, shape):
            return ap.to_broadcast(shape)

        def rc_bank(c, k):
            return rc[(7 * c + k) % 2]

        SCAN_D1 = 7
        CHAIN_PREP = (2 + RMS_STEPS) * (NCH // TW) + 19
        F_PER = 2 + RMS_STEPS + 9

        w2_sb = area[0][:, :].rearrange("p (e f d) -> p e f d", e=NE, f=NF)
        w1raw = area[1][:, :].rearrange("p (e n) -> p e n", e=NE)
        w1h = area[2][:, :].bitcast(F16)
        w1_hi = w1h[:, 0:NE * FF].rearrange("p (e n) -> p e n", e=NE)
        w1_lo = w1h[:, NE * FF:2 * NE * FF].rearrange("p (e n) -> p e n", e=NE)
        hbuf = area[3][:, :].rearrange("p (r f n) -> p r f n", r=2, f=NF)
        xn2 = G[:, 0:TW, :]
        acc = G[:, TW:2 * TW, :]
        x2T = rhs[:, 0:TW, :].rearrange("p a b -> p (a b)")
        x2_hi = Us[:, 0:2, :].rearrange("p a b -> p (a b)").bitcast(F16)
        x2_lo = Us[:, 2:4, :].rearrange("p a b -> p (a b)").bitcast(F16)
        wT = GTs[:, 0:TW, :].rearrange("p a b -> p (a b)")
        rt = [ssq4[:, k, :] for k in range(4)]

        @block.sync
        def _(sp):
            for dst, src in ((ident, eye), (par_eye, parity_eye), (tri, low_tri), (keep, keep_in),
                             (taps, conv_w.rearrange("(t p) o k -> p t (o k)", p=128)),
                             (nw, norm_w.rearrange("(p o) -> p o", o=1)),
                             (dtb, bc(dt_bias.rearrange("(o h) -> o h", o=1), [128, H])),
                             (alog, bc(a_log.rearrange("(o h) -> o h", o=1), [128, H]))):
                sp.dma_start(dst[tuple(slice(None) for _ in dst.shape)], src).then_inc(s_const, 16)
            xt = x_in.rearrange("b (c p) d -> p (b c) d", p=128)
            for i in range(4):
                sp.dma_start(x_sb[:, 8 * i:8 * i + 8, :], xt[:, 8 * i:8 * i + 8, :]).then_inc(s_x, 16)
            sp.dma_start(kflat, qkv_t[:, 0:2048]).then_inc(s_wraw, 16)
            sp.dma_start(qflat[:, 0:1024], qkv_t[:, 2048:3072]).then_inc(s_wraw, 16)
            sp.dma_start(qflat[:, 1024:2048], z_t).then_inc(s_wraw, 16)
            sp.dma_start(vflat[:, 0:16], ab_t).then_inc(s_wraw, 16)
            sp.dma_start(ow[:, :, :], out_t.rearrange("(h p) d -> p h d", p=128)).then_inc(s_wraw, 16)
            sp.wait_ge(s_crow, 1)
            sp.dma_start(scr_alpha.rearrange("b p t -> p b t"), rows0).then_inc(s_scr, 16)
            sp.dma_start(scr_acum.rearrange("b p t -> p b t"), crow).then_inc(s_scr, 16)
            sp.wait_ge(s_scr, 32)
            with sp.Fori(0, NG) as g:
                for c in range(GC):
                    sp.wait_ge(s_scr, 32)
                    sp.wait_ge(decay_done, g * GC + c + 1)
                    sp.dma_start(alpha_b[:, c, :, :].rearrange("p h t -> p (h t)"),
                                 bc(alpha_rows[ds(g * GC + c, 1), :], [128, H * C])).then_inc(alpha_in[c], 16)
                    sp.wait_ge(s_scr, 32)
                    sp.wait_ge(aq_ready, g * GC + c + 1)
                    sp.wait_ge(scale_ready, g * GC + c + 1)
                    sp.dma_start(acum_b[:, c, :, :].rearrange("p h t -> p (h t)"),
                                 bc(acum_rows[ds(g * GC + c, 1), :], [128, H * C])).then_inc(acum_in[c], 16)
                for c in range(GC):
                    sp.wait_ge(n_ready, g * HALVES + U * c + 2)
                    for b in range(NB):
                        q = (c * NB + b) * H
                        sp.dma_start(scr_n[q:q + H].rearrange("h i j -> i h j"),
                                     Nm[BLK * b:BLK * b + BLK, c, :, BLK * b:BLK * b + BLK]).then_inc(n_out, 16)
                sp.wait_ge(inv_done, g + 1)
                sp.wait_ge(n_out, g * (16 * GC * NB) + 16 * GC * NB)
                for par in range(2):
                    sp.dma_start(blkN[64 * par:64 * par + 64, :, :], scr_n).then_inc(blk_in, 16)
                sp.wait_ge(s_scr, 32)
                sp.wait_ge(inv_done, g + 2)
                for par in range(2):
                    sp.dma_start(scr_t.rearrange("q (a p) m -> p q a m", p=2)[par],
                                 blkT[64 * par:64 * par + 64, :, :]).then_inc(t_out, 16)
                sp.wait_ge(s_scr, 32)
                sp.wait_ge(t_out, g * 32 + 32)
                for c in range(GC):
                    for b in range(NB):
                        q = (c * NB + b) * H
                        r = slice(BLK * b, BLK * b + BLK)
                        dst = T64[r, c, :, r] if b < 2 else T32[r, c, :, :]
                        sp.dma_start(dst, scr_t[q:q + H].rearrange("h i j -> i h j")).then_inc(t_in, 16)
            sp.wait_ge(x2_ready, NCH + 1)
            for e in range(NE):
                sp.dma_start(w1raw[:, e, :], w1[e]).then_inc(f_w1raw, 16)
                sp.dma_start(w2_sb[:, e, :, :], w2[e].rearrange("(f p) d -> p f d", p=128)).then_inc(f_w2, 16)
            sp.dma_start(rw[:, :], router_w).then_inc(f_small, 16)
            sp.dma_start(rb[:, :], bc(router_b.rearrange("(o e) -> o e", o=1), [128, NE])).then_inc(f_small, 16)
            sp.dma_start(b1_sb[:, :, :], b1.rearrange("e (f p) -> p e f", p=128)).then_inc(f_small, 16)
            sp.dma_start(b2_sb[0:NE, :], b2).then_inc(f_small, 16)
            yt = out.rearrange("b (c p) d -> p (b c) d", p=128)
            with sp.Fori(0, NCH // TW) as i:
                sp.wait_ge(s_x, 64)
                sp.wait_ge(f_y, i * NE + NE + 1)
                sp.dma_start(yt[:, ds(i * TW, TW), :], x_sb[:, ds(i * TW, TW), :]).then_inc(f_out, 16)
            sp.wait_ge(f_out, 16 * (NCH // TW))

        @block.gpsimd
        def _(pool):
            nc.gpsimd.memset(T64[:, :, :, :], 0.0)
            nc.gpsimd.memset(R, 0.0)
            nc.gpsimd.memset(S[:, :, :, :], 0.0)
            nc.gpsimd.memset(xn_hi[:, :, 0:PAD], 0.0)
            nc.gpsimd.memset(xn_lo[:, :, 0:PAD], 0.0).then_inc(s_zero, 1)
            pool.sem_inc(aq_ready, GC)
            pool.wait_ge(s_const, 128)
            pool.wait_ge(s_g, 1)
            with pool.Fori(0, NG) as g:
                def diag(c):
                    pool.wait_ge(decay_done, g * GC + c + GC)
                    nc.gpsimd.tensor_tensor(
                        beta_d[:, :, :], bc(ident[:, :].rearrange("p (o c) -> p o c", o=1), [128, H, C]),
                        bc(beta[:, ds(g * GC + c, 1), :].rearrange("p o (h u) -> p (o h) u", u=1), [128, H, C]),
                        ALU.mult).then_inc(diag_ready, 1)
                diag(0)
                for n in range(NT):
                    pool.wait_ge(prod_ready, g * NT + n + 1)
                    nc.gpsimd.tensor_tensor(tapA[:, n % RING, :], tapA[:, n % RING, :], tapB[:, n % RING, :],
                                            ALU.add).then_inc(sum_ready, 1)
                    if n == SCAN_D1:
                        diag(1)
                for c in range(GC):
                    pool.wait_ge(acum_in[c], g * 16 + 16)
                    pool.wait_ge(kq_ready, g * HALVES + U * c + 2)
                    qc = qT[:, :, C * c:C * c + C]
                    nc.gpsimd.tensor_tensor(qc, qc, acum_b[:, c, :, :], ALU.mult).then_inc(aq_ready, 1)

        @block.scalar
        def _(act):
            act.wait_ge(s_wraw, 80)
            for dst, src in ((wq_hi[:, 0:2048], kflat), (wq_hi[:, 2048:3072], qflat[:, 0:1024]),
                             (wz_hi[:, :], qflat[:, 1024:2048]), (wab_hi[:, :], vflat[:, 0:16])):
                nc.scalar.activation(dst, src, ACT.Copy, scale=WSCALE).then_inc(s_whi, 1)
            act.wait_ge(s_const, 128)
            nc.scalar.activation(nexp_a[:, :], alog[:, :], ACT.Exp).then_inc(s_nexp, 1)
            with act.Fori(0, NCH // TW) as i:
                act.wait_ge(s_xt, i + 1)
                nc.scalar.activation(xtile(xn_hi, i), pj[0][:, :], ACT.Copy).then_inc(s_xhi, 1)
                act.wait_ge(s_ab, i + 1)
                nc.scalar.activation(ab[:, ds(i * TW, TW), :].rearrange("p a b -> p (a b)"), kx[0][:, 0:TW * 2 * H],
                                     ACT.Copy, scale=1.0 / WSCALE).then_inc(s_abc, 1)
            act.wait_ge(s_abc, NCH // TW)
            nc.scalar.activation(beta[:, :, :], ab[:, :, 0:H], ACT.Exp, scale=-1.0).then_inc(s_gate_e, 1)
            act.wait_ge(s_gate_u, 1)
            nc.scalar.activation(tmp[1], tmp[1], ACT.Exp, scale=-1.0).then_inc(s_gate_e, 1)
            act.wait_ge(s_g, 1)
            nc.scalar.activation(alpha_t, tmp[0], ACT.Exp, scale=-1.0).then_inc(s_alpha, 1)
            act.wait_ge(s_arow, 1)
            nc.scalar.activation(rows, pj[0][:, 0:256].rearrange("p (a b) -> p a b", a=2), ACT.Copy).then_inc(s_arow_sb, 1)
            act.wait_ge(s_ccol, 1)
            nc.scalar.activation(neg_acum[:, :, :].rearrange("p a b -> p (a b)"), pj[1][:, 0:256], ACT.Copy,
                                 scale=-1.0).then_inc(s_ncum, 1)
            act.sem_inc(gt_ready, HALVES)
            act.sem_inc(sq_done, U)

            with act.Fori(0, NG) as g:
                def evacuate(n):
                    act.wait_ge(proj_ready, g * NT + n + 1)
                    act.wait_ge(conv_done, g * NT + n + 1)
                    nc.scalar.activation(raw[:, n % RING, 0:W], pj[n % 2][:, 0:W], ACT.Copy,
                                         scale=1.0 / WSCALE).then_inc(raw_ready, 1)

                def products(n):
                    t = order[n]
                    act.wait_ge(raw_ready, g * NT + n + 1)
                    nc.scalar.activation(tapB[:, n % RING, :], raw[:, n % RING, 2:2 + GT], ACT.Copy,
                                         scale=taps[:, t, 2:3])
                    nc.scalar.activation(tapA[:, n % RING, :], raw[:, n % RING, 3:3 + GT], ACT.Copy,
                                         scale=taps[:, t, 3:4]).then_inc(prod_ready, 1)

                evacuate(0)
                for n in range(NT):
                    if n + 1 < NT:
                        evacuate(n + 1)
                    products(n)
                for c in range(GC):
                    for u in range(U):
                        act.wait_ge(vtr_ready, g * HALVES + U * c + u + 1)
                        nc.scalar.activation(V[:, c, HU * u:HU * u + HU, :], heads(kx_bank("vtr", c, u)),
                                             ACT.Copy).then_inc(v_ready, 1)
                for c in range(GC):
                    for u in range(U):
                        act.wait_ge(z_mm, g * HALVES + U * c + u + 1)
                        nc.scalar.activation(zg[:, c, HU * u:HU * u + HU, :], heads(pj[u]), ACT.Tanh,
                                             scale=0.5 / WSCALE).then_inc(z_tanh, 1)
                for c in range(GC):
                    act.wait_ge(y32_mm, g * GC + c + 1)
                    py = ob[0][:, 0:H * BLK].rearrange("p (h c) -> p h c", h=H)
                    nc.scalar.activation(Y32[96:128, :, :], py[96:128], ACT.Copy)
                    nc.scalar.activation(Y32[32:64, :, :], py[32:64], ACT.Copy).then_inc(y32_sb, 1)
                    act.wait_ge(r32_mm, g * GC + c + 1)
                    pr = ob[1][:, 0:H * BLK].rearrange("p (h c) -> p h c", h=H)
                    nc.scalar.activation(T64[32:64, c, :, 0:32], pr[32:64], ACT.Copy, scale=-1.0)
                    nc.scalar.activation(R[64:96, c, :, 96:128], pr[64:96], ACT.Copy, scale=-1.0)
                    nc.scalar.activation(R[0:32, c, :, 32:64], pr[0:32], ACT.Copy, scale=-1.0).then_inc(r32_sb, 1)
                    act.wait_ge(y64_mm, g * GC + c + 1)
                    nc.scalar.activation(Y64[64:128, :, :], ob[0][64:128, :].rearrange("p (h c) -> p h c", h=H),
                                         ACT.Copy).then_inc(y64_sb, 1)
                    act.wait_ge(r64_mm, g * GC + c + 1)
                    nc.scalar.activation(R[0:64, c, :, 64:128], ob[1][0:64, :].rearrange("p (h c) -> p h c", h=H),
                                         ACT.Copy, scale=-1.0).then_inc(R_ready, 1)
                for c in range(GC):
                    for u in range(U):
                        act.wait_ge(u_mm, g * HALVES + U * c + u + 1)
                        nc.scalar.activation(Us[:, HU * u:HU * u + HU, :], heads(rc_bank(c, 2 + u)),
                                             ACT.Copy).then_inc(u_ready, 1)
                    for u in range(U):
                        act.wait_ge(o_mm, g * HALVES + U * c + u + 1)
                        act.wait_ge(sq_done, g * HALVES + U * c + u + U)
                        for h in range(HU):
                            last = nc.scalar.activation(decay[:, c, HU * u + h, :], heads(ob[u])[:, h, :], ACT.Square,
                                                        accum_out=ssq[:, HU * u + h:HU * u + h + 1])
                        last.then_inc(sq_done, 1)
                    for u in range(U):
                        act.wait_ge(gtr_mm, g * HALVES + U * c + u + 1)
                        nc.scalar.activation(GTs[:, HU * u:HU * u + HU, :], heads(kx_bank("gtr", c, u)),
                                             ACT.Copy).then_inc(gt_ready, 1)
            for e in range(NE):
                act.wait_ge(f_w1raw, 16 * NE)
                nc.scalar.activation(w1_hi[:, e, :], w1raw[:, e, :], ACT.Copy, scale=WSCALE).then_inc(f_whi, 1)
            act.wait_ge(f_small, 64)
            with act.Fori(0, NCH // TW) as i:
                act.wait_ge(f_xt, i + 1)
                nc.scalar.activation(x2T[:, :], kx[0][:, :], ACT.Copy)
                nc.scalar.activation(x2_hi[:, :], kx[0][:, :], ACT.Copy).then_inc(f_xhi, 1)
                act.wait_ge(f_sub, i + 1)
                nc.scalar.activation(rt[2], rt[1], ACT.Exp).then_inc(f_exp, 1)
                for e in range(NE):
                    for f in range(NF):
                        act.wait_ge(f_h_mm, i * (NE * NF) + e * NF + f + 1)
                        if f == 0:
                            act.wait_ge(f_y_mm, i * NE + e + 1)
                        nc.scalar.activation(hbuf[:, e % 2, f, :], pj[f % 2][:, :], ACT.Relu, bias=b1_sb[:, e, f:f + 1],
                                             scale=1.0 / WSCALE).then_inc(f_relu, 1)
                    if e == 0:
                        act.wait_ge(f_wt, i + 1)
                        nc.scalar.activation(wT[0:NE, :], kx[1][0:NE, :], ACT.Copy).then_inc(f_wtsb, 1)

        @block.vector
        def _(dve):
            count = [0]

            def link(ins, base=0):
                count[0] += 1
                ins.then_inc(s_chain, 1)
                dve.wait_ge(s_chain, base + count[0])

            dve.wait_ge(s_wraw, 80)
            for k, (dst, src, hi) in enumerate(((wq_lo[:, 0:2048], kflat, wq_hi[:, 0:2048]),
                                                (wq_lo[:, 2048:3072], qflat[:, 0:1024], wq_hi[:, 2048:3072]),
                                                (wz_lo[:, :], qflat[:, 1024:2048], wz_hi[:, :]),
                                                (wab_lo[:, :], vflat[:, 0:16], wab_hi[:, :]))):
                dve.wait_ge(s_whi, k + 1)
                nc.vector.scalar_tensor_tensor(out=dst, in0=src, scalar=WSCALE, in1=hi, op0=ALU.mult, op1=ALU.subtract)
            dve.wait_ge(s_const, 128)
            nc.vector.tensor_scalar(ow[:, :, :], ow[:, :, :], nw[:, 0:1], 0.5 / WSCALE, ALU.mult,
                                    ALU.mult).then_inc(s_wsplit, 1)
            dve.wait_ge(s_x, 64)
            PER = 2 + RMS_STEPS

            def layernorm(i, dst, base):
                for j in range(TW):
                    ins = nc.vector.bn_stats(bst[:, j, :], x_sb[:, ds(i * TW + j, 1), :].rearrange("p a b -> p (a b)"))
                count[0] += 1
                ins.then_inc(s_chain, 1)
                dve.wait_ge(s_chain, base + count[0])
                nc.vector.memset(rs[:, 3, 0:1], 0.0)
                for j in range(TW):
                    ins = nc.vector.bn_aggr(mv[:, j, :], bst[:, j, :])
                link(ins, base)
                link(nc.vector.tensor_scalar_add(rs[:, 0, 0:TW], mv[:, :, 1], 1e-5), base)
                rsqrt(dve, lambda ins: link(ins, base), rs[:, 0, 0:TW], rs[:, 1, 0:TW], rs[:, 2, 0:TW])
                for j in range(TW):
                    ins = nc.vector.tensor_scalar(dst[:, j, :], x_sb[:, ds(i * TW + j, 1), :].rearrange("p a b -> p (a b)"),
                                                  mv[:, j, 0:1], rs[:, 1, j:j + 1], ALU.subtract, ALU.mult)
                return ins

            with dve.Fori(0, NCH // TW) as i:
                count[0] = 0
                layernorm(i, xn, i * PER).then_inc(s_xn, 1)
                assert count[0] == PER
                dve.wait_ge(s_xhi, i + 1)
                nc.vector.tensor_tensor(xtile(xn_lo, i), pj[0][:, :], xtile(xn_hi, i), ALU.subtract).then_inc(s_xlo, 1)
            count[0] = PER * (NCH // TW)
            v3 = lambda ap: ap.rearrange("p (c h) -> p c h", h=H)
            dve.wait_ge(s_abc, NCH // TW)
            link(nc.vector.tensor_tensor(v3(tmp[0]), ab[:, :, H:2 * H],
                                         bc(dtb[:, :].rearrange("p (o h) -> p o h", o=1), [128, NCH, H]), ALU.add))
            nc.vector.scalar_tensor_tensor(out=tmp[1], in0=tmp[0], scalar=-1.0, in1=tmp[0], op0=ALU.mult,
                                           op1=ALU.max).then_inc(s_gate_u, 1)
            dve.wait_ge(s_gate_e, 1)
            link(nc.vector.tensor_scalar_add(beta[:, :, :], beta[:, :, :], 1.0))
            link(nc.vector.reciprocal(beta[:, :, :], beta[:, :, :]))
            dve.wait_ge(s_gate_e, 2)
            link(nc.vector.tensor_scalar_add(tmp[2], tmp[1], 2.0))
            link(nc.vector.reciprocal(tmp[2], tmp[2]))
            link(nc.vector.tensor_tensor(tmp[1], tmp[1], tmp[2], ALU.mult))
            link(nc.vector.tensor_tensor(tmp[2], tmp[1], tmp[1], ALU.mult))
            link(nc.vector.tensor_scalar(tmp[3], tmp[2], ATANH[8], None, ALU.mult))
            for k in range(7, 0, -1):
                link(nc.vector.scalar_tensor_tensor(out=tmp[3], in0=tmp[3], scalar=ATANH[k], in1=tmp[2],
                                                    op0=ALU.add, op1=ALU.mult))
            link(nc.vector.scalar_tensor_tensor(out=tmp[3], in0=tmp[3], scalar=1.0, in1=tmp[1], op0=ALU.add, op1=ALU.mult))
            link(nc.vector.tensor_scalar(tmp[3], tmp[3], 2.0, None, ALU.mult))
            link(nc.vector.scalar_tensor_tensor(out=tmp[0], in0=tmp[0], scalar=0.0, in1=tmp[3], op0=ALU.max, op1=ALU.add))
            dve.wait_ge(s_nexp, 1)
            nc.vector.tensor_tensor(v3(tmp[0]), v3(tmp[0]),
                                    bc(nexp_a[:, :].rearrange("p (o h) -> p o h", o=1), [128, NCH, H]),
                                    ALU.mult).then_inc(s_g, 1)
            nc.vector.memset(zrow, 0.0)
            dve.wait_ge(s_arow_sb, 1)
            link(nc.vector.tensor_copy(rows0, rows))
            assert count[0] == CHAIN_PREP
            nc.vector.memset(rows0[:, :, 0:1], 0.0)
            nc.vector.tensor_tensor_scan(crow[:, 0, :], rows[:, 0, :], zrow, 1.0, ALU.mult, ALU.add)
            nc.vector.tensor_tensor_scan(crow[:, 1, :], rows[:, 1, :], zrow, 1.0, ALU.mult, ALU.add).then_inc(s_crow, 1)
            dve.wait_ge(s_scr, 32)
            dve.wait_ge(s_ncum, 1)
            dve.wait_ge(s_zero, 1)
            dve.sem_inc(decay_done, GC)
            dve.sem_inc(scale_ready, GC)
            dve.sem_inc(conv_done, RING)
            dve.sem_inc(zg_ready, HALVES)
            dve.sem_inc(inv_done, 1)
            dve.sem_inc(x2_ready, 1)
            dve.sem_inc(S_ready, U)
            dve.sem_inc(g_ready, U)

            with dve.Fori(0, NG) as g:
                def conv_first(n):
                    dve.wait_ge(sum_ready, g * NT + n + 1)
                    nc.vector.scalar_tensor_tensor(out=tapB[:, n % RING, :], in0=raw[:, n % RING, 1:1 + GT],
                                                   scalar=taps[:, order[n], 1:2], in1=tapA[:, n % RING, :],
                                                   op0=ALU.mult, op1=ALU.add).then_inc(conv_mid, 1)

                def conv_last(n):
                    dst, h = conv_out[n]
                    dve.wait_ge(conv_mid, g * NT + n + 1)
                    nc.vector.scalar_tensor_tensor(out=dst[:, h, :], in0=raw[:, n % RING, 0:GT],
                                                   scalar=taps[:, order[n], 0:1], in1=tapB[:, n % RING, :],
                                                   op0=ALU.mult, op1=ALU.add).then_inc(conv_done, 1)

                def scan(c):
                    dve.wait_ge(alpha_in[c], g * 16 + 16)
                    dve.wait_ge(diag_ready, g * GC + c + 1)
                    nc.vector.tensor_tensor_scan(decay[:, c, :, :].rearrange("p h c -> p (h c)"),
                                                 alpha_b[:, c, :, :].rearrange("p h c -> p (h c)"),
                                                 beta_d[:, :, :].rearrange("p h c -> p (h c)"),
                                                 0.0, ALU.mult, ALU.add).then_inc(decay_done, 1)

                def half(t, c, u):
                    return t[:, c, HU * u:HU * u + HU, :]

                def decayed_kk(c, u):
                    dve.wait_ge(kk_ready, g * HALVES + U * c + u + 1)
                    dve.wait_ge(decay_done, g * GC + c + 1 + GC)
                    nc.vector.tensor_tensor(half(Nm, c, u), heads(kx_bank("kk", c, u)), half(decay, c, u),
                                            ALU.mult).then_inc(n_ready, 1)

                conv_first(0)
                for n in range(NT):
                    if n + 1 < NT:
                        conv_first(n + 1)
                    conv_last(n)
                    if n in SCAN_AT:
                        scan(SCAN_AT[n])
                    if n in KK_AT:
                        for u in range(U):
                            decayed_kk(KK_AT[n], u)
                for c in range(GC):
                    dve.wait_ge(acum_in[c], g * 16 + 16)
                    end = keep[:, ds(g, 1)] if c == GC - 1 else 1.0
                    nc.vector.tensor_scalar(kd_scale[:, c, :], decay[:, c, :, C - 1], end, None, ALU.mult)
                    nc.vector.tensor_scalar(a_end[:, c, :], acum_b[:, c, :, C - 1], end, None, ALU.mult)
                    nc.vector.tensor_copy(nac[:, c, :], neg_acum[:, ds(g * GC + c, 1), :].rearrange("p a h -> p (a h)")
                                          ).then_inc(scale_ready, 1)
                for c in range(GC):
                    for u in range(U):
                        dve.wait_ge(ktr_ready, g * HALVES + U * c + u + 1)
                        dve.wait_ge(scale_ready, g * GC + c + 1 + GC)
                        sc = kd_scale[:, c, HU * u:HU * u + HU].rearrange("p (h o) -> p h o", o=1)
                        nc.vector.tensor_tensor(half(kd, c, u), heads(kx_bank("ktr", c, u)), bc(sc, [128, HU, C]),
                                                ALU.mult).then_inc(kd_ready, 1)
                for c in range(GC):
                    for u in range(U):
                        dve.wait_ge(kq_ready, g * HALVES + U * c + u + 1)
                        nc.vector.tensor_tensor(half(AT, c, u), heads(kx_bank("kq", c, u)), half(decay, c, u),
                                                ALU.mult).then_inc(at_ready, 1)
                for c in range(GC):
                    for u in range(U):
                        dve.wait_ge(z_tanh, g * HALVES + U * c + u + 1)
                        nc.vector.scalar_tensor_tensor(out=half(zg, c, u), in0=half(zg, c, u), scalar=1.0,
                                                       in1=heads(pj[u]), op0=ALU.add, op1=ALU.mult).then_inc(zg_ready, 1)
                steps = [0]

                def inv_link(ins):
                    steps[0] += 1
                    ins.then_inc(inv_step, 1)
                    dve.wait_ge(inv_step, g * INV_STEPS + steps[0])
                inv_link(nc.vector.tensor_copy(blkT[:, :, :], par_eye[:, :, :]))
                dve.wait_ge(blk_in, g * 32 + 32)
                inv_link(nc.vector.memset(blkN[:, :, :].rearrange("p a b -> p (a b)")[:, 0:BLK * BLK:BLK + 1], -1.0))
                for j in range(BLK - 2, -1, -1):
                    r0, wd = (j + 1) // 2, BLK - j
                    nr = BLK // 2 - r0
                    inv_link(nc.vector.tensor_tensor(prod[:, 0:nr, 0:wd], blkT[:, r0:, j:],
                                                     bc(blkN[:, j:j + 1, j:], [128, nr, wd]), ALU.mult))
                    red = nc.vector.tensor_reduce(blkT[:, r0:, j:j + 1], prod[:, 0:nr, 0:wd], AX.X, ALU.add, negate=True)
                    if j:
                        inv_link(red)
                    else:
                        red.then_inc(inv_done, 1)
                assert steps[0] == INV_STEPS - 1
                dve.sem_inc(inv_step, 1)
                dve.wait_ge(t_in, g * (16 * GC * NB) + 16 * GC * NB)
                for c in range(GC):
                    for b in range(NB):
                        r = slice(BLK * b, BLK * b + BLK)
                        ins = nc.vector.transpose(R[r, c, :, r], T64[r, c, :, r] if b < 2 else T32[r, c, :, :])
                    ins.then_inc(rdiag, 1)
                for c in range(GC):
                    for u in range(U):
                        dve.wait_ge(ks_mm, g * HALVES + U * c + u + 1)
                        dve.wait_ge(v_ready, g * HALVES + U * c + u + 1)
                        for h in range(HU):
                            hh = HU * u + h
                            ins = nc.vector.scalar_tensor_tensor(out=rhs[:, hh, :], in0=heads(rc_bank(c, u))[:, h, :],
                                                                 scalar=nac[:, c, hh:hh + 1], in1=V[:, c, hh, :],
                                                                 op0=ALU.mult, op1=ALU.add)
                        ins.then_inc(rhs_ready, 1)
                    for u in range(U):
                        dve.wait_ge(sd_mm, g * HALVES + U * c + u + 1)
                        for h in range(HU):
                            hh = HU * u + h
                            ins = nc.vector.scalar_tensor_tensor(out=S[:, 1 - c, hh, :], in0=S[:, c, hh, :],
                                                                 scalar=a_end[:, c, hh:hh + 1],
                                                                 in1=heads(rc_bank(c, 4 + u))[:, h, :],
                                                                 op0=ALU.mult, op1=ALU.add)
                        ins.then_inc(S_ready, 1)
                    dve.wait_ge(sq_done, g * HALVES + U * c + 2 + U)
                    rms = [0]

                    def rms_link(ins):
                        rms[0] += 1
                        ins.then_inc(rms_step, 1)
                        dve.wait_ge(rms_step, (g * GC + c) * RMS_STEPS + rms[0])
                    rms_link(nc.vector.tensor_scalar(rs[:, 0, 0:H], ssq[:, :], 1.0 / C, 1e-6, ALU.mult, ALU.add))
                    rsqrt(dve, rms_link, rs[:, 0, 0:H], rs[:, 1, 0:H], rs[:, 2, 0:H])
                    assert rms[0] == RMS_STEPS
                    for u in range(U):
                        for h in range(HU):
                            hh = HU * u + h
                            ins = nc.vector.scalar_tensor_tensor(out=G[:, hh, :], in0=heads(ob[u])[:, h, :],
                                                                 scalar=rs[:, 1, hh:hh + 1], in1=zg[:, c, hh, :],
                                                                 op0=ALU.mult, op1=ALU.mult)
                        ins.then_inc(g_ready, 1)
                    dve.wait_ge(out_mm, g * GC + c + 1)
                    xc = x_sb[:, ds(g * GC + c, 1), :].rearrange("p a d -> p (a d)")
                    nc.vector.tensor_tensor(xc, rc_bank(c, 6)[:, 0:D], xc, ALU.add).then_inc(x2_ready, 1)
            for e in range(NE):
                dve.wait_ge(f_whi, e + 1)
                nc.vector.scalar_tensor_tensor(out=w1_lo[:, e, :], in0=w1raw[:, e, :], scalar=WSCALE,
                                               in1=w1_hi[:, e, :], op0=ALU.mult, op1=ALU.subtract).then_inc(f_wlo, 1)
            dve.wait_ge(f_small, 64)
            dve.wait_ge(x2_ready, NCH + 1)
            dve.sem_inc(f_y, 1)
            base0 = CHAIN_PREP
            with dve.Fori(0, NCH // TW) as i:
                count[0] = 0
                base = i * F_PER + base0
                layernorm(i, xn2, base).then_inc(f_acc, 1)
                dve.wait_ge(f_xhi, i + 1)
                nc.vector.tensor_tensor(x2_lo[:, :], kx[0][:, :], x2_hi[:, :], ALU.subtract).then_inc(f_xlo, 1)
                lg, df, ex, wt = (r.rearrange("p (a b) -> p a b", b=NE) for r in rt)
                dve.wait_ge(f_lg, i + 1)
                link(nc.vector.tensor_tensor(lg, kx[1][:, 0:TW * NE].rearrange("p (a b) -> p a b", b=NE),
                                             bc(rb[:, :].rearrange("p (o e) -> p o e", o=1), [128, TW, NE]), ALU.add), base)
                link(nc.vector.tensor_reduce(mx[:, 0, :], lg, AX.X, ALU.max), base)
                col = lambda t: t.rearrange("p (a o) -> p a o", o=1)
                nc.vector.tensor_tensor(df, lg, bc(col(mx[:, 0, :]), [128, TW, NE]), ALU.subtract).then_inc(f_sub, 1)
                four = [128, TW, NE, NE]
                lj = bc(lg.rearrange("p a (o j) -> p a o j", o=1), four)
                le = bc(lg.rearrange("p a (e o) -> p a e o", o=1), four)
                nc.vector.tensor_tensor(cmp[:, 0], lj, le, ALU.is_gt)
                link(nc.vector.tensor_tensor(cmp[:, 1], lj, le, ALU.is_equal), base)
                link(nc.vector.tensor_tensor(cmp[:, 1], cmp[:, 1],
                                             bc(tri[:, :, :].rearrange("p (o e) j -> p o e j", o=1), four), ALU.mult), base)
                link(nc.vector.tensor_tensor(cmp[:, 0], cmp[:, 0], cmp[:, 1], ALU.add), base)
                link(nc.vector.tensor_reduce(lg, cmp[:, 0], AX.X, ALU.add), base)
                dve.wait_ge(f_exp, i + 1)
                link(nc.vector.scalar_tensor_tensor(out=wt, in0=lg, scalar=2.0, in1=ex, op0=ALU.is_lt, op1=ALU.mult), base)
                link(nc.vector.tensor_reduce(mx[:, 1, :], wt, AX.X, ALU.add), base)
                link(nc.vector.reciprocal(mx[:, 1, :], mx[:, 1, :]), base)
                dve.wait_ge(f_y, i * NE + 1)
                nc.vector.tensor_tensor(wts[:, :, :], wt, bc(col(mx[:, 1, :]), [128, TW, NE]), ALU.mult).then_inc(f_acc, 1)
                assert count[0] == F_PER
                dve.wait_ge(f_b2, i + 1)
                xs = x_sb[:, ds(i * TW, TW), :]
                nc.vector.tensor_tensor(acc[:, :, :], kx[0][:, :].rearrange("p (a b) -> p a b", b=D), xs,
                                        ALU.add).then_inc(f_acc, 1)
                for e in range(NE):
                    dve.wait_ge(f_y_mm, i * NE + e + 3)
                    if e == 0:
                        dve.wait_ge(f_acc, i * 3 + 3)
                    else:
                        dve.wait_ge(f_y, i * NE + e + 1)
                    dst = xs if e == NE - 1 else acc[:, :, :]
                    py = rc[e % 2][:, :].rearrange("p (a b) -> p a b", b=D)
                    for j in range(TW):
                        ins = nc.vector.scalar_tensor_tensor(
                            out=x_sb[:, ds(i * TW + j, 1), :].rearrange("p a d -> p (a d)") if e == NE - 1 else acc[:, j, :],
                            in0=py[:, j, :], scalar=wts[:, j, e:e + 1],
                            in1=acc[:, j, :], op0=ALU.mult, op1=ALU.add)
                    ins.then_inc(f_y, 1)

        @block.tensor
        def _(pe):
            mm, tr = nc.tensor.matmul, nc.tensor.transpose

            def carry(o):
                mm(o, wab_hi[:, :], wab_hi[:, :], start=True, stop=True)
            pe.wait_ge(s_const, 128)
            pe.wait_ge(s_wsplit, 1)
            with pe.Fori(0, NCH // TW) as i:
                pe.wait_ge(s_xn, i + 1)
                for j in range(TW):
                    ins = tr(pj[0][:, C * j:C * j + C], xn[:, j, :], ident[:, :])
                ins.then_inc(s_xt, 1)
                pe.wait_ge(s_xlo, i + 1)
                for j in range(TW):
                    hi = xtile(xn_hi, i)[:, C * j:C * j + C]
                    lo = xtile(xn_lo, i)[:, C * j:C * j + C]
                    o = kx[0][:, 2 * H * j:2 * H * j + 2 * H]
                    mm(o, hi, wab_hi[:, :], start=True, stop=False)
                    mm(o, hi, wab_lo[:, :], start=False, stop=False)
                    ins = mm(o, lo, wab_hi[:, :], start=False, stop=True)
                ins.then_inc(s_ab, 1)
            pe.wait_ge(s_alpha, 1)
            for b in range(B):
                ins = tr(pj[0][:, C * b:C * b + C], alpha_t[:, C * b:C * b + C], ident[:, :])
            ins.then_inc(s_arow, 1)
            pe.wait_ge(s_crow, 1)
            for b in range(B):
                ins = tr(pj[1][:, C * b:C * b + C], crow[:, b, :], ident[:, :])
            ins.then_inc(s_ccol, 1)
            pe.wait_ge(s_zero, 1)
            pe.wait_ge(s_ncum, 1)
            with pe.Fori(0, NG) as g:
                def project(n):
                    t = order[n]
                    if n >= 2:
                        pe.wait_ge(raw_ready, g * NT + n - 1)
                    else:
                        pe.wait_ge(zg_ready, g * HALVES + U * (GC - 1) + n + 1)
                    w = slice(128 * t, 128 * t + 128)
                    cols = ds(column(g, 0) - PAD, W)
                    o = pj[n % 2][:, 0:W]
                    mm(o, wq_hi[:, w], xflat(xn_hi)[:, cols], start=True, stop=False)
                    mm(o, wq_lo[:, w], xflat(xn_hi)[:, cols], start=False, stop=False)
                    mm(o, wq_hi[:, w], xflat(xn_lo)[:, cols], start=False, stop=True).then_inc(proj_ready, 1)

                def by_head(kind, c, u, lhs, rhs_, done, need):
                    pe.wait_ge(conv_done, g * NT + need + RING)
                    wait_kx(pe, g, kind, c, u)
                    for h in range(HU):
                        hh = HU * u + h
                        o = heads(kx_bank(kind, c, u))[:, h, :]
                        cs = slice(C * c, C * c + C)
                        if rhs_ is None:
                            ins = tr(o, lhs[:, hh, cs], ident[:, :])
                        else:
                            ins = mm(o, lhs[:, hh, cs], rhs_[:, hh, cs], start=True, stop=True)
                    ins.then_inc(done, 1)

                for n in range(NT):
                    if n in KK_AT:
                        for u in range(U):
                            by_head("kk", KK_AT[n], u, kT, kT, kk_ready, H)
                    project(n)
                for c in range(GC):
                    for u in range(U):
                        by_head("ktr", c, u, kT, None, ktr_ready, H)
                for c in range(GC):
                    for u in range(U):
                        by_head("kq", c, u, kT, qT, kq_ready, 2 * H)
                for c in range(GC):
                    for u in range(U):
                        by_head("vtr", c, u, vT, None, vtr_ready, 3 * H)
                for c in range(GC):
                    for u in range(U):
                        if c == 0:
                            pe.wait_ge(raw_ready, g * NT + NT - 1 + u)
                        else:
                            pe.wait_ge(zg_ready, g * HALVES + U * (c - 1) + u + 1 + HALVES)
                        cols = ds(column(g, c), C)
                        hi, lo = xflat(xn_hi)[:, cols], xflat(xn_lo)[:, cols]
                        w = slice(512 * u, 512 * u + 512)
                        mm(pj[u][:, :], hi, wz_hi[:, w], start=True, stop=False)
                        mm(pj[u][:, :], hi, wz_lo[:, w], start=False, stop=False)
                        mm(pj[u][:, :], lo, wz_hi[:, w], start=False, stop=True).then_inc(z_mm, 1)
                for c in range(GC):
                    k = g * GC + c
                    pe.wait_ge(t_in, g * (16 * GC * NB) + 16 * GC * NB)
                    if c == 0:
                        pe.wait_ge(rdiag, k + GC)
                    else:
                        pe.wait_ge(R_ready, k)
                    carry(ob[0][0:2 * H, 0:2 * H])
                    py = ob[0][:, 0:H * BLK].rearrange("p (h c) -> p h c", h=H)
                    for h in range(H):
                        mm(py[32:64, h], Nm[0:32, c, h, 32:64], T64[0:32, c, h, 0:32], start=True, stop=True)
                        ins = mm(py[96:128, h], Nm[64:96, c, h, 96:128], T32[64:96, c, h, :], start=True, stop=True)
                    ins.then_inc(y32_mm, 1)
                    pe.wait_ge(y32_sb, k + 1)
                    carry(ob[1][96:96 + 2 * H, 0:2 * H])
                    pr = ob[1][:, 0:H * BLK].rearrange("p (h c) -> p h c", h=H)
                    for h in range(H):
                        mm(pr[0:32, h], Y32[32:64, h, :], R[32:64, c, h, 32:64], start=True, stop=True)
                        mm(pr[32:64, h], R[32:64, c, h, 32:64], Y32[32:64, h, :], start=True, stop=True)
                        ins = mm(pr[64:96, h], Y32[96:128, h, :], R[96:128, c, h, 96:128], start=True, stop=True)
                    ins.then_inc(r32_mm, 1)
                    pe.wait_ge(r32_sb, k + 1)
                    carry(ob[0][0:2 * H, 0:2 * H])
                    py = ob[0][64:128, :].rearrange("p (h c) -> p h c", h=H)
                    for h in range(H):
                        ins = mm(py[:, h], Nm[0:64, c, h, 64:128], T64[0:64, c, h, :], start=True, stop=True)
                    ins.then_inc(y64_mm, 1)
                    pe.wait_ge(y64_sb, k + 1)
                    carry(ob[1][96:96 + 2 * H, 0:2 * H])
                    pr = ob[1][0:64, :].rearrange("p (h c) -> p h c", h=H)
                    for h in range(H):
                        ins = mm(pr[:, h], Y64[64:128, h, :], R[64:128, c, h, 64:128], start=True, stop=True)
                    ins.then_inc(r64_mm, 1)
                pe.wait_ge(R_ready, g * GC + GC)
                for c in range(GC):
                    cs = slice(C * c, C * c + C)
                    for u in range(U):
                        pe.wait_ge(S_ready, g * HALVES + U * c + u + 1)
                        if u == 1:
                            pe.wait_ge(x2_ready, g * GC + c + 1)
                        for h in range(HU):
                            hh = HU * u + h
                            ins = mm(heads(rc_bank(c, u))[:, h, :], kT[:, hh, cs], S[:, c, hh, :], start=True, stop=True)
                        ins.then_inc(ks_mm, 1)
                    for u in range(U):
                        pe.wait_ge(rhs_ready, g * HALVES + U * c + u + 1)
                        for h in range(HU):
                            hh = HU * u + h
                            ins = mm(heads(rc_bank(c, 2 + u))[:, h, :], R[:, c, hh, :], rhs[:, hh, :], start=True, stop=True)
                        ins.then_inc(u_mm, 1)
                    for u in range(U):
                        pe.wait_ge(u_ready, g * HALVES + U * c + u + 1)
                        pe.wait_ge(kd_ready, g * HALVES + U * c + u + 1)
                        for h in range(HU):
                            hh = HU * u + h
                            ins = mm(heads(rc_bank(c, 4 + u))[:, h, :], kd[:, c, hh, :], Us[:, hh, :], start=True, stop=True)
                        ins.then_inc(sd_mm, 1)
                    for u in range(U):
                        pe.wait_ge(aq_ready, g * GC + c + 1 + GC)
                        pe.wait_ge(at_ready, g * HALVES + U * c + u + 1)
                        pe.wait_ge(g_ready, g * HALVES + U * c + u + 1)
                        for h in range(HU):
                            hh = HU * u + h
                            o = heads(ob[u])[:, h, :]
                            mm(o, qT[:, hh, cs], S[:, c, hh, :], start=True, stop=False)
                            ins = mm(o, AT[:, c, hh, :], Us[:, hh, :], start=False, stop=True)
                        ins.then_inc(o_mm, 1)
                    for u in range(U):
                        pe.wait_ge(g_ready, g * HALVES + U * c + u + 1 + U)
                        wait_kx(pe, g, "gtr", c, u)
                        for h in range(HU):
                            ins = tr(heads(kx_bank("gtr", c, u))[:, h, :], G[:, HU * u + h, :], ident[:, :])
                        ins.then_inc(gtr_mm, 1)
                    pe.wait_ge(gt_ready, g * HALVES + U * c + 2 + HALVES)
                    pe.wait_ge(S_ready, g * HALVES + U * c + 1 + U)
                    for hh in range(H):
                        ins = mm(rc_bank(c, 6)[:, 0:D], GTs[:, hh, :], ow[:, hh, :], start=(hh == 0), stop=(hh == H - 1))
                    ins.then_inc(out_mm, 1)
            pe.wait_ge(f_small, 64)
            pe.wait_ge(f_w2, 16 * NE)
            pe.wait_ge(f_wlo, NE)
            pe.sem_inc(f_y_mm, 2)
            with pe.Fori(0, NCH // TW) as i:
                pe.wait_ge(f_acc, i * 3 + 1)
                for j in range(TW):
                    ins = tr(kx[0][:, C * j:C * j + C], xn2[:, j, :], ident[:, :])
                ins.then_inc(f_xt, 1)
                pe.wait_ge(f_xlo, i + 1)
                for j in range(TW):
                    ins = mm(kx[1][:, NE * j:NE * j + NE], x2T[:, C * j:C * j + C], rw[:, :], start=True, stop=True)
                ins.then_inc(f_lg, 1)

                def up(e):
                    for f in range(NF):
                        n = e * NF + f
                        if n >= 2:
                            pe.wait_ge(f_relu, i * (NE * NF) + n - 1)
                        w = slice(128 * f, 128 * f + 128)
                        mm(pj[f % 2][:, :], w1_hi[:, e, w], x2_hi[:, :], start=True, stop=False)
                        mm(pj[f % 2][:, :], w1_lo[:, e, w], x2_hi[:, :], start=False, stop=False)
                        mm(pj[f % 2][:, :], w1_hi[:, e, w], x2_lo[:, :], start=False, stop=True).then_inc(f_h_mm, 1)

                def down(e):
                    pe.wait_ge(f_relu, i * (NE * NF) + e * NF + NF)
                    if e >= 2:
                        pe.wait_ge(f_y, i * NE + e)
                    for j in range(TW):
                        for f in range(NF):
                            ins = mm(rc[e % 2][:, D * j:D * j + D], hbuf[:, e % 2, f, C * j:C * j + C],
                                     w2_sb[:, e, f, :], start=(f == 0), stop=(f == NF - 1))
                    ins.then_inc(f_y_mm, 1)

                up(0)
                pe.wait_ge(f_acc, i * 3 + 2)
                for j in range(TW):
                    ins = tr(kx[1][0:NE, C * j:C * j + C], wts[:, j, :], ident[:, :])
                ins.then_inc(f_wt, 1)
                pe.wait_ge(f_wtsb, i + 1)
                for j in range(TW):
                    ins = mm(kx[0][:, D * j:D * j + D], wT[0:NE, C * j:C * j + C], b2_sb[0:NE, :], start=True, stop=True)
                ins.then_inc(f_b2, 1)
                for e in range(NE):
                    if e + 1 < NE:
                        up(e + 1)
                    down(e)


def kernel(**inputs):
    import concourse.bacc as _bacc
    from concourse.bass_utils import run_bass_kernel_spmd as _run

    a = {k.replace("L0_", ""): np.asarray(v) for k, v in inputs.items()}
    t = lambda m: np.ascontiguousarray(m.T)
    NGROUPS, PER = 16, 8
    blk = 32
    par = np.zeros((2, 64, blk // 2, blk), np.float32)
    for p in range(2):
        for r in range(blk // 2):
            par[p, :, r, 2 * r + p] = 1.0
    keep = np.ones((128, NGROUPS), np.float32)
    keep[:, PER - 1::PER] = 0.0
    tri = np.broadcast_to(np.tril(np.ones((8, 8), np.float32), -1), (128, 8, 8))
    laid = [
        ("x", a["attn_hidden_states"]),
        ("qkv_t", t(a["attn_qkv_w"])),
        ("z_t", t(a["attn_z_w"])),
        ("ab_t", np.ascontiguousarray(np.concatenate([a["attn_b_w"], a["attn_a_w"]], 0).T)),
        ("conv_w", a["attn_conv_w"]),
        ("dt_bias", a["attn_dt_bias"]),
        ("a_log", a["attn_A_log"]),
        ("norm_w", a["attn_norm_w"]),
        ("out_t", t(a["attn_out_w"])),
        ("router_w", a["ffn_W_router"]),
        ("router_b", a["ffn_b_router"]),
        ("w1", a["ffn_W1"]),
        ("b1", a["ffn_b1"]),
        ("w2", a["ffn_W2"]),
        ("b2", a["ffn_b2"]),
        ("eye", np.eye(128, dtype=np.float32)),
        ("parity_eye", np.ascontiguousarray(par.reshape(128, blk // 2, blk))),
        ("low_tri", np.ascontiguousarray(tri)),
        ("keep", keep),
    ]
    nc = _bacc.Bacc("TRN2", target_bir_lowering=False, num_devices=1)
    arrays, args = {}, []
    for name, v in laid:
        v = np.ascontiguousarray(v)
        arrays[f"in_{name}"] = v
        args.append(nc.dram_tensor(f"in_{name}", v.shape, mybir.dt.from_np(v.dtype), kind="ExternalInput").ap())
    shape = a["attn_hidden_states"].shape
    args.append(nc.dram_tensor("out_0", shape, mybir.dt.float32, kind="ExternalOutput").ap())
    preln_delta_moe_kernel(nc, *args)
    r = _run(nc, [arrays], core_ids=[0])
    return r.results[0]["out_0"]
```

```python
import concourse.bass as bass
from concourse import mybir
from contextlib import ExitStack
import numpy as np


def preln_delta_moe_kernel(nc, x_in, qkv_t, z_t, ab_t, conv_w, dt_bias, a_log, norm_w, out_t,
                           router_w, router_b, w1, b1, w2, b2, eye, parity_eye, low_tri, keep_in, out):
    F32, F16, I32 = mybir.dt.float32, mybir.dt.float16, mybir.dt.int32
    ALU, ACT, AX = mybir.AluOpType, mybir.ActivationFunctionType, mybir.AxisListType
    ds = bass.ds

    B, T, D = x_in.shape
    H = ab_t.shape[1] // 2
    C = 128
    NCH = B * T // C
    GC = 2
    GT = GC * C
    NG = NCH // GC
    NT = qkv_t.shape[1] // 128
    TAPS = conv_w.shape[2]
    PAD = TAPS - 1
    W = GT + PAD
    U = 2
    HU = H // U
    BLK = 32
    NB = C // BLK
    NE = router_w.shape[1]
    FF = w1.shape[2]
    NF = FF // 128
    TW = 4
    WSCALE = 64.0
    AHEAD = 4
    RING = AHEAD + 2
    TAPB = 3

    ctx = ExitStack()
    with ctx:
        ctx.enter_context(nc.allow_non_contiguous_dma("layout of blocks"))

        def sb(name, shape, dt=F32):
            return ctx.enter_context(nc.sbuf_tensor(name, shape, dt))

        def sem(name):
            return ctx.enter_context(nc.semaphore(name))

        xn_hi = sb("xn_hi", [128, B, PAD + T], F16)
        xn_lo = sb("xn_lo", [128, B, PAD + T], F16)
        wq_hi = sb("wq_hi", [128, NT * 128], F16)
        wq_lo = sb("wq_lo", [128, NT * 128], F16)
        wz_hi = sb("wz_hi", [128, H * 128], F16)
        wz_lo = sb("wz_lo", [128, H * 128], F16)
        wab_hi = sb("wab_hi", [128, 2 * H], F16)
        wab_lo = sb("wab_lo", [128, 2 * H], F16)
        ow = sb("ow", [128, H, D])
        ident = sb("ident", [128, 128])
        par_eye = sb("par_eye", [128, BLK // 2, BLK], F16)
        tri = sb("tri", [128, NE, NE])
        keep = sb("keep", [128, NG])
        taps = sb("taps", [128, NT, TAPS])
        nw = sb("nw", [128, 1])
        dtb = sb("dtb", [128, H])
        alog = sb("alog", [128, H])
        nexp_a = sb("nexp_a", [128, H])
        beta = sb("beta", [128, NCH, H])
        neg_acum = sb("neg_acum", [128, NCH, H])
        kq = sb("kq", [128, 2, 2, H, GT])
        kT = [kq[:, p, 0] for p in range(2)]
        qT = [kq[:, p, 1] for p in range(2)]
        xres = sb("xres", [128, GC, D])
        vT = sb("vT", [128, H, GT])
        raw = sb("raw", [128, RING, 260])
        tapA = sb("tapA", [128, RING, GT])
        area = [sb(f"area{i}", [128, 2 * GC * H * C]) for i in range(4)]

        def part(i, k):
            n = GC * H * C
            return area[i][:, n * k:n * k + n].rearrange("p (g h c) -> p g h c", g=GC, h=H)
        alpha_b = part(0, 0)[:, 0]
        tapB = part(0, 0)[:, 1].rearrange("p h c -> p (h c)")[:, 0:TAPB * GT].rearrange("p (r t) -> p r t", r=TAPB)
        acum_b = part(0, 1)
        Nm, AT = part(1, 0), part(1, 1)
        kd, V = part(2, 0), part(2, 1)
        R, zg = part(3, 0), part(3, 1)
        beta_d = sb("beta_d", [128, H, C])
        decay = sb("decay", [128, GC, H, C])
        kd_scale = sb("kd_scale", [128, GC, H])
        a_end = sb("a_end", [128, GC, H])
        blkN = sb("blkN", [128, BLK, BLK])
        blkT = sb("blkT", [128, BLK // 2, BLK])
        T64 = sb("T64", [128, GC, H, 2 * BLK])
        T32 = T64[:, :, :, 0:BLK]
        Y32 = [sb("Y32", [128, H, BLK])[:, :, :]]
        Y64 = [sb("Y64", [128, H, 2 * BLK])[:, :, :]]
        prod = Y64[0].rearrange("p a b -> p (a b)").rearrange("p (a b) -> p a b", b=BLK)
        S = sb("S", [128, 2, H, 128])
        rhs = sb("rhs", [128, H, C])
        Us = sb("Us", [128, H, C])
        G = sb("G", [128, H, C])
        GTs = sb("GTs", [128, H, C])
        Y32.append(GTs[:, 4:6, :].rearrange("p a b -> p (a b)").rearrange("p (h c) -> p h c", h=H))
        Y64.append(GTs[:, 0:4, :].rearrange("p a b -> p (a b)").rearrange("p (h c) -> p h c", h=H))

        ssq = sb("ssq", [128, H])
        nac = sb("nac", [128, GC, H])
        rs = sb("rs", [128, 4, H])
        bst_t = sb("bst_t", [128, TW, 6])
        mv_t = sb("mv_t", [128, TW, 2])
        ssq4 = GTs[:, 6, :].rearrange("p (a b) -> p a b", a=4)
        mx = sb("mx", [128, 2, TW])
        cmp = beta_d[:, 0:4, :].rearrange("p a b -> p (a b)").rearrange("p (k a b c) -> p k a b c", k=2, a=TW, b=NE)
        wts = GTs[:, 7, 0:TW * NE].rearrange("p (a b) -> p a b", b=NE)
        rw = sb("rw", [128, NE])
        rb = sb("rb", [128, NE])
        b1_sb = GTs[:, 5, 0:NE * NF].rearrange("p (a b) -> p a b", b=NF)
        b2_sb = GTs[:, 4, :]
        kflat = kT[0].rearrange("p a b -> p (a b)")
        qflat = qT[0].rearrange("p a b -> p (a b)")
        x_sb = kq[:, 1].rearrange("p k h t -> p (k h t)").rearrange("p (c d) -> p c d", d=D)
        vflat = vT[:, :, :].rearrange("p a b -> p (a b)")
        ab = vflat[:, 1024:1024 + NCH * 2 * H].rearrange("p (c k) -> p c k", c=NCH)
        rows = AT[:, 0, 0:2, :]
        rows0 = AT[:, 0, 2:4, :]
        crow = AT[:, 0, 4:6, :]
        zrow = AT[:, 0, 6, :]
        alpha_t = kd[:, 0, 0:2, :].rearrange("p a b -> p (a b)")
        tmp = [kd[:, 1, 2 * i:2 * i + 2, :].rearrange("p a b -> p (a b)") for i in range(4)]
        par_eye32 = AT[:, 1, 0:4, :].rearrange("p h c -> p (h c)").rearrange("p (a b) -> p a b", b=BLK)
        xn = V[:, 0, 0:TW, :]
        bst = bst_t[:, :, :]
        mv = mv_t[:, :, :]

        pj = [ctx.enter_context(nc.psum_tensor(f"pj{i}", [128, 512], F32)) for i in range(2)]
        kx = [ctx.enter_context(nc.psum_tensor(f"kx{i}", [128, 512], F32)) for i in range(2)]
        rc = [ctx.enter_context(nc.psum_tensor(f"rc{i}", [128, 512], F32)) for i in range(2)]
        ob = [ctx.enter_context(nc.psum_tensor(f"ob{i}", [128, 512], F32)) for i in range(2)]

        merge_banks = [ob, kx]

        def heads(bank):
            return bank[:, :].rearrange("p (h c) -> p h c", h=HU)

        scr_alpha = nc.dram_tensor("scr_alpha", (B, 128, C), F32, kind="Internal").ap()
        scr_acum = nc.dram_tensor("scr_acum", (B, 128, C), F32, kind="Internal").ap()
        scr_x2 = nc.dram_tensor("scr_x2", (128, NCH, D), F32, kind="Internal").ap()
        scr_n = nc.dram_tensor("scr_n", (GC * NB * H, BLK, BLK), F32, kind="Internal").ap()
        scr_t = nc.dram_tensor("scr_t", (GC * NB * H, BLK, BLK), F32, kind="Internal").ap()
        alpha_rows = scr_alpha.rearrange("b (c h) t -> (b c) (h t)", h=H)
        acum_rows = scr_acum.rearrange("b (c h) t -> (b c) (h t)", h=H)

        def sems(names):
            return [sem(n) for n in names.split()]
        (s_const, s_x, s_wraw, s_whi, s_wsplit, s_zero, s_xn, s_xt, s_xhi, s_xlo, s_ab, s_abc, s_chain, s_nexp,
         s_gate_e, s_gate_u, s_g, s_alpha, s_arow, s_arow_sb, s_crow, s_ccol, s_ncum, s_scr) = sems(
            "s_const s_x s_wraw s_whi s_wsplit s_zero s_xn s_xt s_xhi s_xlo s_ab s_abc s_chain s_nexp "
            "s_gate_e s_gate_u s_g s_alpha s_arow s_arow_sb s_crow s_ccol s_ncum s_scr")
        proj_ready, raw_ready, prod_ready, sum_ready, conv_mid, conv_done = sems(
            "proj_ready raw_ready prod_ready sum_ready conv_mid conv_done")
        alpha_in, acum_in = sem("alpha_in"), sems("acum_in0 acum_in1")
        (diag_ready, decay_done, kk_ready, n_ready, ktr_ready, kd_ready, scale_ready, kq_ready, at_ready, aq_ready,
         vtr_ready, v_ready, z_mm, z_tanh, zg_ready) = sems(
            "diag_ready decay_done kk_ready n_ready ktr_ready kd_ready scale_ready kq_ready at_ready aq_ready "
            "vtr_ready v_ready z_mm z_tanh zg_ready")
        (n_out, blk_in, inv_step, inv_done, t_out, t_in, rdiag, y32_mm, y32_sb, r32_mm, r32_sb, y64_mm, y64_sb,
         r64_mm, R_ready) = sems(
            "n_out blk_in inv_step inv_done t_out t_in rdiag y32_mm y32_sb r32_mm r32_sb y64_mm y64_sb r64_mm R_ready")
        (ks_mm, rhs_ready, u_mm, u_ready, sd_mm, S_ready, o_mm, sq_done, rms_step, g_ready, gtr_mm, gt_ready, out_mm,
         x2_ready) = sems(
            "ks_mm rhs_ready u_mm u_ready sd_mm S_ready o_mm sq_done rms_step g_ready gtr_mm gt_ready out_mm x2_ready")
        x2_out, xres_in = sem("x2_out"), sems("xres_in0 xres_in1")
        (f_w1raw, f_w2, f_small, f_whi, f_wlo, f_chain, f_xt, f_xhi, f_xlo, f_lg, f_sub, f_exp, f_wt, f_wtsb, f_b2,
         f_acc, f_h_mm, f_relu, f_y_mm, f_y, f_out) = sems(
            "f_w1raw f_w2 f_small f_whi f_wlo f_chain f_xt f_xhi f_xlo f_lg f_sub f_exp f_wt f_wtsb f_b2 "
            "f_acc f_h_mm f_relu f_y_mm f_y f_out")

        block = ctx.enter_context(nc.Block())

        def rsqrt_step(s, v, y, t):
            if s == 0:
                return nc.vector.tensor_single_scalar(t.bitcast(I32), v.bitcast(I32), 1, ALU.arith_shift_right)
            if s == 1:
                return nc.vector.tensor_scalar(y.bitcast(I32), t.bitcast(I32), -1.0, float(0x5F3759DF), ALU.mult, ALU.add)
            if s % 3 == 2:
                return nc.vector.tensor_tensor(t, y, y, ALU.mult)
            if s % 3 == 0:
                return nc.vector.scalar_tensor_tensor(out=t, in0=t, scalar=-0.5, in1=v, op0=ALU.mult, op1=ALU.mult)
            return nc.vector.scalar_tensor_tensor(out=y, in0=t, scalar=1.5, in1=y, op0=ALU.add, op1=ALU.mult)
        RSQ = 2 + 3 * 3

        HALVES = GC * U

        order = [H + h for h in range(H)] + [2 * H + h for h in range(H)] + list(range(H))
        INV = 2 * BLK
        RMS = 1 + RSQ

        def woven(*lists):
            return [x[i] for i in range(max(map(len, lists))) for x in lists if i < len(x)]

        def tiles(n0, n1, fill=()):
            out, fill = [], list(fill)
            per = -(-len(fill) // (2 * (n1 - n0)))
            for n in range(n0, n1):
                out += [("conv", n), ("first", n + 1)] + fill[:per] + [("last", n)] + fill[per:2 * per]
                fill = fill[2 * per:]
            return out

        def inv(s0, s1):
            return [("inv", s) for s in range(s0, s1)]

        def rms(c):
            return [("rms", c, s) for s in range(RMS)]

        STEPS = ([("begin",)] + tiles(-AHEAD, -2) + [("ks", 0)] + tiles(-2, 1) + [("rdiag",), ("merge", 0), ("aq", 0), ("aq", 1)]
                 + tiles(1, 3) + [("scan", 0), ("merge", 1)] + tiles(3, 5) + [("scan", 1), ("merge", 2)] + tiles(5, 7)
                 + [("merge", 3)] + tiles(7, 8) + [("u", 0)] + tiles(8, 9) + [("kk", 0), ("kk", 1)] + tiles(9, 10)
                 + [("sd", 0)] + tiles(10, 11) + [("scale", 0), ("ks", 1), ("o", 0)] + tiles(11, 12)
                 + [("ktr", 0), ("u", 1)] + tiles(12, 14) + [("sd", 1)] + tiles(14, 15, inv(0, 2) + rms(0))
                 + [("g", 0), ("scale", 1)] + tiles(15, 17, inv(2, 14)) + [("out", 0), ("ktr", 1), ("o", 1)]
                 + tiles(17, 18, inv(14, 22)) + [("vtr", 0)] + woven(rms(1), inv(22, 22 + RMS)) + [("g", 1)]
                 + tiles(18, 20, inv(22 + RMS, 52)) + [("out", 1)] + tiles(20, 21, inv(52, INV)) + [("vtr", 1), ("z", 0)]
                 + tiles(21, 23) + [("z", 1)] + tiles(23, 24) + [("kq", 0), ("kq", 1)])
        KX_USES = [(s, c) for s, *arg in STEPS if s in ("kk", "g", "ktr", "kq", "vtr") for c in arg]
        KX_TAKEN = {"kk": n_ready, "ktr": kd_ready, "kq": at_ready, "vtr": v_ready, "g": gt_ready}
        RMS_STEPS = 1 + RSQ
        f32n = lambda v: float(np.float32(v))
        ATANH = [f32n(1.0 / (2 * k + 1)) for k in range(9)]

        def column(g, c):
            return g * GT + (g // (NG // B)) * PAD + PAD + C * c

        def xflat(t):
            return t[:, :, :].rearrange("p b t -> p (b t)")

        def xtile(t, i):
            return xflat(t)[:, ds(i * (TW * C) + (i // (T // (TW * C))) * PAD + PAD, TW * C)]

        def bc(ap, shape):
            return ap.to_broadcast(shape)

        CHAIN_PREP = (2 + RMS_STEPS) * (NCH // TW) + 19
        F_PER = 2 + RMS_STEPS + 9

        w2_sb = area[0][:, :].rearrange("p (e f d) -> p e f d", e=NE, f=NF)
        w1raw = area[1][:, :].rearrange("p (e n) -> p e n", e=NE)
        w1h = area[2][:, :].bitcast(F16)
        w1_hi = w1h[:, 0:NE * FF].rearrange("p (e n) -> p e n", e=NE)
        w1_lo = w1h[:, NE * FF:2 * NE * FF].rearrange("p (e n) -> p e n", e=NE)
        hbuf = area[3][:, :].rearrange("p (r f n) -> p r f n", r=2, f=NF)
        xn2 = G[:, 0:TW, :]
        acc = G[:, TW:2 * TW, :]
        x2T = rhs[:, 0:TW, :].rearrange("p a b -> p (a b)")
        x2_hi = Us[:, 0:2, :].rearrange("p a b -> p (a b)").bitcast(F16)
        x2_lo = Us[:, 2:4, :].rearrange("p a b -> p (a b)").bitcast(F16)
        wT = GTs[:, 0:TW, :].rearrange("p a b -> p (a b)")
        rt = [ssq4[:, k, :] for k in range(4)]

        @block.sync
        def _(sp):
            for dst, src in ((ident, eye), (par_eye32, parity_eye), (tri, low_tri), (keep, keep_in),
                             (taps, conv_w.rearrange("(t p) o k -> p t (o k)", p=128)),
                             (nw, norm_w.rearrange("(p o) -> p o", o=1)),
                             (dtb, bc(dt_bias.rearrange("(o h) -> o h", o=1), [128, H])),
                             (alog, bc(a_log.rearrange("(o h) -> o h", o=1), [128, H]))):
                sp.dma_start(dst[tuple(slice(None) for _ in dst.shape)], src).then_inc(s_const, 16)
            xt = x_in.rearrange("b (c p) d -> p (b c) d", p=128)
            for i in range(4):
                sp.dma_start(x_sb[:, 8 * i:8 * i + 8, :], xt[:, 8 * i:8 * i + 8, :]).then_inc(s_x, 16)
            sp.dma_start(kflat, qkv_t[:, 0:2048]).then_inc(s_wraw, 16)
            sp.dma_start(qflat[:, 0:1024], qkv_t[:, 2048:3072]).then_inc(s_wraw, 16)
            sp.dma_start(qflat[:, 1024:2048], z_t).then_inc(s_wraw, 16)
            sp.dma_start(vflat[:, 0:16], ab_t).then_inc(s_wraw, 16)
            sp.dma_start(ow[:, :, :], out_t.rearrange("(h p) d -> p h d", p=128)).then_inc(s_wraw, 16)
            sp.wait_ge(s_crow, 1)
            sp.dma_start(scr_alpha.rearrange("b p t -> p b t"), rows0).then_inc(s_scr, 16)
            sp.dma_start(scr_acum.rearrange("b p t -> p b t"), crow).then_inc(s_scr, 16)
            sp.wait_ge(s_scr, 32)
            sp.sem_inc(x2_out, 16)

            def alphas(a, c):
                sp.wait_ge(s_scr, 32)
                sp.wait_ge(decay_done, a * GC + c + GC)
                sp.dma_start(alpha_b.rearrange("p h t -> p (h t)"),
                             bc(alpha_rows[ds(a * GC + c, 1), :], [128, H * C])).then_inc(alpha_in, 16)

            def products(a):
                for c in range(GC):
                    sp.wait_ge(s_scr, 32)
                    sp.wait_ge(aq_ready, a * GC + c + 1)
                    sp.wait_ge(scale_ready, a * GC + c + 1)
                    sp.dma_start(acum_b[:, c, :, :].rearrange("p h t -> p (h t)"),
                                 bc(acum_rows[ds(a * GC + c, 1), :], [128, H * C])).then_inc(acum_in[c], 16)

            def blocks_out(a):
                for c in range(GC):
                    sp.wait_ge(n_ready, a * HALVES + U * c + 2)
                    for b in range(NB):
                        q = (c * NB + b) * H
                        sp.dma_start(scr_n[q:q + H].rearrange("h i j -> i h j"),
                                     Nm[BLK * b:BLK * b + BLK, c, :, BLK * b:BLK * b + BLK]).then_inc(n_out, 16)
                sp.wait_ge(inv_done, a + 1)
                sp.wait_ge(n_out, a * (16 * GC * NB) + 16 * GC * NB)
                for par in range(2):
                    sp.dma_start(blkN[64 * par:64 * par + 64, :, :], scr_n).then_inc(blk_in, 16)

            def inverses_in(a):
                sp.wait_ge(s_scr, 32)
                sp.wait_ge(inv_done, a + 2)
                for par in range(2):
                    sp.dma_start(scr_t.rearrange("q (a p) m -> p q a m", p=2)[par],
                                 blkT[64 * par:64 * par + 64, :, :]).then_inc(t_out, 16)
                sp.wait_ge(s_scr, 32)
                sp.wait_ge(t_out, a * 32 + 32)
                for c in range(GC):
                    for b in range(NB):
                        q = (c * NB + b) * H
                        r = slice(BLK * b, BLK * b + BLK)
                        dst = T64[r, c, :, r] if b < 2 else T32[r, c, :, :]
                        sp.dma_start(dst, scr_t[q:q + H].rearrange("h i j -> i h j")).then_inc(t_in, 16)

            def x_load(g):
                for c in range(GC):
                    sp.wait_ge(s_scr, 32)
                    sp.wait_ge(x2_out, g * (16 * GC) + 16)
                    sp.dma_start(xres[:, c, :], xt[:, ds(g * GC + c, 1), :].rearrange("p a d -> p (a d)")
                                 ).then_inc(xres_in[c], 16)

            def x2_store(g, c):
                sp.wait_ge(s_scr, 32)
                sp.wait_ge(x2_ready, g * GC + c + 2)
                sp.dma_start(scr_x2[:, ds(g * GC + c, 1), :].rearrange("p a d -> p (a d)"), xres[:, c, :]).then_inc(x2_out, 16)

            def joined(g):
                alphas(g + 1, 0)
                x_load(g)
                alphas(g + 1, 1)
                products(g + 1)
                blocks_out(g + 1)
                x2_store(g, 0)
                inverses_in(g + 1)
                x2_store(g, 1)

            alphas(0, 0)
            alphas(0, 1)
            products(0)
            blocks_out(0)
            inverses_in(0)
            with sp.Fori(0, (NG - 1) // 2) as i:
                joined(2 * i)
                joined(2 * i + 1)
            joined(NG - 2)
            x_load(NG - 1)
            x2_store(NG - 1, 0)
            x2_store(NG - 1, 1)
            sp.wait_ge(x2_out, 16 * NCH + 16)
            sp.dma_start(x_sb, scr_x2).then_inc(s_x, 16)
            sp.wait_ge(x2_ready, NCH + 1)
            for e in range(NE):
                sp.dma_start(w1raw[:, e, :], w1[e]).then_inc(f_w1raw, 16)
                sp.dma_start(w2_sb[:, e, :, :], w2[e].rearrange("(f p) d -> p f d", p=128)).then_inc(f_w2, 16)
            sp.dma_start(rw[:, :], router_w).then_inc(f_small, 16)
            sp.dma_start(rb[:, :], bc(router_b.rearrange("(o e) -> o e", o=1), [128, NE])).then_inc(f_small, 16)
            sp.dma_start(b1_sb[:, :, :], b1.rearrange("e (f p) -> p e f", p=128)).then_inc(f_small, 16)
            sp.dma_start(b2_sb[0:NE, :], b2).then_inc(f_small, 16)
            yt = out.rearrange("b (c p) d -> p (b c) d", p=128)
            with sp.Fori(0, NCH // TW) as i:
                sp.wait_ge(f_y, i * NE + NE + 1)
                sp.dma_start(yt[:, ds(i * TW, TW), :], x_sb[:, ds(i * TW, TW), :]).then_inc(f_out, 16)
            sp.wait_ge(f_out, 16 * (NCH // TW))

        @block.gpsimd
        def _(pool):
            nc.gpsimd.memset(T64[:, :, :, :], 0.0)
            nc.gpsimd.memset(R, 0.0)
            nc.gpsimd.memset(S[:, :, :, :], 0.0)
            nc.gpsimd.memset(xn_hi[:, :, 0:PAD], 0.0)
            nc.gpsimd.memset(xn_lo[:, :, 0:PAD], 0.0).then_inc(s_zero, 1)
            pool.sem_inc(aq_ready, GC)
            pool.wait_ge(s_const, 128)
            pool.wait_ge(s_g, 1)
            pool.sem_inc(sum_ready, TAPB)

            def stages(g, a, par):
                def diag(c):
                    pool.wait_ge(decay_done, a * GC + c + GC)
                    nc.gpsimd.tensor_tensor(
                        beta_d[:, :, :], bc(ident[:, :].rearrange("p (o c) -> p o c", o=1), [128, H, C]),
                        bc(beta[:, ds(a * GC + c, 1), :].rearrange("p o (h u) -> p (o h) u", u=1), [128, H, C]),
                        ALU.mult).then_inc(diag_ready, 1)

                def add(n):
                    pool.wait_ge(prod_ready, a * NT + n + 1)
                    nc.gpsimd.tensor_tensor(tapA[:, n % RING, :], tapA[:, n % RING, :], tapB[:, n % TAPB, :],
                                            ALU.add).then_inc(sum_ready, 1)

                for step, *arg in STEPS:
                    if step == "begin" and a is not None:
                        diag(0)
                    elif step == "conv" and a is not None and arg[0] + AHEAD < NT:
                        add(arg[0] + AHEAD)
                    elif step == "scan" and a is not None and arg[0] == 0:
                        diag(1)
                    elif step == "aq" and g is not None:
                        c, = arg
                        pool.wait_ge(acum_in[c], g * 16 + 16)
                        pool.wait_ge(kq_ready, g * HALVES + U * c + 2)
                        qc = qT[1 - par][:, :, C * c:C * c + C]
                        nc.gpsimd.tensor_tensor(qc, qc, acum_b[:, c, :, :], ALU.mult).then_inc(aq_ready, 1)

            stages(None, 0, 0)
            with pool.Fori(0, (NG - 1) // 2) as i:
                stages(2 * i, 2 * i + 1, 1)
                stages(2 * i + 1, 2 * i + 2, 0)
            stages(NG - 2, NG - 1, 1)
            stages(NG - 1, None, 0)

        @block.scalar
        def _(act):
            act.wait_ge(s_wraw, 80)
            for dst, src in ((wq_hi[:, 0:2048], kflat), (wq_hi[:, 2048:3072], qflat[:, 0:1024]),
                             (wz_hi[:, :], qflat[:, 1024:2048]), (wab_hi[:, :], vflat[:, 0:16])):
                nc.scalar.activation(dst, src, ACT.Copy, scale=WSCALE).then_inc(s_whi, 1)
            act.wait_ge(s_const, 128)
            nc.scalar.activation(nexp_a[:, :], alog[:, :], ACT.Exp).then_inc(s_nexp, 1)
            with act.Fori(0, NCH // TW) as i:
                act.wait_ge(s_xt, i + 1)
                nc.scalar.activation(xtile(xn_hi, i), pj[0][:, :], ACT.Copy).then_inc(s_xhi, 1)
                act.wait_ge(s_ab, i + 1)
                nc.scalar.activation(ab[:, ds(i * TW, TW), :].rearrange("p a b -> p (a b)"), kx[0][:, 0:TW * 2 * H],
                                     ACT.Copy, scale=1.0 / WSCALE).then_inc(s_abc, 1)
            act.wait_ge(s_abc, NCH // TW)
            nc.scalar.activation(beta[:, :, :], ab[:, :, 0:H], ACT.Exp, scale=-1.0).then_inc(s_gate_e, 1)
            act.wait_ge(s_gate_u, 1)
            nc.scalar.activation(tmp[1], tmp[1], ACT.Exp, scale=-1.0).then_inc(s_gate_e, 1)
            act.wait_ge(s_g, 1)
            nc.scalar.activation(alpha_t, tmp[0], ACT.Exp, scale=-1.0).then_inc(s_alpha, 1)
            act.wait_ge(s_arow, 1)
            nc.scalar.activation(rows, pj[0][:, 0:256].rearrange("p (a b) -> p a b", a=2), ACT.Copy).then_inc(s_arow_sb, 1)
            act.wait_ge(s_ccol, 1)
            nc.scalar.activation(neg_acum[:, :, :].rearrange("p a b -> p (a b)"), pj[1][:, 0:256], ACT.Copy,
                                 scale=-1.0).then_inc(s_ncum, 1)
            act.sem_inc(gt_ready, HALVES)
            act.sem_inc(sq_done, U)

            def prepare(step, arg, a):
                def evacuate(n):
                    act.wait_ge(proj_ready, a * NT + n + 1)
                    act.wait_ge(conv_done, a * NT + n + 1)
                    nc.scalar.activation(raw[:, n % RING, 0:W], pj[n % 2][:, 0:W], ACT.Copy,
                                         scale=1.0 / WSCALE).then_inc(raw_ready, 1)

                def products(n):
                    t = order[n]
                    act.wait_ge(raw_ready, a * NT + n + 1)
                    act.wait_ge(sum_ready, a * NT + n + 1)
                    nc.scalar.activation(tapB[:, n % TAPB, :], raw[:, n % RING, 2:2 + GT], ACT.Copy,
                                         scale=taps[:, t, 2:3])
                    nc.scalar.activation(tapA[:, n % RING, :], raw[:, n % RING, 3:3 + GT], ACT.Copy,
                                         scale=taps[:, t, 3:4]).then_inc(prod_ready, 1)

                if step == "begin":
                    evacuate(0)
                elif step == "conv":
                    n, = arg
                    if n + AHEAD + 1 < NT:
                        evacuate(n + AHEAD + 1)
                    if n + AHEAD < NT:
                        products(n + AHEAD)
                elif step == "vtr":
                    c, = arg
                    for u in range(U):
                        act.wait_ge(vtr_ready, a * HALVES + U * c + u + 1)
                        nc.scalar.activation(V[:, c, HU * u:HU * u + HU, :], heads(kx[u]), ACT.Copy).then_inc(v_ready, 1)
                elif step == "z":
                    c, = arg
                    for u in range(U):
                        act.wait_ge(z_mm, a * HALVES + U * c + u + 1)
                        nc.scalar.activation(zg[:, c, HU * u:HU * u + HU, :], heads(pj[u]), ACT.Tanh,
                                             scale=0.5 / WSCALE).then_inc(z_tanh, 1)

            def finish(step, arg, g):
                if step == "merge":
                    hop, = arg
                    for c in range(GC):
                        k = g * GC + c
                        y_bank, r_bank = merge_banks[c]
                        if hop == 0:
                            act.wait_ge(y32_mm, k + 1)
                            py = y_bank[:, 0:H * BLK].rearrange("p (h c) -> p h c", h=H)
                            nc.scalar.activation(Y32[c][96:128], py[96:128], ACT.Copy)
                            nc.scalar.activation(Y32[c][32:64], py[32:64], ACT.Copy).then_inc(y32_sb, 1)
                        elif hop == 1:
                            act.wait_ge(r32_mm, k + 1)
                            pr = r_bank[:, 0:H * BLK].rearrange("p (h c) -> p h c", h=H)
                            nc.scalar.activation(T64[32:64, c, :, 0:32], pr[32:64], ACT.Copy, scale=-1.0)
                            nc.scalar.activation(R[64:96, c, :, 96:128], pr[64:96], ACT.Copy, scale=-1.0)
                            nc.scalar.activation(R[0:32, c, :, 32:64], pr[0:32], ACT.Copy, scale=-1.0).then_inc(r32_sb, 1)
                        elif hop == 2:
                            act.wait_ge(y64_mm, k + 1)
                            nc.scalar.activation(Y64[c][64:128], y_bank[64:128, :].rearrange("p (h c) -> p h c", h=H),
                                                 ACT.Copy).then_inc(y64_sb, 1)
                        else:
                            act.wait_ge(r64_mm, k + 1)
                            nc.scalar.activation(R[0:64, c, :, 64:128], r_bank[0:64, :].rearrange("p (h c) -> p h c", h=H),
                                                 ACT.Copy, scale=-1.0).then_inc(R_ready, 1)
                elif step == "u":
                    c, = arg
                    for u in range(U):
                        act.wait_ge(u_mm, g * HALVES + U * c + u + 1)
                        nc.scalar.activation(Us[:, HU * u:HU * u + HU, :], heads(rc[u]), ACT.Copy).then_inc(u_ready, 1)
                elif step == "o":
                    c, = arg
                    for u in range(U):
                        act.wait_ge(o_mm, g * HALVES + U * c + u + 1)
                        act.wait_ge(sq_done, g * HALVES + U * c + u + U)
                        for h in range(HU):
                            last = nc.scalar.activation(G[:, HU * u + h, :], heads(ob[u])[:, h, :], ACT.Square,
                                                        accum_out=ssq[:, HU * u + h:HU * u + h + 1])
                        last.then_inc(sq_done, 1)
                elif step == "g":
                    c, = arg
                    for u in range(U):
                        act.wait_ge(gtr_mm, g * HALVES + U * c + u + 1)
                        nc.scalar.activation(GTs[:, HU * u:HU * u + HU, :], heads(kx[u]), ACT.Copy).then_inc(gt_ready, 1)

            def stages(g, a):
                for step, *arg in STEPS:
                    if g is not None:
                        finish(step, arg, g)
                    if a is not None:
                        prepare(step, arg, a)

            stages(None, 0)
            with act.Fori(0, (NG - 1) // 2) as i:
                stages(2 * i, 2 * i + 1)
                stages(2 * i + 1, 2 * i + 2)
            stages(NG - 2, NG - 1)
            stages(NG - 1, None)
            for e in range(NE):
                act.wait_ge(f_w1raw, 16 * NE)
                nc.scalar.activation(w1_hi[:, e, :], w1raw[:, e, :], ACT.Copy, scale=WSCALE).then_inc(f_whi, 1)
            act.wait_ge(f_small, 64)
            with act.Fori(0, NCH // TW) as i:
                act.wait_ge(f_xt, i + 1)
                nc.scalar.activation(x2T[:, :], kx[0][:, :], ACT.Copy)
                nc.scalar.activation(x2_hi[:, :], kx[0][:, :], ACT.Copy).then_inc(f_xhi, 1)
                act.wait_ge(f_sub, i + 1)
                nc.scalar.activation(rt[2], rt[1], ACT.Exp).then_inc(f_exp, 1)
                for e in range(NE):
                    for f in range(NF):
                        act.wait_ge(f_h_mm, i * (NE * NF) + e * NF + f + 1)
                        if f == 0:
                            act.wait_ge(f_y_mm, i * NE + e + 1)
                        nc.scalar.activation(hbuf[:, e % 2, f, :], pj[f % 2][:, :], ACT.Relu, bias=b1_sb[:, e, f:f + 1],
                                             scale=1.0 / WSCALE).then_inc(f_relu, 1)
                    if e == 0:
                        act.wait_ge(f_wt, i + 1)
                        nc.scalar.activation(wT[0:NE, :], kx[1][0:NE, :], ACT.Copy).then_inc(f_wtsb, 1)

        @block.vector
        def _(dve):
            count = [0]

            def link(ins, base=0):
                count[0] += 1
                ins.then_inc(s_chain, 1)
                dve.wait_ge(s_chain, base + count[0])

            dve.wait_ge(s_wraw, 80)
            for k, (dst, src, hi) in enumerate(((wq_lo[:, 0:2048], kflat, wq_hi[:, 0:2048]),
                                                (wq_lo[:, 2048:3072], qflat[:, 0:1024], wq_hi[:, 2048:3072]),
                                                (wz_lo[:, :], qflat[:, 1024:2048], wz_hi[:, :]),
                                                (wab_lo[:, :], vflat[:, 0:16], wab_hi[:, :]))):
                dve.wait_ge(s_whi, k + 1)
                nc.vector.scalar_tensor_tensor(out=dst, in0=src, scalar=WSCALE, in1=hi, op0=ALU.mult, op1=ALU.subtract)
            dve.wait_ge(s_const, 128)
            nc.vector.tensor_copy(par_eye[:, :, :], par_eye32)
            nc.vector.tensor_scalar(ow[:, :, :], ow[:, :, :], nw[:, 0:1], 0.5 / WSCALE, ALU.mult,
                                    ALU.mult).then_inc(s_wsplit, 1)
            dve.wait_ge(s_x, 64)
            PER = 2 + RMS_STEPS

            def layernorm(i, dst, base):
                for j in range(TW):
                    ins = nc.vector.bn_stats(bst[:, j, :], x_sb[:, ds(i * TW + j, 1), :].rearrange("p a b -> p (a b)"))
                count[0] += 1
                ins.then_inc(s_chain, 1)
                dve.wait_ge(s_chain, base + count[0])
                nc.vector.memset(rs[:, 3, 0:1], 0.0)
                for j in range(TW):
                    ins = nc.vector.bn_aggr(mv[:, j, :], bst[:, j, :])
                link(ins, base)
                link(nc.vector.tensor_scalar_add(rs[:, 0, 0:TW], mv[:, :, 1], 1e-5), base)
                for s in range(RSQ):
                    link(rsqrt_step(s, rs[:, 0, 0:TW], rs[:, 1, 0:TW], rs[:, 2, 0:TW]), base)
                for j in range(TW):
                    ins = nc.vector.tensor_scalar(dst[:, j, :], x_sb[:, ds(i * TW + j, 1), :].rearrange("p a b -> p (a b)"),
                                                  mv[:, j, 0:1], rs[:, 1, j:j + 1], ALU.subtract, ALU.mult)
                return ins

            with dve.Fori(0, NCH // TW) as i:
                count[0] = 0
                layernorm(i, xn, i * PER).then_inc(s_xn, 1)
                assert count[0] == PER
                dve.wait_ge(s_xhi, i + 1)
                nc.vector.tensor_tensor(xtile(xn_lo, i), pj[0][:, :], xtile(xn_hi, i), ALU.subtract).then_inc(s_xlo, 1)
            count[0] = PER * (NCH // TW)
            v3 = lambda ap: ap.rearrange("p (c h) -> p c h", h=H)
            dve.wait_ge(s_abc, NCH // TW)
            link(nc.vector.tensor_tensor(v3(tmp[0]), ab[:, :, H:2 * H],
                                         bc(dtb[:, :].rearrange("p (o h) -> p o h", o=1), [128, NCH, H]), ALU.add))
            nc.vector.scalar_tensor_tensor(out=tmp[1], in0=tmp[0], scalar=-1.0, in1=tmp[0], op0=ALU.mult,
                                           op1=ALU.max).then_inc(s_gate_u, 1)
            dve.wait_ge(s_gate_e, 1)
            link(nc.vector.tensor_scalar_add(beta[:, :, :], beta[:, :, :], 1.0))
            link(nc.vector.reciprocal(beta[:, :, :], beta[:, :, :]))
            dve.wait_ge(s_gate_e, 2)
            link(nc.vector.tensor_scalar_add(tmp[2], tmp[1], 2.0))
            link(nc.vector.reciprocal(tmp[2], tmp[2]))
            link(nc.vector.tensor_tensor(tmp[1], tmp[1], tmp[2], ALU.mult))
            link(nc.vector.tensor_tensor(tmp[2], tmp[1], tmp[1], ALU.mult))
            link(nc.vector.tensor_scalar(tmp[3], tmp[2], ATANH[8], None, ALU.mult))
            for k in range(7, 0, -1):
                link(nc.vector.scalar_tensor_tensor(out=tmp[3], in0=tmp[3], scalar=ATANH[k], in1=tmp[2],
                                                    op0=ALU.add, op1=ALU.mult))
            link(nc.vector.scalar_tensor_tensor(out=tmp[3], in0=tmp[3], scalar=1.0, in1=tmp[1], op0=ALU.add, op1=ALU.mult))
            link(nc.vector.tensor_scalar(tmp[3], tmp[3], 2.0, None, ALU.mult))
            link(nc.vector.scalar_tensor_tensor(out=tmp[0], in0=tmp[0], scalar=0.0, in1=tmp[3], op0=ALU.max, op1=ALU.add))
            dve.wait_ge(s_nexp, 1)
            nc.vector.tensor_tensor(v3(tmp[0]), v3(tmp[0]),
                                    bc(nexp_a[:, :].rearrange("p (o h) -> p o h", o=1), [128, NCH, H]),
                                    ALU.mult).then_inc(s_g, 1)
            nc.vector.memset(zrow, 0.0)
            dve.wait_ge(s_arow_sb, 1)
            link(nc.vector.tensor_copy(rows0, rows))
            assert count[0] == CHAIN_PREP
            nc.vector.memset(rows0[:, :, 0:1], 0.0)
            nc.vector.tensor_tensor_scan(crow[:, 0, :], rows[:, 0, :], zrow, 1.0, ALU.mult, ALU.add)
            nc.vector.tensor_tensor_scan(crow[:, 1, :], rows[:, 1, :], zrow, 1.0, ALU.mult, ALU.add).then_inc(s_crow, 1)
            dve.wait_ge(s_scr, 32)
            dve.wait_ge(s_ncum, 1)
            dve.wait_ge(s_zero, 1)
            dve.sem_inc(decay_done, GC)
            dve.sem_inc(scale_ready, GC)
            dve.sem_inc(conv_done, RING)
            dve.sem_inc(zg_ready, HALVES)
            dve.sem_inc(inv_done, 1)
            dve.sem_inc(x2_ready, 1)
            dve.sem_inc(S_ready, U)
            dve.sem_inc(g_ready, U)

            def half(t, c, u):
                return t[:, c, HU * u:HU * u + HU, :]

            def prepare(step, arg, g, a, par):
                if step == "first" and 0 <= arg[0] < NT:
                    n, = arg
                    dve.wait_ge(sum_ready, a * NT + n + 1 + TAPB)
                    nc.vector.scalar_tensor_tensor(out=tapA[:, n % RING, :], in0=raw[:, n % RING, 1:1 + GT],
                                                   scalar=taps[:, order[n], 1:2], in1=tapA[:, n % RING, :],
                                                   op0=ALU.mult, op1=ALU.add).then_inc(conv_mid, 1)
                elif step == "last" and arg[0] >= 0:
                    n, = arg
                    dst = (kT[par], vT, qT[par])[n // H]
                    dve.wait_ge(conv_mid, a * NT + n + 1)
                    nc.vector.scalar_tensor_tensor(out=dst[:, n % H, :], in0=raw[:, n % RING, 0:GT],
                                                   scalar=taps[:, order[n], 0:1], in1=tapA[:, n % RING, :],
                                                   op0=ALU.mult, op1=ALU.add).then_inc(conv_done, 1)
                elif step == "scan":
                    c, = arg
                    dve.wait_ge(alpha_in, a * (16 * GC) + 16 * c + 16)
                    dve.wait_ge(diag_ready, a * GC + c + 1)
                    nc.vector.tensor_tensor_scan(decay[:, c, :, :].rearrange("p h c -> p (h c)"),
                                                 alpha_b.rearrange("p h c -> p (h c)"),
                                                 beta_d[:, :, :].rearrange("p h c -> p (h c)"),
                                                 0.0, ALU.mult, ALU.add).then_inc(decay_done, 1)
                elif step == "kk":
                    c, = arg
                    for u in range(U):
                        dve.wait_ge(kk_ready, a * HALVES + U * c + u + 1)
                        dve.wait_ge(decay_done, a * GC + c + 1 + GC)
                        nc.vector.tensor_tensor(half(Nm, c, u), heads(kx[u]), half(decay, c, u),
                                                ALU.mult).then_inc(n_ready, 1)
                elif step == "inv":
                    s, = arg
                    if s:
                        dve.wait_ge(inv_step, a * (INV - 1) + s)
                    if s == 0:
                        ins = nc.vector.tensor_copy(blkT[:, :, :], par_eye[:, :, :])
                    elif s == 1:
                        dve.wait_ge(blk_in, a * 32 + 32)
                        ins = nc.vector.memset(blkN[:, :, :].rearrange("p a b -> p (a b)")[:, 0:BLK * BLK:BLK + 1], -1.0)
                    else:
                        j = BLK - 1 - s // 2
                        r0, wd = (j + 1) // 2, BLK - j
                        nr = BLK // 2 - r0
                        if s % 2 == 0:
                            ins = nc.vector.tensor_tensor(prod[:, 0:nr, 0:wd], blkT[:, r0:, j:],
                                                          bc(blkN[:, j:j + 1, j:], [128, nr, wd]), ALU.mult)
                        else:
                            ins = nc.vector.tensor_reduce(blkT[:, r0:, j:j + 1], prod[:, 0:nr, 0:wd], AX.X, ALU.add,
                                                          negate=True)
                    ins.then_inc(inv_step if s < INV - 1 else inv_done, 1)
                elif step == "scale":
                    c, = arg
                    if g is not None:
                        dve.wait_ge(S_ready, g * HALVES + U * c + 2 + U)
                    dve.wait_ge(acum_in[c], a * 16 + 16)
                    end = keep[:, ds(a, 1)] if c == GC - 1 else 1.0
                    nc.vector.tensor_scalar(kd_scale[:, c, :], decay[:, c, :, C - 1], end, None, ALU.mult)
                    nc.vector.tensor_scalar(a_end[:, c, :], acum_b[:, c, :, C - 1], end, None, ALU.mult)
                    nc.vector.tensor_copy(nac[:, c, :], neg_acum[:, ds(a * GC + c, 1), :].rearrange("p a h -> p (a h)")
                                          ).then_inc(scale_ready, 1)
                elif step == "ktr":
                    c, = arg
                    for u in range(U):
                        dve.wait_ge(ktr_ready, a * HALVES + U * c + u + 1)
                        dve.wait_ge(scale_ready, a * GC + c + 1 + GC)
                        sc = kd_scale[:, c, HU * u:HU * u + HU].rearrange("p (h o) -> p h o", o=1)
                        nc.vector.tensor_tensor(half(kd, c, u), heads(kx[u]), bc(sc, [128, HU, C]),
                                                ALU.mult).then_inc(kd_ready, 1)
                elif step == "kq":
                    c, = arg
                    for u in range(U):
                        dve.wait_ge(kq_ready, a * HALVES + U * c + u + 1)
                        nc.vector.tensor_tensor(half(AT, c, u), heads(kx[u]), half(decay, c, u),
                                                ALU.mult).then_inc(at_ready, 1)
                elif step == "z":
                    c, = arg
                    for u in range(U):
                        dve.wait_ge(z_tanh, a * HALVES + U * c + u + 1)
                        nc.vector.scalar_tensor_tensor(out=half(zg, c, u), in0=half(zg, c, u), scalar=1.0,
                                                       in1=heads(pj[u]), op0=ALU.add, op1=ALU.mult).then_inc(zg_ready, 1)

            def finish(step, arg, g):
                if step == "rdiag":
                    dve.wait_ge(t_in, g * (16 * GC * NB) + 16 * GC * NB)
                    for c in range(GC):
                        for b in range(NB):
                            r = slice(BLK * b, BLK * b + BLK)
                            ins = nc.vector.transpose(R[r, c, :, r], T64[r, c, :, r] if b < 2 else T32[r, c, :, :])
                        ins.then_inc(rdiag, 1)
                elif step == "ks":
                    c, = arg
                    for u in range(U):
                        dve.wait_ge(ks_mm, g * HALVES + U * c + u + 1)
                        dve.wait_ge(v_ready, g * HALVES + U * c + u + 1)
                        for h in range(HU):
                            hh = HU * u + h
                            ins = nc.vector.scalar_tensor_tensor(out=rhs[:, hh, :], in0=heads(rc[u])[:, h, :],
                                                                 scalar=nac[:, c, hh:hh + 1], in1=V[:, c, hh, :],
                                                                 op0=ALU.mult, op1=ALU.add)
                        ins.then_inc(rhs_ready, 1)
                elif step == "sd":
                    c, = arg
                    for u in range(U):
                        dve.wait_ge(sd_mm, g * HALVES + U * c + u + 1)
                        for h in range(HU):
                            hh = HU * u + h
                            ins = nc.vector.scalar_tensor_tensor(out=S[:, 1 - c, hh, :], in0=S[:, c, hh, :],
                                                                 scalar=a_end[:, c, hh:hh + 1],
                                                                 in1=heads(rc[u])[:, h, :],
                                                                 op0=ALU.mult, op1=ALU.add)
                        ins.then_inc(S_ready, 1)
                elif step == "rms":
                    c, s = arg
                    if s == 0:
                        dve.wait_ge(sq_done, g * HALVES + U * c + 2 + U)
                        ins = nc.vector.tensor_scalar(rs[:, 0, 0:H], ssq[:, :], 1.0 / C, 1e-6, ALU.mult, ALU.add)
                    else:
                        dve.wait_ge(rms_step, (g * GC + c) * RMS + s)
                        ins = rsqrt_step(s - 1, rs[:, 0, 0:H], rs[:, 1, 0:H], rs[:, 2, 0:H])
                    ins.then_inc(rms_step, 1)
                elif step == "g":
                    c, = arg
                    dve.wait_ge(rms_step, (g * GC + c) * RMS + RMS)
                    for u in range(U):
                        for h in range(HU):
                            hh = HU * u + h
                            ins = nc.vector.scalar_tensor_tensor(out=G[:, hh, :], in0=heads(ob[u])[:, h, :],
                                                                 scalar=rs[:, 1, hh:hh + 1], in1=zg[:, c, hh, :],
                                                                 op0=ALU.mult, op1=ALU.mult)
                        ins.then_inc(g_ready, 1)
                elif step == "out":
                    c, = arg
                    dve.wait_ge(xres_in[c], g * 16 + 16)
                    dve.wait_ge(out_mm, g * GC + c + 1)
                    nc.vector.tensor_tensor(xres[:, c, :], ob[0][:, 0:D], xres[:, c, :], ALU.add).then_inc(x2_ready, 1)

            def stages(g, a, par):
                for step, *arg in STEPS:
                    if g is not None:
                        finish(step, arg, g)
                    if a is not None:
                        prepare(step, arg, g, a, par)

            stages(None, 0, 0)
            with dve.Fori(0, (NG - 1) // 2) as i:
                stages(2 * i, 2 * i + 1, 1)
                stages(2 * i + 1, 2 * i + 2, 0)
            stages(NG - 2, NG - 1, 1)
            stages(NG - 1, None, 0)
            for e in range(NE):
                dve.wait_ge(f_whi, e + 1)
                nc.vector.scalar_tensor_tensor(out=w1_lo[:, e, :], in0=w1raw[:, e, :], scalar=WSCALE,
                                               in1=w1_hi[:, e, :], op0=ALU.mult, op1=ALU.subtract).then_inc(f_wlo, 1)
            dve.wait_ge(f_small, 64)
            dve.wait_ge(s_x, 64 + 16)
            dve.sem_inc(f_y, 1)
            base0 = CHAIN_PREP
            with dve.Fori(0, NCH // TW) as i:
                count[0] = 0
                base = i * F_PER + base0
                layernorm(i, xn2, base).then_inc(f_acc, 1)
                dve.wait_ge(f_xhi, i + 1)
                nc.vector.tensor_tensor(x2_lo[:, :], kx[0][:, :], x2_hi[:, :], ALU.subtract).then_inc(f_xlo, 1)
                lg, df, ex, wt = (r.rearrange("p (a b) -> p a b", b=NE) for r in rt)
                dve.wait_ge(f_lg, i + 1)
                link(nc.vector.tensor_tensor(lg, kx[1][:, 0:TW * NE].rearrange("p (a b) -> p a b", b=NE),
                                             bc(rb[:, :].rearrange("p (o e) -> p o e", o=1), [128, TW, NE]), ALU.add), base)
                link(nc.vector.tensor_reduce(mx[:, 0, :], lg, AX.X, ALU.max), base)
                col = lambda t: t.rearrange("p (a o) -> p a o", o=1)
                nc.vector.tensor_tensor(df, lg, bc(col(mx[:, 0, :]), [128, TW, NE]), ALU.subtract).then_inc(f_sub, 1)
                four = [128, TW, NE, NE]
                lj = bc(lg.rearrange("p a (o j) -> p a o j", o=1), four)
                le = bc(lg.rearrange("p a (e o) -> p a e o", o=1), four)
                nc.vector.tensor_tensor(cmp[:, 0], lj, le, ALU.is_gt)
                link(nc.vector.tensor_tensor(cmp[:, 1], lj, le, ALU.is_equal), base)
                link(nc.vector.tensor_tensor(cmp[:, 1], cmp[:, 1],
                                             bc(tri[:, :, :].rearrange("p (o e) j -> p o e j", o=1), four), ALU.mult), base)
                link(nc.vector.tensor_tensor(cmp[:, 0], cmp[:, 0], cmp[:, 1], ALU.add), base)
                link(nc.vector.tensor_reduce(lg, cmp[:, 0], AX.X, ALU.add), base)
                dve.wait_ge(f_exp, i + 1)
                link(nc.vector.scalar_tensor_tensor(out=wt, in0=lg, scalar=2.0, in1=ex, op0=ALU.is_lt, op1=ALU.mult), base)
                link(nc.vector.tensor_reduce(mx[:, 1, :], wt, AX.X, ALU.add), base)
                link(nc.vector.reciprocal(mx[:, 1, :], mx[:, 1, :]), base)
                dve.wait_ge(f_y, i * NE + 1)
                nc.vector.tensor_tensor(wts[:, :, :], wt, bc(col(mx[:, 1, :]), [128, TW, NE]), ALU.mult).then_inc(f_acc, 1)
                assert count[0] == F_PER
                dve.wait_ge(f_b2, i + 1)
                xs = x_sb[:, ds(i * TW, TW), :]
                nc.vector.tensor_tensor(acc[:, :, :], kx[0][:, :].rearrange("p (a b) -> p a b", b=D), xs,
                                        ALU.add).then_inc(f_acc, 1)
                for e in range(NE):
                    dve.wait_ge(f_y_mm, i * NE + e + 3)
                    if e == 0:
                        dve.wait_ge(f_acc, i * 3 + 3)
                    else:
                        dve.wait_ge(f_y, i * NE + e + 1)
                    dst = xs if e == NE - 1 else acc[:, :, :]
                    py = rc[e % 2][:, :].rearrange("p (a b) -> p a b", b=D)
                    for j in range(TW):
                        ins = nc.vector.scalar_tensor_tensor(
                            out=x_sb[:, ds(i * TW + j, 1), :].rearrange("p a d -> p (a d)") if e == NE - 1 else acc[:, j, :],
                            in0=py[:, j, :], scalar=wts[:, j, e:e + 1],
                            in1=acc[:, j, :], op0=ALU.mult, op1=ALU.add)
                    ins.then_inc(f_y, 1)

        @block.tensor
        def _(pe):
            mm, tr = nc.tensor.matmul, nc.tensor.transpose

            def carry(o):
                mm(o, wab_hi[:, :], wab_hi[:, :], start=True, stop=True)
            pe.wait_ge(s_const, 128)
            pe.wait_ge(s_wsplit, 1)
            with pe.Fori(0, NCH // TW) as i:
                pe.wait_ge(s_xn, i + 1)
                for j in range(TW):
                    ins = tr(pj[0][:, C * j:C * j + C], xn[:, j, :], ident[:, :])
                ins.then_inc(s_xt, 1)
                pe.wait_ge(s_xlo, i + 1)
                for j in range(TW):
                    hi = xtile(xn_hi, i)[:, C * j:C * j + C]
                    lo = xtile(xn_lo, i)[:, C * j:C * j + C]
                    o = kx[0][:, 2 * H * j:2 * H * j + 2 * H]
                    mm(o, hi, wab_hi[:, :], start=True, stop=False)
                    mm(o, hi, wab_lo[:, :], start=False, stop=False)
                    ins = mm(o, lo, wab_hi[:, :], start=False, stop=True)
                ins.then_inc(s_ab, 1)
            pe.wait_ge(s_alpha, 1)
            for b in range(B):
                ins = tr(pj[0][:, C * b:C * b + C], alpha_t[:, C * b:C * b + C], ident[:, :])
            ins.then_inc(s_arow, 1)
            pe.wait_ge(s_crow, 1)
            for b in range(B):
                ins = tr(pj[1][:, C * b:C * b + C], crow[:, b, :], ident[:, :])
            ins.then_inc(s_ccol, 1)
            pe.wait_ge(s_zero, 1)
            pe.wait_ge(s_ncum, 1)
            def wait_kx(step, c, u, g, a):
                k = KX_USES.index((step, c)) - 1
                while True:
                    kind, c0 = KX_USES[k]
                    if k < 0:
                        if g is not None:
                            pe.wait_ge(R_ready, g * GC + GC)
                        return
                    if (g if kind == "g" else a) is not None:
                        pe.wait_ge(KX_TAKEN[kind], (g if kind == "g" else a) * HALVES
                                   + U * c0 + u + 1 + (HALVES if kind == "g" else 0))
                        return
                    k -= 1

            def prepare(step, arg, g, a, par):
                def project(n):
                    t = order[n]
                    if n >= 2:
                        pe.wait_ge(raw_ready, a * NT + n - 1)
                    else:
                        pe.wait_ge(zg_ready, a * HALVES + U * (GC - 1) + n + 1)
                    w = slice(128 * t, 128 * t + 128)
                    cols = ds(column(a, 0) - PAD, W)
                    o = pj[n % 2][:, 0:W]
                    mm(o, wq_hi[:, w], xflat(xn_hi)[:, cols], start=True, stop=False)
                    mm(o, wq_lo[:, w], xflat(xn_hi)[:, cols], start=False, stop=False)
                    mm(o, wq_hi[:, w], xflat(xn_lo)[:, cols], start=False, stop=True).then_inc(proj_ready, 1)

                def by_head(c, u, lhs, rhs_, done, need):
                    pe.wait_ge(conv_done, a * NT + need + RING)
                    wait_kx(step, c, u, g, a)
                    for h in range(HU):
                        hh = HU * u + h
                        o = heads(kx[u])[:, h, :]
                        cs = slice(C * c, C * c + C)
                        if rhs_ is None:
                            ins = tr(o, lhs[:, hh, cs], ident[:, :])
                        else:
                            ins = mm(o, lhs[:, hh, cs], rhs_[:, hh, cs], start=True, stop=True)
                    ins.then_inc(done, 1)

                if step == "begin":
                    project(0)
                    project(1)
                elif step == "conv" and arg[0] + AHEAD + 2 < NT:
                    project(arg[0] + AHEAD + 2)
                elif step == "kk":
                    for u in range(U):
                        by_head(arg[0], u, kT[par], kT[par], kk_ready, H)
                elif step == "ktr":
                    for u in range(U):
                        by_head(arg[0], u, kT[par], None, ktr_ready, H)
                elif step == "kq":
                    for u in range(U):
                        by_head(arg[0], u, kT[par], qT[par], kq_ready, 3 * H)
                elif step == "vtr":
                    for u in range(U):
                        by_head(arg[0], u, vT, None, vtr_ready, 2 * H)
                elif step == "z":
                    c, = arg
                    for u in range(U):
                        if c == 0:
                            pe.wait_ge(raw_ready, a * NT + NT - 1 + u)
                        else:
                            pe.wait_ge(zg_ready, a * HALVES + U * (c - 1) + u + 1 + HALVES)
                        cols = ds(column(a, c), C)
                        hi, lo = xflat(xn_hi)[:, cols], xflat(xn_lo)[:, cols]
                        w = slice(512 * u, 512 * u + 512)
                        mm(pj[u][:, :], hi, wz_hi[:, w], start=True, stop=False)
                        mm(pj[u][:, :], hi, wz_lo[:, w], start=False, stop=False)
                        mm(pj[u][:, :], lo, wz_hi[:, w], start=False, stop=True).then_inc(z_mm, 1)

            def merge(g, c, hop):
                k = g * GC + c
                y_bank, r_bank = merge_banks[c]
                if hop == 0:
                    pe.wait_ge(t_in, g * (16 * GC * NB) + 16 * GC * NB)
                    pe.wait_ge(rdiag, k + 1)
                    if c == 0:
                        pe.wait_ge(x2_ready, k + 1)
                    else:
                        pe.wait_ge(v_ready, g * HALVES + HALVES)
                    carry(y_bank[0:2 * H, 0:2 * H])
                    py = y_bank[:, 0:H * BLK].rearrange("p (h c) -> p h c", h=H)
                    for h in range(H):
                        mm(py[32:64, h], Nm[0:32, c, h, 32:64], T64[0:32, c, h, 0:32], start=True, stop=True)
                        ins = mm(py[96:128, h], Nm[64:96, c, h, 96:128], T32[64:96, c, h, :], start=True, stop=True)
                    ins.then_inc(y32_mm, 1)
                elif hop == 1:
                    pe.wait_ge(y32_sb, k + 1)
                    if c == 0:
                        pe.wait_ge(g_ready, g * HALVES + U)
                    carry(r_bank[96:96 + 2 * H, 0:2 * H])
                    pr = r_bank[:, 0:H * BLK].rearrange("p (h c) -> p h c", h=H)
                    for h in range(H):
                        mm(pr[0:32, h], Y32[c][32:64, h, :], R[32:64, c, h, 32:64], start=True, stop=True)
                        mm(pr[32:64, h], R[32:64, c, h, 32:64], Y32[c][32:64, h, :], start=True, stop=True)
                        ins = mm(pr[64:96, h], Y32[c][96:128, h, :], R[96:128, c, h, 96:128], start=True, stop=True)
                    ins.then_inc(r32_mm, 1)
                elif hop == 2:
                    pe.wait_ge(r32_sb, k + 1)
                    carry(y_bank[0:2 * H, 0:2 * H])
                    py = y_bank[64:128, :].rearrange("p (h c) -> p h c", h=H)
                    for h in range(H):
                        ins = mm(py[:, h], Nm[0:64, c, h, 64:128], T64[0:64, c, h, :], start=True, stop=True)
                    ins.then_inc(y64_mm, 1)
                else:
                    pe.wait_ge(y64_sb, k + 1)
                    carry(r_bank[96:96 + 2 * H, 0:2 * H])
                    pr = r_bank[0:64, :].rearrange("p (h c) -> p h c", h=H)
                    for h in range(H):
                        ins = mm(pr[:, h], Y64[c][64:128, h, :], R[64:128, c, h, 64:128], start=True, stop=True)
                    ins.then_inc(r64_mm, 1)

            def finish(step, arg, g, a, par):
                if step == "merge":
                    for c in range(GC):
                        merge(g, c, *arg)
                elif step == "ks":
                    c, = arg
                    for u in range(U):
                        pe.wait_ge(S_ready, g * HALVES + U * c + u + 1)
                        for h in range(HU):
                            hh = HU * u + h
                            ins = mm(heads(rc[u])[:, h, :], kT[1 - par][:, hh, C * c:C * c + C], S[:, c, hh, :],
                                     start=True, stop=True)
                        ins.then_inc(ks_mm, 1)
                elif step == "u":
                    c, = arg
                    pe.wait_ge(R_ready, g * GC + c + 1)
                    for u in range(U):
                        pe.wait_ge(rhs_ready, g * HALVES + U * c + u + 1)
                        for h in range(HU):
                            hh = HU * u + h
                            ins = mm(heads(rc[u])[:, h, :], R[:, c, hh, :], rhs[:, hh, :], start=True, stop=True)
                        ins.then_inc(u_mm, 1)
                elif step == "sd":
                    c, = arg
                    for u in range(U):
                        pe.wait_ge(u_ready, g * HALVES + U * c + u + 1)
                        pe.wait_ge(kd_ready, g * HALVES + U * c + u + 1)
                        for h in range(HU):
                            hh = HU * u + h
                            ins = mm(heads(rc[u])[:, h, :], kd[:, c, hh, :], Us[:, hh, :], start=True, stop=True)
                        ins.then_inc(sd_mm, 1)
                elif step == "o":
                    c, = arg
                    pe.wait_ge(aq_ready, g * GC + c + 1 + GC)
                    pe.wait_ge(R_ready, g * GC + GC)
                    pe.wait_ge(x2_ready, g * GC + c + 1)
                    for u in range(U):
                        pe.wait_ge(u_ready, g * HALVES + U * c + u + 1)
                        pe.wait_ge(at_ready, g * HALVES + U * c + u + 1)
                        pe.wait_ge(g_ready, g * HALVES + U * c + u + 1)
                        for h in range(HU):
                            hh = HU * u + h
                            o = heads(ob[u])[:, h, :]
                            mm(o, qT[1 - par][:, hh, C * c:C * c + C], S[:, c, hh, :], start=True, stop=False)
                            ins = mm(o, AT[:, c, hh, :], Us[:, hh, :], start=False, stop=True)
                        ins.then_inc(o_mm, 1)
                elif step == "g":
                    c, = arg
                    for u in range(U):
                        pe.wait_ge(g_ready, g * HALVES + U * c + u + 1 + U)
                        wait_kx(step, c, u, g, a)
                        for h in range(HU):
                            ins = tr(heads(kx[u])[:, h, :], G[:, HU * u + h, :], ident[:, :])
                        ins.then_inc(gtr_mm, 1)
                elif step == "out":
                    c, = arg
                    pe.wait_ge(gt_ready, g * HALVES + U * c + 2 + HALVES)
                    for hh in range(H):
                        ins = mm(ob[0][:, 0:D], GTs[:, hh, :], ow[:, hh, :], start=(hh == 0), stop=(hh == H - 1))
                    ins.then_inc(out_mm, 1)

            def stages(g, a, par):
                for step, *arg in STEPS:
                    if g is not None:
                        finish(step, arg, g, a, par)
                    if a is not None:
                        prepare(step, arg, g, a, par)

            stages(None, 0, 0)
            with pe.Fori(0, (NG - 1) // 2) as i:
                stages(2 * i, 2 * i + 1, 1)
                stages(2 * i + 1, 2 * i + 2, 0)
            stages(NG - 2, NG - 1, 1)
            stages(NG - 1, None, 0)
            pe.wait_ge(f_small, 64)
            pe.wait_ge(f_w2, 16 * NE)
            pe.wait_ge(f_wlo, NE)
            pe.sem_inc(f_y_mm, 2)
            with pe.Fori(0, NCH // TW) as i:
                pe.wait_ge(f_acc, i * 3 + 1)
                for j in range(TW):
                    ins = tr(kx[0][:, C * j:C * j + C], xn2[:, j, :], ident[:, :])
                ins.then_inc(f_xt, 1)
                pe.wait_ge(f_xlo, i + 1)
                for j in range(TW):
                    ins = mm(kx[1][:, NE * j:NE * j + NE], x2T[:, C * j:C * j + C], rw[:, :], start=True, stop=True)
                ins.then_inc(f_lg, 1)

                def up(e):
                    for f in range(NF):
                        n = e * NF + f
                        if n >= 2:
                            pe.wait_ge(f_relu, i * (NE * NF) + n - 1)
                        w = slice(128 * f, 128 * f + 128)
                        mm(pj[f % 2][:, :], w1_hi[:, e, w], x2_hi[:, :], start=True, stop=False)
                        mm(pj[f % 2][:, :], w1_lo[:, e, w], x2_hi[:, :], start=False, stop=False)
                        mm(pj[f % 2][:, :], w1_hi[:, e, w], x2_lo[:, :], start=False, stop=True).then_inc(f_h_mm, 1)

                def down(e):
                    pe.wait_ge(f_relu, i * (NE * NF) + e * NF + NF)
                    if e >= 2:
                        pe.wait_ge(f_y, i * NE + e)
                    for j in range(TW):
                        for f in range(NF):
                            ins = mm(rc[e % 2][:, D * j:D * j + D], hbuf[:, e % 2, f, C * j:C * j + C],
                                     w2_sb[:, e, f, :], start=(f == 0), stop=(f == NF - 1))
                    ins.then_inc(f_y_mm, 1)

                up(0)
                pe.wait_ge(f_acc, i * 3 + 2)
                for j in range(TW):
                    ins = tr(kx[1][0:NE, C * j:C * j + C], wts[:, j, :], ident[:, :])
                ins.then_inc(f_wt, 1)
                pe.wait_ge(f_wtsb, i + 1)
                for j in range(TW):
                    ins = mm(kx[0][:, D * j:D * j + D], wT[0:NE, C * j:C * j + C], b2_sb[0:NE, :], start=True, stop=True)
                ins.then_inc(f_b2, 1)
                for e in range(NE):
                    if e + 1 < NE:
                        up(e + 1)
                    down(e)


def kernel(**inputs):
    import concourse.bacc as _bacc
    from concourse.bass_utils import run_bass_kernel_spmd as _run

    a = {k.replace("L0_", ""): np.asarray(v) for k, v in inputs.items()}
    t = lambda m: np.ascontiguousarray(m.T)
    NGROUPS, PER = 16, 8
    blk = 32
    par = np.zeros((2, 64, blk // 2, blk), np.float32)
    for p in range(2):
        for r in range(blk // 2):
            par[p, :, r, 2 * r + p] = 1.0
    keep = np.ones((128, NGROUPS), np.float32)
    keep[:, PER - 1::PER] = 0.0
    tri = np.broadcast_to(np.tril(np.ones((8, 8), np.float32), -1), (128, 8, 8))
    laid = [
        ("x", a["attn_hidden_states"]),
        ("qkv_t", t(a["attn_qkv_w"])),
        ("z_t", t(a["attn_z_w"])),
        ("ab_t", np.ascontiguousarray(np.concatenate([a["attn_b_w"], a["attn_a_w"]], 0).T)),
        ("conv_w", a["attn_conv_w"]),
        ("dt_bias", a["attn_dt_bias"]),
        ("a_log", a["attn_A_log"]),
        ("norm_w", a["attn_norm_w"]),
        ("out_t", t(a["attn_out_w"])),
        ("router_w", a["ffn_W_router"]),
        ("router_b", a["ffn_b_router"]),
        ("w1", a["ffn_W1"]),
        ("b1", a["ffn_b1"]),
        ("w2", a["ffn_W2"]),
        ("b2", a["ffn_b2"]),
        ("eye", np.eye(128, dtype=np.float32)),
        ("parity_eye", np.ascontiguousarray(par.reshape(128, blk // 2, blk))),
        ("low_tri", np.ascontiguousarray(tri)),
        ("keep", keep),
    ]
    nc = _bacc.Bacc("TRN2", target_bir_lowering=False, num_devices=1)
    arrays, args = {}, []
    for name, v in laid:
        v = np.ascontiguousarray(v)
        arrays[f"in_{name}"] = v
        args.append(nc.dram_tensor(f"in_{name}", v.shape, mybir.dt.from_np(v.dtype), kind="ExternalInput").ap())
    shape = a["attn_hidden_states"].shape
    args.append(nc.dram_tensor("out_0", shape, mybir.dt.float32, kind="ExternalOutput").ap())
    preln_delta_moe_kernel(nc, *args)
    r = _run(nc, [arrays], core_ids=[0])
    return r.results[0]["out_0"]
```

```python
import concourse.bass as bass
from concourse import mybir
from contextlib import ExitStack
import numpy as np


def preln_delta_moe_kernel(nc, x_in, qkv_t, z_t, ab_t, conv_w, dt_bias, a_log, norm_w, out_t,
                           router_w, router_b, w1, b1, w2, b2, eye, parity_eye, low_tri, keep_in, out):
    F32, F16, I32 = mybir.dt.float32, mybir.dt.float16, mybir.dt.int32
    ALU, ACT, AX = mybir.AluOpType, mybir.ActivationFunctionType, mybir.AxisListType
    ds = bass.ds

    B, T, D = x_in.shape
    H = ab_t.shape[1] // 2
    C = 128
    NCH = B * T // C
    GC = 2
    GT = GC * C
    NG = NCH // GC
    NT = qkv_t.shape[1] // 128
    TAPS = conv_w.shape[2]
    PAD = TAPS - 1
    W = GT + PAD
    U = 2
    HU = H // U
    BLK = 32
    NB = C // BLK
    NE = router_w.shape[1]
    FF = w1.shape[2]
    NF = FF // 128
    TW = 4
    WSCALE = 64.0
    AHEAD = 4
    RING = AHEAD + 2
    TAPB = 3

    ctx = ExitStack()
    with ctx:
        ctx.enter_context(nc.allow_non_contiguous_dma("layout of blocks"))

        def sb(name, shape, dt=F32):
            return ctx.enter_context(nc.sbuf_tensor(name, shape, dt))

        def sem(name):
            return ctx.enter_context(nc.semaphore(name))

        xn_hi = sb("xn_hi", [128, B, PAD + T], F16)
        xn_lo = sb("xn_lo", [128, B, PAD + T], F16)
        w_hi = sb("w_hi", [128, (NT + H) * 128], F16)
        w_lo = sb("w_lo", [128, (NT + H) * 128], F16)
        wq_hi, wz_hi = w_hi[:, 0:NT * 128], w_hi[:, NT * 128:]
        wq_lo, wz_lo = w_lo[:, 0:NT * 128], w_lo[:, NT * 128:]
        wab_hi = sb("wab_hi", [128, 2 * H], F16)
        wab_lo = sb("wab_lo", [128, 2 * H], F16)
        ow = sb("ow", [128, H, D])
        ident = sb("ident", [128, 128])
        par_eye = sb("par_eye", [128, BLK // 2, BLK], F16)
        tri = sb("tri", [128, NE, NE])
        keep = sb("keep", [128, NG])
        taps = sb("taps", [128, NT, TAPS])
        nw = sb("nw", [128, 1])
        dtb = sb("dtb", [128, H])
        alog = sb("alog", [128, H])
        nexp_a = sb("nexp_a", [128, H])
        beta = sb("beta", [128, NCH, H])
        neg_acum = sb("neg_acum", [128, NCH, H])
        kq = sb("kq", [128, 2, 2, H, GT])
        kT = [kq[:, p, 0] for p in range(2)]
        qT = [kq[:, p, 1] for p in range(2)]
        xres = sb("xres", [128, GC, D])
        vT = sb("vT", [128, H, GT])
        raw = sb("raw", [128, RING, 260])
        tapA = sb("tapA", [128, RING, GT])
        area = [sb(f"area{i}", [128, 2 * GC * H * C]) for i in range(4)]

        def part(i, k):
            n = GC * H * C
            return area[i][:, n * k:n * k + n].rearrange("p (g h c) -> p g h c", g=GC, h=H)
        alpha_b = part(0, 0)[:, 0]
        tapB = part(0, 0)[:, 1].rearrange("p h c -> p (h c)")[:, 0:TAPB * GT].rearrange("p (r t) -> p r t", r=TAPB)
        acum_b = part(0, 1)
        Nm, AT = part(1, 0), part(1, 1)
        kd, V = part(2, 0), part(2, 1)
        R, zg = part(3, 0), part(3, 1)
        beta_d = sb("beta_d", [128, H, C])
        decay = sb("decay", [128, GC, H, C])
        kd_scale = sb("kd_scale", [128, GC, H])
        a_end = sb("a_end", [128, GC, H])
        blkN = sb("blkN", [128, BLK, BLK])
        blkT = sb("blkT", [128, BLK // 2, BLK])
        T64 = sb("T64", [128, GC, H, 2 * BLK])
        T32 = T64[:, :, :, 0:BLK]
        Y32 = [sb("Y32", [128, H, BLK])[:, :, :]]
        Y64 = [sb("Y64", [128, H, 2 * BLK])[:, :, :]]
        prod = Y64[0].rearrange("p a b -> p (a b)").rearrange("p (a b) -> p a b", b=BLK)
        S = sb("S", [128, 2, H, 128])
        rhs = sb("rhs", [128, H, C])
        Us = sb("Us", [128, H, C])
        G = sb("G", [128, H, C])
        GTs = sb("GTs", [128, H, C])
        Y32.append(GTs[:, 4:6, :].rearrange("p a b -> p (a b)").rearrange("p (h c) -> p h c", h=H))
        Y64.append(GTs[:, 0:4, :].rearrange("p a b -> p (a b)").rearrange("p (h c) -> p h c", h=H))

        ssq = sb("ssq", [128, H])
        nac = sb("nac", [128, GC, H])
        rs = sb("rs", [128, 4, H])
        bst_t = sb("bst_t", [128, TW, 6])
        mv_t = sb("mv_t", [128, TW, 2])
        ssq4 = GTs[:, 6, :].rearrange("p (a b) -> p a b", a=4)
        mx = sb("mx", [128, 2, TW])
        cmp = beta_d[:, 0:4, :].rearrange("p a b -> p (a b)").rearrange("p (k a b c) -> p k a b c", k=2, a=TW, b=NE)
        wts = [GTs[:, 7, 32 * p:32 * p + TW * NE].rearrange("p (a b) -> p a b", b=NE) for p in range(2)]
        rw = sb("rw", [128, NE])
        rb = sb("rb", [128, NE])
        b1_sb = GTs[:, 5, 0:NE * NF].rearrange("p (a b) -> p a b", b=NF)
        b2_sb = GTs[:, 4, :]
        kflat = kT[0].rearrange("p a b -> p (a b)")
        qflat = qT[0].rearrange("p a b -> p (a b)")
        x_sb = kq[:, 1].rearrange("p k h t -> p (k h t)").rearrange("p (c d) -> p c d", d=D)
        vflat = vT[:, :, :].rearrange("p a b -> p (a b)")
        ab = vflat[:, 1024:1024 + NCH * 2 * H].rearrange("p (c k) -> p c k", c=NCH)
        rows = AT[:, 0, 0:2, :]
        rows0 = AT[:, 0, 2:4, :]
        crow = AT[:, 0, 4:6, :]
        zrow = AT[:, 0, 6, :]
        alpha_t = kd[:, 0, 0:2, :].rearrange("p a b -> p (a b)")
        tmp = [kd[:, 1, 2 * i:2 * i + 2, :].rearrange("p a b -> p (a b)") for i in range(4)]
        par_eye32 = AT[:, 1, 0:4, :].rearrange("p h c -> p (h c)").rearrange("p (a b) -> p a b", b=BLK)
        xn = [V[:, 0, TW * p:TW * p + TW, :] for p in range(2)]
        stats = kd[:, 0, 2:4, :].rearrange("p a b -> p (a b)")
        bst_all = stats[:, 0:6 * NCH].rearrange("p (c k) -> p c k", k=6)
        mv_all = stats[:, 6 * NCH:8 * NCH].rearrange("p (c k) -> p c k", k=2)
        rs_all = kd[:, 0, 4, :].rearrange("p (k c) -> p k c", c=NCH)
        bst = bst_t[:, :, :]
        mv = mv_t[:, :, :]

        pj = [ctx.enter_context(nc.psum_tensor(f"pj{i}", [128, 512], F32)) for i in range(2)]
        kx = [ctx.enter_context(nc.psum_tensor(f"kx{i}", [128, 512], F32)) for i in range(2)]
        rc = [ctx.enter_context(nc.psum_tensor(f"rc{i}", [128, 512], F32)) for i in range(2)]
        ob = [ctx.enter_context(nc.psum_tensor(f"ob{i}", [128, 512], F32)) for i in range(2)]

        merge_banks = [ob, kx]

        def heads(bank):
            return bank[:, :].rearrange("p (h c) -> p h c", h=HU)

        scr_alpha = nc.dram_tensor("scr_alpha", (B, 128, C), F32, kind="Internal").ap()
        scr_acum = nc.dram_tensor("scr_acum", (B, 128, C), F32, kind="Internal").ap()
        scr_x2 = nc.dram_tensor("scr_x2", (128, NCH, D), F32, kind="Internal").ap()
        scr_n = nc.dram_tensor("scr_n", (GC * NB * H, BLK, BLK), F32, kind="Internal").ap()
        scr_t = nc.dram_tensor("scr_t", (GC * NB * H, BLK, BLK), F32, kind="Internal").ap()
        alpha_rows = scr_alpha.rearrange("b (c h) t -> (b c) (h t)", h=H)
        acum_rows = scr_acum.rearrange("b (c h) t -> (b c) (h t)", h=H)

        def sems(names):
            return [sem(n) for n in names.split()]
        (s_const, s_x, s_stats, s_wraw, s_whi, s_wsplit, s_zero, s_xn, s_xt, s_xhi, s_xlo, s_ab, s_abc, s_chain, s_nexp,
         s_gate_e, s_gate_u, s_g, s_alpha, s_arow, s_arow_sb, s_crow, s_ccol, s_ncum, s_scr) = sems(
            "s_const s_x s_stats s_wraw s_whi s_wsplit s_zero s_xn s_xt s_xhi s_xlo s_ab s_abc s_chain s_nexp "
            "s_gate_e s_gate_u s_g s_alpha s_arow s_arow_sb s_crow s_ccol s_ncum s_scr")
        proj_ready, raw_ready, prod_ready, sum_ready, conv_mid, conv_done = sems(
            "proj_ready raw_ready prod_ready sum_ready conv_mid conv_done")
        alpha_in, acum_in = sem("alpha_in"), sems("acum_in0 acum_in1")
        (diag_ready, decay_done, kk_ready, n_ready, ktr_ready, kd_ready, scale_ready, kq_ready, at_ready, aq_ready,
         vtr_ready, v_ready, z_mm, z_tanh, zg_ready) = sems(
            "diag_ready decay_done kk_ready n_ready ktr_ready kd_ready scale_ready kq_ready at_ready aq_ready "
            "vtr_ready v_ready z_mm z_tanh zg_ready")
        (n_out, blk_in, inv_step, inv_done, t_out, t_in, rdiag, y32_mm, y32_sb, r32_mm, r32_sb, y64_mm, y64_sb,
         r64_mm, R_ready) = sems(
            "n_out blk_in inv_step inv_done t_out t_in rdiag y32_mm y32_sb r32_mm r32_sb y64_mm y64_sb r64_mm R_ready")
        (ks_mm, rhs_ready, u_mm, u_ready, sd_mm, S_ready, o_mm, sq_done, rms_step, g_ready, gtr_mm, gt_ready, out_mm,
         x2_ready) = sems(
            "ks_mm rhs_ready u_mm u_ready sd_mm S_ready o_mm sq_done rms_step g_ready gtr_mm gt_ready out_mm x2_ready")
        x2_out, xres_in = sem("x2_out"), sems("xres_in0 xres_in1")
        (f_w1raw, f_w2raw, f_small, f_whi, f_wlo, f_xt, f_xhi, f_xlo, f_lg, f_sub, f_exp, f_wt, f_wtsb, f_b2,
         f_acc, f_h_mm, f_relu, f_lo, f_y_mm, f_y, f_out) = sems(
            "f_w1raw f_w2raw f_small f_whi f_wlo f_xt f_xhi f_xlo f_lg f_sub f_exp f_wt f_wtsb f_b2 "
            "f_acc f_h_mm f_relu f_lo f_y_mm f_y f_out")

        block = ctx.enter_context(nc.Block())

        def rsqrt_step(s, v, y, t):
            if s == 0:
                return nc.vector.tensor_single_scalar(t.bitcast(I32), v.bitcast(I32), 1, ALU.arith_shift_right)
            if s == 1:
                return nc.vector.tensor_scalar(y.bitcast(I32), t.bitcast(I32), -1.0, float(0x5F3759DF), ALU.mult, ALU.add)
            if s % 3 == 2:
                return nc.vector.tensor_tensor(t, y, y, ALU.mult)
            if s % 3 == 0:
                return nc.vector.scalar_tensor_tensor(out=t, in0=t, scalar=-0.5, in1=v, op0=ALU.mult, op1=ALU.mult)
            return nc.vector.scalar_tensor_tensor(out=y, in0=t, scalar=1.5, in1=y, op0=ALU.add, op1=ALU.mult)
        RSQ = 2 + 3 * 3

        HALVES = GC * U

        order = [H + h for h in range(H)] + [2 * H + h for h in range(H)] + list(range(H))
        INV = 2 * BLK
        RMS = 1 + RSQ

        def woven(*lists):
            return [x[i] for i in range(max(map(len, lists))) for x in lists if i < len(x)]

        def tiles(n0, n1, fill=()):
            out, fill = [], list(fill)
            per = -(-len(fill) // (2 * (n1 - n0)))
            for n in range(n0, n1):
                out += [("conv", n), ("first", n + 1)] + fill[:per] + [("last", n)] + fill[per:2 * per]
                fill = fill[2 * per:]
            return out

        def inv(s0, s1):
            return [("inv", s) for s in range(s0, s1)]

        def rms(c):
            return [("rms", c, s) for s in range(RMS)]

        STEPS = ([("begin",)] + tiles(-AHEAD, -2) + [("rdiag", 0), ("rdiag", 1), ("merge", 0, 0), ("ks", 0), ("merge", 1, 0)]
                 + tiles(-2, 1) + [("merge", 0, 1)] + tiles(1, 2) + [("aq", 0), ("merge", 1, 1), ("scan", 0)]
                 + tiles(2, 3) + [("merge", 0, 2)] + tiles(3, 4) + [("merge", 1, 2)] + tiles(4, 5) + [("merge", 0, 3), ("aq", 1)]
                 + tiles(5, 6) + [("scan", 1), ("merge", 1, 3)] + tiles(6, 8) + [("u", 0)] + tiles(8, 9) + [("kk", 0)]
                 + tiles(9, 10) + [("sd", 0)] + tiles(10, 11) + [("kk", 1)] + [("scale", 0), ("ks", 1), ("ktr", 0)]
                 + tiles(11, 12) + [("o", 0), ("u", 1)] + tiles(12, 14) + inv(0, 10) + [("sd", 1)]
                 + tiles(14, 15, inv(10, 12) + rms(0)) + [("g", 0), ("scale", 1)] + tiles(15, 16, inv(12, 20))
                 + [("ktr", 1)] + tiles(16, 17, inv(20, 24)) + [("out", 0), ("o", 1)] + inv(24, 34)
                 + tiles(17, 18, inv(34, 36)) + [("vtr", 0)] + woven(rms(1), inv(36, 36 + RMS)) + [("g", 1)]
                 + tiles(18, 19, inv(36 + RMS, 54)) + inv(54, 60) + [("out", 1)] + tiles(19, 20) + inv(60, INV)
                 + [("vtr", 1), ("z", 0)] + tiles(20, 22) + [("z", 1)] + tiles(22, 24) + [("kq", 0), ("kq", 1)])
        KX_USES = [(s, c) for s, *arg in STEPS if s in ("kk", "g", "ktr", "kq", "vtr") for c in arg]
        KX_TAKEN = {"kk": n_ready, "ktr": kd_ready, "kq": at_ready, "vtr": v_ready, "g": gt_ready}
        RMS_STEPS = 1 + RSQ
        f32n = lambda v: float(np.float32(v))
        ATANH = [f32n(1.0 / (2 * k + 1)) for k in range(9)]

        def column(g, c):
            return g * GT + (g // (NG // B)) * PAD + PAD + C * c

        def xflat(t):
            return t[:, :, :].rearrange("p b t -> p (b t)")

        def xtile(t, i):
            return xflat(t)[:, ds(i * (TW * C) + (i // (T // (TW * C))) * PAD + PAD, TW * C)]

        def bc(ap, shape):
            return ap.to_broadcast(shape)

        CHAIN_PREP = RMS_STEPS + 19
        F_PER = 2 + RMS_STEPS + 9

        w1_raw = kq[:, 0].rearrange("p k h t -> p (k h t)").rearrange("p (e n) -> p e n", e=NE)
        w2_raw = [b.rearrange("p (e n) -> p e n", e=NE // 2) for b in
                  (vflat, decay[:, :, :, :].rearrange("p g h c -> p (g h c)"))]
        w1_hi, w1_lo = (xflat(t)[:, 0:NE * FF].rearrange("p (e n) -> p e n", e=NE) for t in (xn_hi, xn_lo))
        w2_hi, w2_lo = (t[:, :].rearrange("p (e n) -> p e n", e=NE) for t in (w_hi, w_lo))
        h16 = area[1][:, :].bitcast(F16).rearrange("p (k r f n) -> p k r f n", k=2, r=2, f=NF)
        h_hi, h_lo = h16[:, 0], h16[:, 1]
        h32 = area[3][:, 0:NF * 512].rearrange("p (f n) -> p f n", f=NF)
        h_bank = pj + ob
        xn2 = G[:, 0:TW, :]
        acc = [G[:, TW:2 * TW, :], rhs[:, TW:2 * TW, :]]
        x2T = rhs[:, 0:TW, :].rearrange("p a b -> p (a b)")
        x2_hi, x2_lo = ([Us[:, 4 * p + k:4 * p + k + 2, :].rearrange("p a b -> p (a b)").bitcast(F16) for p in range(2)]
                        for k in (0, 2))
        wT = GTs[:, 0:TW, :].rearrange("p a b -> p (a b)")
        rt = [ssq4[:, k, :] for k in range(4)]

        TILES = NCH // TW
        FSTEPS = [("expert", 0), ("norm",), ("expert", 1), ("expert", 2), ("turn",), ("expert", 3), ("logits",), ("expert", 4),
                  ("rank",), ("expert", 5), ("weights",), ("expert", 6), ("bias",), ("expert", 7)]

        def split_piece(n):
            e = n % NE
            if n < NE:
                return w1_raw[:, e, :], w1_hi[:, e, :], w1_lo[:, e, :]
            return w2_raw[e // (NE // 2)][:, e % (NE // 2), :], w2_hi[:, e, :], w2_lo[:, e, :]
        SPLIT_AT = NT - 2 * NE

        @block.sync
        def _(sp):
            xt = x_in.rearrange("b (c p) d -> p (b c) d", p=128)
            for i in range(4):
                sp.dma_start(x_sb[:, 8 * i:8 * i + 8, :], xt[:, 8 * i:8 * i + 8, :]).then_inc(s_x, 16)
            for dst, src in ((ident, eye), (par_eye32, parity_eye), (tri, low_tri), (keep, keep_in),
                             (taps, conv_w.rearrange("(t p) o k -> p t (o k)", p=128)),
                             (nw, norm_w.rearrange("(p o) -> p o", o=1)),
                             (dtb, bc(dt_bias.rearrange("(o h) -> o h", o=1), [128, H])),
                             (alog, bc(a_log.rearrange("(o h) -> o h", o=1), [128, H]))):
                sp.dma_start(dst[tuple(slice(None) for _ in dst.shape)], src).then_inc(s_const, 16)
            sp.dma_start(kflat, qkv_t[:, 0:2048]).then_inc(s_wraw, 16)
            sp.dma_start(qflat[:, 0:1024], qkv_t[:, 2048:3072]).then_inc(s_wraw, 16)
            sp.dma_start(qflat[:, 1024:2048], z_t).then_inc(s_wraw, 16)
            sp.dma_start(vflat[:, 0:16], ab_t).then_inc(s_wraw, 16)
            sp.dma_start(ow[:, :, :], out_t.rearrange("(h p) d -> p h d", p=128)).then_inc(s_wraw, 16)
            sp.wait_ge(s_crow, 1)
            sp.dma_start(scr_alpha.rearrange("b p t -> p b t"), rows0).then_inc(s_scr, 16)
            sp.dma_start(scr_acum.rearrange("b p t -> p b t"), crow).then_inc(s_scr, 16)
            sp.wait_ge(s_scr, 32)
            sp.sem_inc(x2_out, 16)

            def alphas(a, c):
                sp.wait_ge(s_scr, 32)
                sp.wait_ge(decay_done, a * GC + c + GC)
                sp.dma_start(alpha_b.rearrange("p h t -> p (h t)"),
                             bc(alpha_rows[ds(a * GC + c, 1), :], [128, H * C])).then_inc(alpha_in, 16)

            def products(a):
                for c in range(GC):
                    sp.wait_ge(s_scr, 32)
                    sp.wait_ge(aq_ready, a * GC + c + 1)
                    sp.wait_ge(scale_ready, a * GC + c + 1)
                    sp.dma_start(acum_b[:, c, :, :].rearrange("p h t -> p (h t)"),
                                 bc(acum_rows[ds(a * GC + c, 1), :], [128, H * C])).then_inc(acum_in[c], 16)

            def blocks_out(a):
                for c in range(GC):
                    sp.wait_ge(n_ready, a * HALVES + U * c + 2)
                    for b in range(NB):
                        q = (c * NB + b) * H
                        sp.dma_start(scr_n[q:q + H].rearrange("h i j -> i h j"),
                                     Nm[BLK * b:BLK * b + BLK, c, :, BLK * b:BLK * b + BLK]).then_inc(n_out, 16)
                sp.wait_ge(inv_done, a + 1)
                sp.wait_ge(n_out, a * (16 * GC * NB) + 16 * GC * NB)
                for par in range(2):
                    sp.dma_start(blkN[64 * par:64 * par + 64, :, :], scr_n).then_inc(blk_in, 16)

            def inverses_in(a):
                sp.wait_ge(s_scr, 32)
                sp.wait_ge(inv_done, a + 2)
                for par in range(2):
                    sp.dma_start(scr_t.rearrange("q (a p) m -> p q a m", p=2)[par],
                                 blkT[64 * par:64 * par + 64, :, :]).then_inc(t_out, 16)
                sp.wait_ge(s_scr, 32)
                sp.wait_ge(t_out, a * 32 + 32)
                for c in range(GC):
                    for b in range(NB):
                        q = (c * NB + b) * H
                        r = slice(BLK * b, BLK * b + BLK)
                        dst = T64[r, c, :, r] if b < 2 else T32[r, c, :, :]
                        sp.dma_start(dst, scr_t[q:q + H].rearrange("h i j -> i h j")).then_inc(t_in, 16)

            def x_load(g):
                for c in range(GC):
                    sp.wait_ge(s_scr, 32)
                    sp.wait_ge(x2_out, g * (16 * GC) + 16)
                    sp.dma_start(xres[:, c, :], xt[:, ds(g * GC + c, 1), :].rearrange("p a d -> p (a d)")
                                 ).then_inc(xres_in[c], 16)

            def x2_store(g, c):
                sp.wait_ge(s_scr, 32)
                sp.wait_ge(x2_ready, g * GC + c + 2)
                sp.dma_start(scr_x2[:, ds(g * GC + c, 1), :].rearrange("p a d -> p (a d)"), xres[:, c, :]).then_inc(x2_out, 16)

            def joined(g):
                alphas(g + 1, 0)
                x_load(g)
                alphas(g + 1, 1)
                products(g + 1)
                blocks_out(g + 1)
                x2_store(g, 0)
                inverses_in(g + 1)
                x2_store(g, 1)

            alphas(0, 0)
            alphas(0, 1)
            products(0)
            blocks_out(0)
            inverses_in(0)
            with sp.Fori(0, (NG - 1) // 2) as i:
                joined(2 * i)
                joined(2 * i + 1)
            joined(NG - 2)
            x_load(NG - 1)
            sp.wait_ge(x2_ready, NCH - GC + 1)
            for e in range(NE):
                sp.dma_start(w1_raw[:, e, :], w1[e]).then_inc(f_w1raw, 16)
            sp.wait_ge(v_ready, NG * HALVES)
            sp.wait_ge(at_ready, NG * HALVES)
            for e in range(NE):
                sp.dma_start(w2_raw[e // (NE // 2)][:, e % (NE // 2), :].rearrange("p (f d) -> p f d", f=NF),
                             w2[e].rearrange("(f p) d -> p f d", p=128)).then_inc(f_w2raw, 16)
            x2_store(NG - 1, 0)
            x2_store(NG - 1, 1)
            sp.wait_ge(x2_out, 16 * NCH + 16)
            sp.dma_start(x_sb, scr_x2).then_inc(s_x, 16)
            sp.wait_ge(x2_ready, NCH + 1)
            sp.dma_start(rw[:, :], router_w).then_inc(f_small, 16)
            sp.dma_start(rb[:, :], bc(router_b.rearrange("(o e) -> o e", o=1), [128, NE])).then_inc(f_small, 16)
            sp.dma_start(b1_sb[:, :, :], b1.rearrange("e (f p) -> p e f", p=128)).then_inc(f_small, 16)
            sp.dma_start(b2_sb[0:NE, :], b2).then_inc(f_small, 16)
            yt = out.rearrange("b (c p) d -> p (b c) d", p=128)
            with sp.Fori(0, NCH // TW) as i:
                sp.wait_ge(f_y, i * NE + NE + 1)
                sp.dma_start(yt[:, ds(i * TW, TW), :], x_sb[:, ds(i * TW, TW), :]).then_inc(f_out, 16)
            sp.wait_ge(f_out, 16 * (NCH // TW))

        @block.gpsimd
        def _(pool):
            nc.gpsimd.memset(T64[:, :, :, :], 0.0)
            nc.gpsimd.memset(R, 0.0)
            nc.gpsimd.memset(S[:, :, :, :], 0.0)
            nc.gpsimd.memset(xn_hi[:, :, 0:PAD], 0.0)
            nc.gpsimd.memset(xn_lo[:, :, 0:PAD], 0.0).then_inc(s_zero, 1)
            pool.sem_inc(aq_ready, GC)
            pool.wait_ge(s_const, 128)
            pool.wait_ge(s_g, 1)
            pool.sem_inc(sum_ready, TAPB)

            def stages(g, a, par):
                def diag(c):
                    pool.wait_ge(decay_done, a * GC + c + GC)
                    nc.gpsimd.tensor_tensor(
                        beta_d[:, :, :], bc(ident[:, :].rearrange("p (o c) -> p o c", o=1), [128, H, C]),
                        bc(beta[:, ds(a * GC + c, 1), :].rearrange("p o (h u) -> p (o h) u", u=1), [128, H, C]),
                        ALU.mult).then_inc(diag_ready, 1)

                def add(n):
                    pool.wait_ge(prod_ready, a * NT + n + 1)
                    nc.gpsimd.tensor_tensor(tapA[:, n % RING, :], tapA[:, n % RING, :], tapB[:, n % TAPB, :],
                                            ALU.add).then_inc(sum_ready, 1)

                for step, *arg in STEPS:
                    if step == "begin" and a is not None:
                        diag(0)
                    elif step == "conv" and a is not None and arg[0] + AHEAD < NT:
                        add(arg[0] + AHEAD)
                    elif step == "scan" and a is not None and arg[0] == 0:
                        diag(1)
                    elif step == "aq" and g is not None:
                        c, = arg
                        pool.wait_ge(acum_in[c], g * 16 + 16)
                        pool.wait_ge(kq_ready, g * HALVES + U * c + 2)
                        qc = qT[1 - par][:, :, C * c:C * c + C]
                        nc.gpsimd.tensor_tensor(qc, qc, acum_b[:, c, :, :], ALU.mult).then_inc(aq_ready, 1)

            stages(None, 0, 0)
            with pool.Fori(0, (NG - 1) // 2) as i:
                stages(2 * i, 2 * i + 1, 1)
                stages(2 * i + 1, 2 * i + 2, 0)
            stages(NG - 2, NG - 1, 1)
            stages(NG - 1, None, 0)

        @block.scalar
        def _(act):
            act.wait_ge(s_wraw, 80)
            for dst, src in ((wq_hi[:, 0:2048], kflat), (wq_hi[:, 2048:3072], qflat[:, 0:1024]),
                             (wz_hi[:, :], qflat[:, 1024:2048]), (wab_hi[:, :], vflat[:, 0:16])):
                nc.scalar.activation(dst, src, ACT.Copy, scale=WSCALE).then_inc(s_whi, 1)
            act.wait_ge(s_const, 128)
            nc.scalar.activation(nexp_a[:, :], alog[:, :], ACT.Exp).then_inc(s_nexp, 1)
            act.sem_inc(s_abc, 2)

            def high_half(t, p):
                act.wait_ge(s_xt, t + 1)
                nc.scalar.activation(xtile(xn_hi, t), pj[p][:, :], ACT.Copy).then_inc(s_xhi, 1)

            def gates_out(t, p):
                act.wait_ge(s_ab, t + 1)
                nc.scalar.activation(ab[:, ds(t * TW, TW), :].rearrange("p a b -> p (a b)"), kx[p][:, 0:TW * 2 * H],
                                     ACT.Copy, scale=1.0 / WSCALE).then_inc(s_abc, 1)
            high_half(0, 0)
            with act.Fori(0, TILES // 2 - 1) as i:
                for p in range(2):
                    high_half(2 * i + p + 1, 1 - p)
                    gates_out(2 * i + p, p)
            high_half(TILES - 1, 1)
            gates_out(TILES - 2, 0)
            gates_out(TILES - 1, 1)
            act.wait_ge(s_abc, TILES + 2)
            nc.scalar.activation(beta[:, :, :], ab[:, :, 0:H], ACT.Exp, scale=-1.0).then_inc(s_gate_e, 1)
            act.wait_ge(s_gate_u, 1)
            nc.scalar.activation(tmp[1], tmp[1], ACT.Exp, scale=-1.0).then_inc(s_gate_e, 1)
            act.wait_ge(s_g, 1)
            nc.scalar.activation(alpha_t, tmp[0], ACT.Exp, scale=-1.0).then_inc(s_alpha, 1)
            act.wait_ge(s_arow, 1)
            nc.scalar.activation(rows, pj[0][:, 0:256].rearrange("p (a b) -> p a b", a=2), ACT.Copy).then_inc(s_arow_sb, 1)
            act.wait_ge(s_ccol, 1)
            nc.scalar.activation(neg_acum[:, :, :].rearrange("p a b -> p (a b)"), pj[1][:, 0:256], ACT.Copy,
                                 scale=-1.0).then_inc(s_ncum, 1)
            act.sem_inc(gt_ready, HALVES)
            act.sem_inc(sq_done, U)

            def prepare(step, arg, a):
                def evacuate(n):
                    act.wait_ge(proj_ready, a * NT + n + 1)
                    act.wait_ge(conv_done, a * NT + n + 1)
                    nc.scalar.activation(raw[:, n % RING, 0:W], pj[n % 2][:, 0:W], ACT.Copy,
                                         scale=1.0 / WSCALE).then_inc(raw_ready, 1)

                def products(n):
                    t = order[n]
                    act.wait_ge(raw_ready, a * NT + n + 1)
                    act.wait_ge(sum_ready, a * NT + n + 1)
                    nc.scalar.activation(tapB[:, n % TAPB, :], raw[:, n % RING, 2:2 + GT], ACT.Copy,
                                         scale=taps[:, t, 2:3])
                    nc.scalar.activation(tapA[:, n % RING, :], raw[:, n % RING, 3:3 + GT], ACT.Copy,
                                         scale=taps[:, t, 3:4]).then_inc(prod_ready, 1)

                if step == "begin":
                    evacuate(0)
                elif step == "conv":
                    n, = arg
                    if n + AHEAD + 1 < NT:
                        evacuate(n + AHEAD + 1)
                    if n + AHEAD < NT:
                        products(n + AHEAD)
                elif step == "vtr":
                    c, = arg
                    for u in range(U):
                        act.wait_ge(vtr_ready, a * HALVES + U * c + u + 1)
                        nc.scalar.activation(V[:, c, HU * u:HU * u + HU, :], heads(kx[u]), ACT.Copy).then_inc(v_ready, 1)
                elif step == "z":
                    c, = arg
                    for u in range(U):
                        act.wait_ge(z_mm, a * HALVES + U * c + u + 1)
                        nc.scalar.activation(zg[:, c, HU * u:HU * u + HU, :], heads(pj[u]), ACT.Tanh,
                                             scale=0.5 / WSCALE).then_inc(z_tanh, 1)

            def finish(step, arg, g):
                if step == "merge":
                    c, hop = arg
                    k = g * GC + c
                    y_bank, r_bank = merge_banks[c]
                    if hop == 0:
                        act.wait_ge(y32_mm, k + 1)
                        py = y_bank[:, 0:H * BLK].rearrange("p (h c) -> p h c", h=H)
                        nc.scalar.activation(Y32[c][96:128], py[96:128], ACT.Copy)
                        nc.scalar.activation(Y32[c][32:64], py[32:64], ACT.Copy).then_inc(y32_sb, 1)
                    elif hop == 1:
                        act.wait_ge(r32_mm, k + 1)
                        pr = r_bank[:, 0:H * BLK].rearrange("p (h c) -> p h c", h=H)
                        nc.scalar.activation(T64[32:64, c, :, 0:32], pr[32:64], ACT.Copy, scale=-1.0)
                        nc.scalar.activation(R[64:96, c, :, 96:128], pr[64:96], ACT.Copy, scale=-1.0)
                        nc.scalar.activation(R[0:32, c, :, 32:64], pr[0:32], ACT.Copy, scale=-1.0).then_inc(r32_sb, 1)
                    elif hop == 2:
                        act.wait_ge(y64_mm, k + 1)
                        nc.scalar.activation(Y64[c][64:128], y_bank[64:128, :].rearrange("p (h c) -> p h c", h=H),
                                             ACT.Copy).then_inc(y64_sb, 1)
                    else:
                        act.wait_ge(r64_mm, k + 1)
                        nc.scalar.activation(R[0:64, c, :, 64:128], r_bank[0:64, :].rearrange("p (h c) -> p h c", h=H),
                                             ACT.Copy, scale=-1.0).then_inc(R_ready, 1)
                elif step == "u":
                    c, = arg
                    for u in range(U):
                        act.wait_ge(u_mm, g * HALVES + U * c + u + 1)
                        nc.scalar.activation(Us[:, HU * u:HU * u + HU, :], heads(rc[u]), ACT.Copy).then_inc(u_ready, 1)
                elif step == "o":
                    c, = arg
                    for u in range(U):
                        act.wait_ge(o_mm, g * HALVES + U * c + u + 1)
                        act.wait_ge(sq_done, g * HALVES + U * c + u + U)
                        for h in range(HU):
                            last = nc.scalar.activation(G[:, HU * u + h, :], heads(ob[u])[:, h, :], ACT.Square,
                                                        accum_out=ssq[:, HU * u + h:HU * u + h + 1])
                        last.then_inc(sq_done, 1)
                elif step == "g":
                    c, = arg
                    for u in range(U):
                        act.wait_ge(gtr_mm, g * HALVES + U * c + u + 1)
                        nc.scalar.activation(GTs[:, HU * u:HU * u + HU, :], heads(kx[u]), ACT.Copy).then_inc(gt_ready, 1)

            def stages(g, a):
                for step, *arg in STEPS:
                    if g is not None:
                        finish(step, arg, g)
                    if a is not None:
                        prepare(step, arg, a)
                    elif step == "conv" and arg[0] >= SPLIT_AT:
                        n = arg[0] - SPLIT_AT
                        act.wait_ge(f_w1raw if n < NE else f_w2raw, 16 * NE)
                        raw_, hi, _ = split_piece(n)
                        nc.scalar.activation(hi, raw_, ACT.Copy, scale=WSCALE).then_inc(f_whi, 1)

            stages(None, 0)
            with act.Fori(0, (NG - 1) // 2) as i:
                stages(2 * i, 2 * i + 1)
                stages(2 * i + 1, 2 * i + 2)
            stages(NG - 2, NG - 1)
            stages(NG - 1, None)
            act.wait_ge(f_small, 64)
            act.sem_inc(f_lo, NF)

            def relus(i, e):
                for f in range(NF):
                    n = e * NF + f
                    act.wait_ge(f_h_mm, i * (NE * NF) + n + 1)
                    if f == 0:
                        act.wait_ge(f_y_mm, i * NE + e + 1)
                    act.wait_ge(f_lo, i * (NE * NF) + n + 1)
                    for h in (h32[:, f, :], h_hi[:, e % 2, f, :]):
                        ins = nc.scalar.activation(h, h_bank[f][:, :], ACT.Relu, bias=b1_sb[:, e, f:f + 1],
                                                   scale=1.0 / WSCALE)
                    ins.then_inc(f_relu, 1)

            def tile_stages(i, r, par):
                for step, *arg in FSTEPS:
                    if step == "expert" and i is not None:
                        if arg[0] + 1 < NE:
                            relus(i, arg[0] + 1)
                        elif r is not None:
                            relus(r, 0)
                    elif step == "turn" and r is not None:
                        act.wait_ge(f_xt, r + 1)
                        nc.scalar.activation(x2T[:, :], kx[0][:, :], ACT.Copy)
                        nc.scalar.activation(x2_hi[par][:, :], kx[0][:, :], ACT.Copy).then_inc(f_xhi, 1)
                    elif step == "rank" and r is not None:
                        act.wait_ge(f_sub, r + 1)
                        nc.scalar.activation(rt[2], rt[1], ACT.Exp).then_inc(f_exp, 1)
                    elif step == "weights" and r is not None:
                        act.wait_ge(f_wt, r + 1)
                        nc.scalar.activation(wT[0:NE, :], kx[1][0:NE, :], ACT.Copy).then_inc(f_wtsb, 1)
            tile_stages(None, 0, 0)
            relus(0, 0)
            with act.Fori(0, (TILES - 1) // 2) as i:
                tile_stages(2 * i, 2 * i + 1, 1)
                tile_stages(2 * i + 1, 2 * i + 2, 0)
            tile_stages(TILES - 2, TILES - 1, 1)
            tile_stages(TILES - 1, None, 0)

        @block.vector
        def _(dve):
            count = [0]

            def link(ins, base=0):
                count[0] += 1
                ins.then_inc(s_chain, 1)
                dve.wait_ge(s_chain, base + count[0])

            def layernorm(i, dst, base):
                for j in range(TW):
                    ins = nc.vector.bn_stats(bst[:, j, :], x_sb[:, ds(i * TW + j, 1), :].rearrange("p a b -> p (a b)"))
                count[0] += 1
                ins.then_inc(s_chain, 1)
                dve.wait_ge(s_chain, base + count[0])
                nc.vector.memset(rs[:, 3, 0:1], 0.0)
                for j in range(TW):
                    ins = nc.vector.bn_aggr(mv[:, j, :], bst[:, j, :])
                link(ins, base)
                link(nc.vector.tensor_scalar_add(rs[:, 0, 0:TW], mv[:, :, 1], 1e-5), base)
                for s in range(RSQ):
                    link(rsqrt_step(s, rs[:, 0, 0:TW], rs[:, 1, 0:TW], rs[:, 2, 0:TW]), base)
                for j in range(TW):
                    ins = nc.vector.tensor_scalar(dst[:, j, :], x_sb[:, ds(i * TW + j, 1), :].rearrange("p a b -> p (a b)"),
                                                  mv[:, j, 0:1], rs[:, 1, j:j + 1], ALU.subtract, ALU.mult)
                return ins

            dve.wait_ge(s_x, 64)
            for c in range(NCH):
                ins = nc.vector.bn_stats(bst_all[:, c, :], x_sb[:, c, :])
            ins.then_inc(s_stats, 1)
            dve.wait_ge(s_stats, 1)
            for c in range(NCH):
                ins = nc.vector.bn_aggr(mv_all[:, c, :], bst_all[:, c, :])
            ins.then_inc(s_stats, 1)
            dve.wait_ge(s_stats, 2)
            link(nc.vector.tensor_scalar_add(rs_all[:, 0, :], mv_all[:, :, 1], 1e-5))
            for s in range(RSQ):
                link(rsqrt_step(s, rs_all[:, 0, :], rs_all[:, 1, :], rs_all[:, 2, :]))
            dve.wait_ge(s_wraw, 80)
            for k, (dst, src, hi) in enumerate(((wq_lo[:, 0:2048], kflat, wq_hi[:, 0:2048]),
                                                (wq_lo[:, 2048:3072], qflat[:, 0:1024], wq_hi[:, 2048:3072]),
                                                (wz_lo[:, :], qflat[:, 1024:2048], wz_hi[:, :]),
                                                (wab_lo[:, :], vflat[:, 0:16], wab_hi[:, :]))):
                dve.wait_ge(s_whi, k + 1)
                nc.vector.scalar_tensor_tensor(out=dst, in0=src, scalar=WSCALE, in1=hi, op0=ALU.mult, op1=ALU.subtract)
            dve.wait_ge(s_const, 128)
            nc.vector.tensor_copy(par_eye[:, :, :], par_eye32)
            nc.vector.tensor_scalar(ow[:, :, :], ow[:, :, :], nw[:, 0:1], 0.5 / WSCALE, ALU.mult,
                                    ALU.mult).then_inc(s_wsplit, 1)
            dve.sem_inc(s_xlo, 1)

            def normalise(t, p):
                for j in range(TW):
                    c = t * TW + j
                    ins = nc.vector.tensor_scalar(xn[p][:, j, :], x_sb[:, ds(c, 1), :].rearrange("p a b -> p (a b)"),
                                                  mv_all[:, ds(c, 1), 0], rs_all[:, 1, ds(c, 1)],
                                                  ALU.subtract, ALU.mult)
                ins.then_inc(s_xn, 1)

            def low_half(t, p):
                dve.wait_ge(s_xhi, t + 1)
                nc.vector.tensor_tensor(xtile(xn_lo, t), pj[p][:, :], xtile(xn_hi, t), ALU.subtract).then_inc(s_xlo, 1)
            normalise(0, 0)
            with dve.Fori(0, TILES // 2 - 1) as i:
                for p in range(2):
                    normalise(2 * i + p + 1, 1 - p)
                    low_half(2 * i + p, p)
            normalise(TILES - 1, 1)
            low_half(TILES - 2, 0)
            low_half(TILES - 1, 1)
            v3 = lambda ap: ap.rearrange("p (c h) -> p c h", h=H)
            dve.wait_ge(s_abc, TILES + 2)
            link(nc.vector.tensor_tensor(v3(tmp[0]), ab[:, :, H:2 * H],
                                         bc(dtb[:, :].rearrange("p (o h) -> p o h", o=1), [128, NCH, H]), ALU.add))
            nc.vector.scalar_tensor_tensor(out=tmp[1], in0=tmp[0], scalar=-1.0, in1=tmp[0], op0=ALU.mult,
                                           op1=ALU.max).then_inc(s_gate_u, 1)
            dve.wait_ge(s_gate_e, 1)
            link(nc.vector.tensor_scalar_add(beta[:, :, :], beta[:, :, :], 1.0))
            link(nc.vector.reciprocal(beta[:, :, :], beta[:, :, :]))
            dve.wait_ge(s_gate_e, 2)
            link(nc.vector.tensor_scalar_add(tmp[2], tmp[1], 2.0))
            link(nc.vector.reciprocal(tmp[2], tmp[2]))
            link(nc.vector.tensor_tensor(tmp[1], tmp[1], tmp[2], ALU.mult))
            link(nc.vector.tensor_tensor(tmp[2], tmp[1], tmp[1], ALU.mult))
            link(nc.vector.tensor_scalar(tmp[3], tmp[2], ATANH[8], None, ALU.mult))
            for k in range(7, 0, -1):
                link(nc.vector.scalar_tensor_tensor(out=tmp[3], in0=tmp[3], scalar=ATANH[k], in1=tmp[2],
                                                    op0=ALU.add, op1=ALU.mult))
            link(nc.vector.scalar_tensor_tensor(out=tmp[3], in0=tmp[3], scalar=1.0, in1=tmp[1], op0=ALU.add, op1=ALU.mult))
            link(nc.vector.tensor_scalar(tmp[3], tmp[3], 2.0, None, ALU.mult))
            link(nc.vector.scalar_tensor_tensor(out=tmp[0], in0=tmp[0], scalar=0.0, in1=tmp[3], op0=ALU.max, op1=ALU.add))
            dve.wait_ge(s_nexp, 1)
            nc.vector.tensor_tensor(v3(tmp[0]), v3(tmp[0]),
                                    bc(nexp_a[:, :].rearrange("p (o h) -> p o h", o=1), [128, NCH, H]),
                                    ALU.mult).then_inc(s_g, 1)
            nc.vector.memset(zrow, 0.0)
            dve.wait_ge(s_arow_sb, 1)
            link(nc.vector.tensor_copy(rows0, rows))
            assert count[0] == CHAIN_PREP
            nc.vector.memset(rows0[:, :, 0:1], 0.0)
            nc.vector.tensor_tensor_scan(crow[:, 0, :], rows[:, 0, :], zrow, 1.0, ALU.mult, ALU.add)
            nc.vector.tensor_tensor_scan(crow[:, 1, :], rows[:, 1, :], zrow, 1.0, ALU.mult, ALU.add).then_inc(s_crow, 1)
            dve.wait_ge(s_scr, 32)
            dve.wait_ge(s_ncum, 1)
            dve.wait_ge(s_zero, 1)
            dve.sem_inc(decay_done, GC)
            dve.sem_inc(scale_ready, GC)
            dve.sem_inc(conv_done, RING)
            dve.sem_inc(zg_ready, HALVES)
            dve.sem_inc(inv_done, 1)
            dve.sem_inc(x2_ready, 1)
            dve.sem_inc(S_ready, U)
            dve.sem_inc(g_ready, U)

            def half(t, c, u):
                return t[:, c, HU * u:HU * u + HU, :]

            def prepare(step, arg, g, a, par):
                if step == "first" and 0 <= arg[0] < NT:
                    n, = arg
                    dve.wait_ge(sum_ready, a * NT + n + 1 + TAPB)
                    nc.vector.scalar_tensor_tensor(out=tapA[:, n % RING, :], in0=raw[:, n % RING, 1:1 + GT],
                                                   scalar=taps[:, order[n], 1:2], in1=tapA[:, n % RING, :],
                                                   op0=ALU.mult, op1=ALU.add).then_inc(conv_mid, 1)
                elif step == "last" and arg[0] >= 0:
                    n, = arg
                    dst = (kT[par], vT, qT[par])[n // H]
                    dve.wait_ge(conv_mid, a * NT + n + 1)
                    nc.vector.scalar_tensor_tensor(out=dst[:, n % H, :], in0=raw[:, n % RING, 0:GT],
                                                   scalar=taps[:, order[n], 0:1], in1=tapA[:, n % RING, :],
                                                   op0=ALU.mult, op1=ALU.add).then_inc(conv_done, 1)
                elif step == "scan":
                    c, = arg
                    dve.wait_ge(alpha_in, a * (16 * GC) + 16 * c + 16)
                    dve.wait_ge(diag_ready, a * GC + c + 1)
                    nc.vector.tensor_tensor_scan(decay[:, c, :, :].rearrange("p h c -> p (h c)"),
                                                 alpha_b.rearrange("p h c -> p (h c)"),
                                                 beta_d[:, :, :].rearrange("p h c -> p (h c)"),
                                                 0.0, ALU.mult, ALU.add).then_inc(decay_done, 1)
                elif step == "kk":
                    c, = arg
                    for u in range(U):
                        dve.wait_ge(kk_ready, a * HALVES + U * c + u + 1)
                        dve.wait_ge(decay_done, a * GC + c + 1 + GC)
                        nc.vector.tensor_tensor(half(Nm, c, u), heads(kx[u]), half(decay, c, u),
                                                ALU.mult).then_inc(n_ready, 1)
                elif step == "inv":
                    s, = arg
                    if s:
                        dve.wait_ge(inv_step, a * (INV - 1) + s)
                    if s == 0:
                        ins = nc.vector.tensor_copy(blkT[:, :, :], par_eye[:, :, :])
                    elif s == 1:
                        dve.wait_ge(blk_in, a * 32 + 32)
                        ins = nc.vector.memset(blkN[:, :, :].rearrange("p a b -> p (a b)")[:, 0:BLK * BLK:BLK + 1], -1.0)
                    else:
                        j = BLK - 1 - s // 2
                        r0, wd = (j + 1) // 2, BLK - j
                        nr = BLK // 2 - r0
                        if s % 2 == 0:
                            ins = nc.vector.tensor_tensor(prod[:, 0:nr, 0:wd], blkT[:, r0:, j:],
                                                          bc(blkN[:, j:j + 1, j:], [128, nr, wd]), ALU.mult)
                        else:
                            ins = nc.vector.tensor_reduce(blkT[:, r0:, j:j + 1], prod[:, 0:nr, 0:wd], AX.X, ALU.add,
                                                          negate=True)
                    ins.then_inc(inv_step if s < INV - 1 else inv_done, 1)
                elif step == "scale":
                    c, = arg
                    if g is not None:
                        dve.wait_ge(S_ready, g * HALVES + U * c + 2 + U)
                    dve.wait_ge(acum_in[c], a * 16 + 16)
                    end = keep[:, ds(a, 1)] if c == GC - 1 else 1.0
                    nc.vector.tensor_scalar(kd_scale[:, c, :], decay[:, c, :, C - 1], end, None, ALU.mult)
                    nc.vector.tensor_scalar(a_end[:, c, :], acum_b[:, c, :, C - 1], end, None, ALU.mult)
                    nc.vector.tensor_copy(nac[:, c, :], neg_acum[:, ds(a * GC + c, 1), :].rearrange("p a h -> p (a h)")
                                          ).then_inc(scale_ready, 1)
                elif step == "ktr":
                    c, = arg
                    for u in range(U):
                        dve.wait_ge(ktr_ready, a * HALVES + U * c + u + 1)
                        dve.wait_ge(scale_ready, a * GC + c + 1 + GC)
                        sc = kd_scale[:, c, HU * u:HU * u + HU].rearrange("p (h o) -> p h o", o=1)
                        nc.vector.tensor_tensor(half(kd, c, u), heads(kx[u]), bc(sc, [128, HU, C]),
                                                ALU.mult).then_inc(kd_ready, 1)
                elif step == "kq":
                    c, = arg
                    for u in range(U):
                        dve.wait_ge(kq_ready, a * HALVES + U * c + u + 1)
                        nc.vector.tensor_tensor(half(AT, c, u), heads(kx[u]), half(decay, c, u),
                                                ALU.mult).then_inc(at_ready, 1)
                elif step == "z":
                    c, = arg
                    for u in range(U):
                        dve.wait_ge(z_tanh, a * HALVES + U * c + u + 1)
                        nc.vector.scalar_tensor_tensor(out=half(zg, c, u), in0=half(zg, c, u), scalar=1.0,
                                                       in1=heads(pj[u]), op0=ALU.add, op1=ALU.mult).then_inc(zg_ready, 1)

            def finish(step, arg, g):
                if step == "rdiag":
                    c, = arg
                    dve.wait_ge(t_in, g * (16 * GC * NB) + 16 * GC * NB)
                    for b in range(NB):
                        r = slice(BLK * b, BLK * b + BLK)
                        ins = nc.vector.transpose(R[r, c, :, r], T64[r, c, :, r] if b < 2 else T32[r, c, :, :])
                    ins.then_inc(rdiag, 1)
                elif step == "ks":
                    c, = arg
                    for u in range(U):
                        dve.wait_ge(ks_mm, g * HALVES + U * c + u + 1)
                        dve.wait_ge(v_ready, g * HALVES + U * c + u + 1)
                        for h in range(HU):
                            hh = HU * u + h
                            ins = nc.vector.scalar_tensor_tensor(out=rhs[:, hh, :], in0=heads(rc[u])[:, h, :],
                                                                 scalar=nac[:, c, hh:hh + 1], in1=V[:, c, hh, :],
                                                                 op0=ALU.mult, op1=ALU.add)
                        ins.then_inc(rhs_ready, 1)
                elif step == "sd":
                    c, = arg
                    for u in range(U):
                        dve.wait_ge(sd_mm, g * HALVES + U * c + u + 1)
                        for h in range(HU):
                            hh = HU * u + h
                            ins = nc.vector.scalar_tensor_tensor(out=S[:, 1 - c, hh, :], in0=S[:, c, hh, :],
                                                                 scalar=a_end[:, c, hh:hh + 1],
                                                                 in1=heads(rc[u])[:, h, :],
                                                                 op0=ALU.mult, op1=ALU.add)
                        ins.then_inc(S_ready, 1)
                elif step == "rms":
                    c, s = arg
                    if s == 0:
                        dve.wait_ge(sq_done, g * HALVES + U * c + 2 + U)
                        ins = nc.vector.tensor_scalar(rs[:, 0, 0:H], ssq[:, :], 1.0 / C, 1e-6, ALU.mult, ALU.add)
                    else:
                        dve.wait_ge(rms_step, (g * GC + c) * RMS + s)
                        ins = rsqrt_step(s - 1, rs[:, 0, 0:H], rs[:, 1, 0:H], rs[:, 2, 0:H])
                    ins.then_inc(rms_step, 1)
                elif step == "g":
                    c, = arg
                    dve.wait_ge(rms_step, (g * GC + c) * RMS + RMS)
                    for u in range(U):
                        for h in range(HU):
                            hh = HU * u + h
                            ins = nc.vector.scalar_tensor_tensor(out=G[:, hh, :], in0=heads(ob[u])[:, h, :],
                                                                 scalar=rs[:, 1, hh:hh + 1], in1=zg[:, c, hh, :],
                                                                 op0=ALU.mult, op1=ALU.mult)
                        ins.then_inc(g_ready, 1)
                elif step == "out":
                    c, = arg
                    dve.wait_ge(xres_in[c], g * 16 + 16)
                    dve.wait_ge(out_mm, g * GC + c + 1)
                    nc.vector.tensor_tensor(xres[:, c, :], ob[0][:, 0:D], xres[:, c, :], ALU.add).then_inc(x2_ready, 1)

            def stages(g, a, par):
                for step, *arg in STEPS:
                    if g is not None:
                        finish(step, arg, g)
                    if a is not None:
                        prepare(step, arg, g, a, par)
                    elif step == "last" and arg[0] >= SPLIT_AT:
                        n = arg[0] - SPLIT_AT
                        dve.wait_ge(f_whi, n + 1)
                        raw_, hi, lo = split_piece(n)
                        nc.vector.scalar_tensor_tensor(out=lo, in0=raw_, scalar=WSCALE, in1=hi, op0=ALU.mult,
                                                       op1=ALU.subtract).then_inc(f_wlo, 1)

            stages(None, 0, 0)
            with dve.Fori(0, (NG - 1) // 2) as i:
                stages(2 * i, 2 * i + 1, 1)
                stages(2 * i + 1, 2 * i + 2, 0)
            stages(NG - 2, NG - 1, 1)
            stages(NG - 1, None, 0)
            dve.wait_ge(f_small, 64)
            link(nc.vector.tensor_scalar(b2_sb[0:NE, :], b2_sb[0:NE, :], WSCALE, None, ALU.mult))
            dve.wait_ge(s_x, 64 + 16)
            dve.sem_inc(f_y, 1)
            base0 = CHAIN_PREP + 1
            col = lambda t: t.rearrange("p (a o) -> p a o", o=1)
            lg, df, ex, wt = (r.rearrange("p (a b) -> p a b", b=NE) for r in rt)
            four = [128, TW, NE, NE]

            def row(t):
                return x_sb[:, ds(t, 1), :].rearrange("p a d -> p (a d)")

            def lows(i, e):
                for f in range(NF):
                    dve.wait_ge(f_relu, i * (NE * NF) + e * NF + f + 1)
                    nc.vector.tensor_tensor(h_lo[:, e % 2, f, :], h32[:, f, :], h_hi[:, e % 2, f, :],
                                            ALU.subtract).then_inc(f_lo, 1)

            def add_expert(i, e, par):
                dve.wait_ge(f_y_mm, i * NE + e + 3)
                dve.wait_ge(f_y, i * NE + e + 1)
                py = rc[e % 2][:, :].rearrange("p (a b) -> p a b", b=D)
                for j in range(TW):
                    ins = nc.vector.scalar_tensor_tensor(
                        out=row(i * TW + j) if e == NE - 1 else acc[par][:, j, :], in0=py[:, j, :],
                        scalar=wts[par][:, j, e:e + 1], in1=acc[par][:, j, :], op0=ALU.mult, op1=ALU.add)
                ins.then_inc(f_y, 1)

            def tile_stages(i, r, par):
                for step, *arg in FSTEPS:
                    if step == "expert" and i is not None:
                        if arg[0] + 1 < NE:
                            lows(i, arg[0] + 1)
                        elif r is not None:
                            lows(r, 0)
                        add_expert(i, arg[0], 1 - par)
                    if r is None:
                        continue
                    base = r * F_PER + base0
                    if step == "norm":
                        count[0] = 0
                        layernorm(r, xn2, base).then_inc(f_acc, 1)
                    elif step == "turn":
                        dve.wait_ge(f_xhi, r + 1)
                        nc.vector.tensor_tensor(x2_lo[par][:, :], kx[0][:, :], x2_hi[par][:, :], ALU.subtract).then_inc(f_xlo, 1)
                    elif step == "logits":
                        dve.wait_ge(f_lg, r + 1)
                        link(nc.vector.tensor_tensor(lg, kx[1][:, 0:TW * NE].rearrange("p (a b) -> p a b", b=NE),
                                                     bc(rb[:, :].rearrange("p (o e) -> p o e", o=1), [128, TW, NE]),
                                                     ALU.add), base)
                        link(nc.vector.tensor_reduce(mx[:, 0, :], lg, AX.X, ALU.max), base)
                        nc.vector.tensor_tensor(df, lg, bc(col(mx[:, 0, :]), [128, TW, NE]), ALU.subtract).then_inc(f_sub, 1)
                        lj = bc(lg.rearrange("p a (o j) -> p a o j", o=1), four)
                        le = bc(lg.rearrange("p a (e o) -> p a e o", o=1), four)
                        nc.vector.tensor_tensor(cmp[:, 0], lj, le, ALU.is_gt)
                        link(nc.vector.tensor_tensor(cmp[:, 1], lj, le, ALU.is_equal), base)
                        link(nc.vector.tensor_tensor(cmp[:, 1], cmp[:, 1],
                                                     bc(tri[:, :, :].rearrange("p (o e) j -> p o e j", o=1), four),
                                                     ALU.mult), base)
                        link(nc.vector.tensor_tensor(cmp[:, 0], cmp[:, 0], cmp[:, 1], ALU.add), base)
                        link(nc.vector.tensor_reduce(lg, cmp[:, 0], AX.X, ALU.add), base)
                    elif step == "rank":
                        dve.wait_ge(f_exp, r + 1)
                        link(nc.vector.scalar_tensor_tensor(out=wt, in0=lg, scalar=2.0, in1=ex, op0=ALU.is_lt,
                                                            op1=ALU.mult), base)
                        link(nc.vector.tensor_reduce(mx[:, 1, :], wt, AX.X, ALU.add), base)
                        link(nc.vector.reciprocal(mx[:, 1, :], mx[:, 1, :]), base)
                        if i is not None:
                            dve.wait_ge(f_y, i * NE + 1)
                        nc.vector.scalar_tensor_tensor(out=wts[par], in0=wt, scalar=1.0 / WSCALE,
                                                       in1=bc(col(mx[:, 1, :]), [128, TW, NE]), op0=ALU.mult,
                                                       op1=ALU.mult).then_inc(f_acc, 1)
                        assert count[0] == F_PER
                    elif step == "bias":
                        dve.wait_ge(f_b2, r + 1)
                        nc.vector.tensor_tensor(acc[par], kx[0][:, :].rearrange("p (a b) -> p a b", b=D),
                                                x_sb[:, ds(r * TW, TW), :], ALU.add).then_inc(f_acc, 1)
            tile_stages(None, 0, 0)
            lows(0, 0)
            dve.wait_ge(f_acc, 3)
            with dve.Fori(0, (TILES - 1) // 2) as i:
                tile_stages(2 * i, 2 * i + 1, 1)
                tile_stages(2 * i + 1, 2 * i + 2, 0)
            tile_stages(TILES - 2, TILES - 1, 1)
            tile_stages(TILES - 1, None, 0)

        @block.tensor
        def _(pe):
            mm, tr = nc.tensor.matmul, nc.tensor.transpose

            def carry(o):
                mm(o, wab_hi[:, :], wab_hi[:, :], start=True, stop=True)
            pe.wait_ge(s_const, 128)
            pe.wait_ge(s_wsplit, 1)

            def turn(t, p):
                pe.wait_ge(s_xn, t + 1)
                if not isinstance(t, int) or t:
                    pe.wait_ge(s_xlo, t)
                for j in range(TW):
                    ins = tr(pj[p][:, C * j:C * j + C], xn[p][:, j, :], ident[:, :])
                ins.then_inc(s_xt, 1)

            def gates(t, p):
                pe.wait_ge(s_xlo, t + 2)
                pe.wait_ge(s_abc, t + 1)
                for j in range(TW):
                    hi = xtile(xn_hi, t)[:, C * j:C * j + C]
                    lo = xtile(xn_lo, t)[:, C * j:C * j + C]
                    o = kx[p][:, 2 * H * j:2 * H * j + 2 * H]
                    mm(o, hi, wab_hi[:, :], start=True, stop=False)
                    mm(o, hi, wab_lo[:, :], start=False, stop=False)
                    ins = mm(o, lo, wab_hi[:, :], start=False, stop=True)
                ins.then_inc(s_ab, 1)
            turn(0, 0)
            with pe.Fori(0, TILES // 2 - 1) as i:
                for p in range(2):
                    turn(2 * i + p + 1, 1 - p)
                    gates(2 * i + p, p)
            turn(TILES - 1, 1)
            gates(TILES - 2, 0)
            gates(TILES - 1, 1)
            pe.wait_ge(s_alpha, 1)
            for b in range(B):
                ins = tr(pj[0][:, C * b:C * b + C], alpha_t[:, C * b:C * b + C], ident[:, :])
            ins.then_inc(s_arow, 1)
            pe.wait_ge(s_crow, 1)
            for b in range(B):
                ins = tr(pj[1][:, C * b:C * b + C], crow[:, b, :], ident[:, :])
            ins.then_inc(s_ccol, 1)
            pe.wait_ge(s_zero, 1)
            pe.wait_ge(s_ncum, 1)
            def wait_kx(step, c, u, g, a):
                k = KX_USES.index((step, c)) - 1
                while True:
                    kind, c0 = KX_USES[k]
                    if k < 0:
                        if g is not None:
                            pe.wait_ge(R_ready, g * GC + GC)
                        return
                    if (g if kind == "g" else a) is not None:
                        pe.wait_ge(KX_TAKEN[kind], (g if kind == "g" else a) * HALVES
                                   + U * c0 + u + 1 + (HALVES if kind == "g" else 0))
                        return
                    k -= 1

            def prepare(step, arg, g, a, par):
                def project(n):
                    t = order[n]
                    if n >= 2:
                        pe.wait_ge(raw_ready, a * NT + n - 1)
                    else:
                        pe.wait_ge(zg_ready, a * HALVES + U * (GC - 1) + n + 1)
                    w = slice(128 * t, 128 * t + 128)
                    cols = ds(column(a, 0) - PAD, W)
                    o = pj[n % 2][:, 0:W]
                    mm(o, wq_hi[:, w], xflat(xn_hi)[:, cols], start=True, stop=False)
                    mm(o, wq_lo[:, w], xflat(xn_hi)[:, cols], start=False, stop=False)
                    mm(o, wq_hi[:, w], xflat(xn_lo)[:, cols], start=False, stop=True).then_inc(proj_ready, 1)

                def by_head(c, u, lhs, rhs_, done, need):
                    pe.wait_ge(conv_done, a * NT + need + HU * (u + 1) + RING)
                    wait_kx(step, c, u, g, a)
                    for h in range(HU):
                        hh = HU * u + h
                        o = heads(kx[u])[:, h, :]
                        cs = slice(C * c, C * c + C)
                        if rhs_ is None:
                            ins = tr(o, lhs[:, hh, cs], ident[:, :])
                        else:
                            ins = mm(o, lhs[:, hh, cs], rhs_[:, hh, cs], start=True, stop=True)
                    ins.then_inc(done, 1)

                if step == "begin":
                    project(0)
                    project(1)
                elif step == "conv" and arg[0] + AHEAD + 2 < NT:
                    project(arg[0] + AHEAD + 2)
                elif step == "kk":
                    for u in range(U):
                        by_head(arg[0], u, kT[par], kT[par], kk_ready, 0)
                elif step == "ktr":
                    for u in range(U):
                        by_head(arg[0], u, kT[par], None, ktr_ready, 0)
                elif step == "kq":
                    for u in range(U):
                        by_head(arg[0], u, kT[par], qT[par], kq_ready, 2 * H)
                elif step == "vtr":
                    for u in range(U):
                        by_head(arg[0], u, vT, None, vtr_ready, H)
                elif step == "z":
                    c, = arg
                    for u in range(U):
                        if c == 0:
                            pe.wait_ge(raw_ready, a * NT + NT - 1 + u)
                        else:
                            pe.wait_ge(zg_ready, a * HALVES + U * (c - 1) + u + 1 + HALVES)
                        cols = ds(column(a, c), C)
                        hi, lo = xflat(xn_hi)[:, cols], xflat(xn_lo)[:, cols]
                        w = slice(512 * u, 512 * u + 512)
                        mm(pj[u][:, :], hi, wz_hi[:, w], start=True, stop=False)
                        mm(pj[u][:, :], hi, wz_lo[:, w], start=False, stop=False)
                        mm(pj[u][:, :], lo, wz_hi[:, w], start=False, stop=True).then_inc(z_mm, 1)

            def merge(g, c, hop):
                k = g * GC + c
                y_bank, r_bank = merge_banks[c]
                if hop == 0:
                    pe.wait_ge(t_in, g * (16 * GC * NB) + 16 * GC * NB)
                    pe.wait_ge(rdiag, k + 1)
                    if c == 0:
                        pe.wait_ge(x2_ready, k + 1)
                    else:
                        pe.wait_ge(v_ready, g * HALVES + HALVES)
                    carry(y_bank[0:2 * H, 0:2 * H])
                    py = y_bank[:, 0:H * BLK].rearrange("p (h c) -> p h c", h=H)
                    for h in range(H):
                        mm(py[32:64, h], Nm[0:32, c, h, 32:64], T64[0:32, c, h, 0:32], start=True, stop=True)
                        ins = mm(py[96:128, h], Nm[64:96, c, h, 96:128], T32[64:96, c, h, :], start=True, stop=True)
                    ins.then_inc(y32_mm, 1)
                elif hop == 1:
                    pe.wait_ge(y32_sb, k + 1)
                    if c == 0:
                        pe.wait_ge(g_ready, g * HALVES + U)
                    carry(r_bank[96:96 + 2 * H, 0:2 * H])
                    pr = r_bank[:, 0:H * BLK].rearrange("p (h c) -> p h c", h=H)
                    for h in range(H):
                        mm(pr[0:32, h], Y32[c][32:64, h, :], R[32:64, c, h, 32:64], start=True, stop=True)
                        mm(pr[32:64, h], R[32:64, c, h, 32:64], Y32[c][32:64, h, :], start=True, stop=True)
                        ins = mm(pr[64:96, h], Y32[c][96:128, h, :], R[96:128, c, h, 96:128], start=True, stop=True)
                    ins.then_inc(r32_mm, 1)
                elif hop == 2:
                    pe.wait_ge(r32_sb, k + 1)
                    carry(y_bank[0:2 * H, 0:2 * H])
                    py = y_bank[64:128, :].rearrange("p (h c) -> p h c", h=H)
                    for h in range(H):
                        ins = mm(py[:, h], Nm[0:64, c, h, 64:128], T64[0:64, c, h, :], start=True, stop=True)
                    ins.then_inc(y64_mm, 1)
                else:
                    pe.wait_ge(y64_sb, k + 1)
                    carry(r_bank[96:96 + 2 * H, 0:2 * H])
                    pr = r_bank[0:64, :].rearrange("p (h c) -> p h c", h=H)
                    for h in range(H):
                        ins = mm(pr[:, h], Y64[c][64:128, h, :], R[64:128, c, h, 64:128], start=True, stop=True)
                    ins.then_inc(r64_mm, 1)

            def finish(step, arg, g, a, par):
                if step == "merge":
                    merge(g, *arg)
                elif step == "ks":
                    c, = arg
                    for u in range(U):
                        pe.wait_ge(S_ready, g * HALVES + U * c + u + 1)
                        for h in range(HU):
                            hh = HU * u + h
                            ins = mm(heads(rc[u])[:, h, :], kT[1 - par][:, hh, C * c:C * c + C], S[:, c, hh, :],
                                     start=True, stop=True)
                        ins.then_inc(ks_mm, 1)
                elif step == "u":
                    c, = arg
                    pe.wait_ge(R_ready, g * GC + c + 1)
                    for u in range(U):
                        pe.wait_ge(rhs_ready, g * HALVES + U * c + u + 1)
                        for h in range(HU):
                            hh = HU * u + h
                            ins = mm(heads(rc[u])[:, h, :], R[:, c, hh, :], rhs[:, hh, :], start=True, stop=True)
                        ins.then_inc(u_mm, 1)
                elif step == "sd":
                    c, = arg
                    for u in range(U):
                        pe.wait_ge(u_ready, g * HALVES + U * c + u + 1)
                        pe.wait_ge(kd_ready, g * HALVES + U * c + u + 1)
                        for h in range(HU):
                            hh = HU * u + h
                            ins = mm(heads(rc[u])[:, h, :], kd[:, c, hh, :], Us[:, hh, :], start=True, stop=True)
                        ins.then_inc(sd_mm, 1)
                elif step == "o":
                    c, = arg
                    pe.wait_ge(aq_ready, g * GC + c + 1 + GC)
                    pe.wait_ge(R_ready, g * GC + GC)
                    pe.wait_ge(x2_ready, g * GC + c + 1)
                    for u in range(U):
                        pe.wait_ge(u_ready, g * HALVES + U * c + u + 1)
                        pe.wait_ge(at_ready, g * HALVES + U * c + u + 1)
                        pe.wait_ge(g_ready, g * HALVES + U * c + u + 1)
                        for h in range(HU):
                            hh = HU * u + h
                            o = heads(ob[u])[:, h, :]
                            mm(o, qT[1 - par][:, hh, C * c:C * c + C], S[:, c, hh, :], start=True, stop=False)
                            ins = mm(o, AT[:, c, hh, :], Us[:, hh, :], start=False, stop=True)
                        ins.then_inc(o_mm, 1)
                elif step == "g":
                    c, = arg
                    for u in range(U):
                        pe.wait_ge(g_ready, g * HALVES + U * c + u + 1 + U)
                        wait_kx(step, c, u, g, a)
                        for h in range(HU):
                            ins = tr(heads(kx[u])[:, h, :], G[:, HU * u + h, :], ident[:, :])
                        ins.then_inc(gtr_mm, 1)
                elif step == "out":
                    c, = arg
                    pe.wait_ge(gt_ready, g * HALVES + U * c + 2 + HALVES)
                    for hh in range(H):
                        ins = mm(ob[0][:, 0:D], GTs[:, hh, :], ow[:, hh, :], start=(hh == 0), stop=(hh == H - 1))
                    ins.then_inc(out_mm, 1)

            def stages(g, a, par):
                for step, *arg in STEPS:
                    if g is not None:
                        finish(step, arg, g, a, par)
                    if a is not None:
                        prepare(step, arg, g, a, par)

            stages(None, 0, 0)
            with pe.Fori(0, (NG - 1) // 2) as i:
                stages(2 * i, 2 * i + 1, 1)
                stages(2 * i + 1, 2 * i + 2, 0)
            stages(NG - 2, NG - 1, 1)
            stages(NG - 1, None, 0)
            pe.wait_ge(f_small, 64)
            pe.wait_ge(f_wlo, 2 * NE)
            pe.sem_inc(f_y_mm, 2)

            def up(i, e, par):
                for f in range(NF):
                    n = e * NF + f
                    if not (isinstance(i, int) and i == 0 and n < NF):
                        pe.wait_ge(f_relu, i * (NE * NF) + n + 1 - NF)
                    w = slice(128 * f, 128 * f + 128)
                    mm(h_bank[f][:, :], w1_hi[:, e, w], x2_hi[par][:, :], start=True, stop=False)
                    mm(h_bank[f][:, :], w1_lo[:, e, w], x2_hi[par][:, :], start=False, stop=False)
                    mm(h_bank[f][:, :], w1_hi[:, e, w], x2_lo[par][:, :], start=False, stop=True).then_inc(f_h_mm, 1)

            def down(i, e):
                pe.wait_ge(f_lo, i * (NE * NF) + e * NF + NF + NF)
                if not (isinstance(i, int) and i == 0 and e == 0):
                    pe.wait_ge(f_y, i * NE + e)
                for j in range(TW):
                    t = slice(C * j, C * j + C)
                    o = rc[e % 2][:, D * j:D * j + D]
                    for f in range(NF):
                        w = slice(D * f, D * f + D)
                        mm(o, h_hi[:, e % 2, f, t], w2_hi[:, e, w], start=(f == 0), stop=False)
                        mm(o, h_hi[:, e % 2, f, t], w2_lo[:, e, w], start=False, stop=False)
                        ins = mm(o, h_lo[:, e % 2, f, t], w2_hi[:, e, w], start=False, stop=(f == NF - 1))
                ins.then_inc(f_y_mm, 1)

            def tile_stages(i, r, par):
                for step, *arg in FSTEPS:
                    if step == "expert" and i is not None:
                        e, = arg
                        if e + 1 < NE:
                            up(i, e + 1, 1 - par)
                        elif r is not None:
                            up(r, 0, par)
                        down(i, e)
                    if r is None:
                        continue
                    if step == "turn":
                        pe.wait_ge(f_acc, r * 3 + 1)
                        for j in range(TW):
                            ins = tr(kx[0][:, C * j:C * j + C], xn2[:, j, :], ident[:, :])
                        ins.then_inc(f_xt, 1)
                    elif step == "logits":
                        pe.wait_ge(f_xlo, r + 1)
                        for j in range(TW):
                            ins = mm(kx[1][:, NE * j:NE * j + NE], x2T[:, C * j:C * j + C], rw[:, :], start=True, stop=True)
                        ins.then_inc(f_lg, 1)
                    elif step == "weights":
                        pe.wait_ge(f_acc, r * 3 + 2)
                        for j in range(TW):
                            ins = tr(kx[1][0:NE, C * j:C * j + C], wts[par][:, j, :], ident[:, :])
                        ins.then_inc(f_wt, 1)
                    elif step == "bias":
                        pe.wait_ge(f_wtsb, r + 1)
                        for j in range(TW):
                            ins = mm(kx[0][:, D * j:D * j + D], wT[0:NE, C * j:C * j + C], b2_sb[0:NE, :],
                                     start=True, stop=True)
                        ins.then_inc(f_b2, 1)
            tile_stages(None, 0, 0)
            up(0, 0, 0)
            with pe.Fori(0, (TILES - 1) // 2) as i:
                tile_stages(2 * i, 2 * i + 1, 1)
                tile_stages(2 * i + 1, 2 * i + 2, 0)
            tile_stages(TILES - 2, TILES - 1, 1)
            tile_stages(TILES - 1, None, 0)


def kernel(**inputs):
    import concourse.bacc as _bacc
    from concourse.bass_utils import run_bass_kernel_spmd as _run

    a = {k.replace("L0_", ""): np.asarray(v) for k, v in inputs.items()}
    t = lambda m: np.ascontiguousarray(m.T)
    NGROUPS, PER = 16, 8
    blk = 32
    par = np.zeros((2, 64, blk // 2, blk), np.float32)
    for p in range(2):
        for r in range(blk // 2):
            par[p, :, r, 2 * r + p] = 1.0
    keep = np.ones((128, NGROUPS), np.float32)
    keep[:, PER - 1::PER] = 0.0
    tri = np.broadcast_to(np.tril(np.ones((8, 8), np.float32), -1), (128, 8, 8))
    laid = [
        ("x", a["attn_hidden_states"]),
        ("qkv_t", t(a["attn_qkv_w"])),
        ("z_t", t(a["attn_z_w"])),
        ("ab_t", np.ascontiguousarray(np.concatenate([a["attn_b_w"], a["attn_a_w"]], 0).T)),
        ("conv_w", a["attn_conv_w"]),
        ("dt_bias", a["attn_dt_bias"]),
        ("a_log", a["attn_A_log"]),
        ("norm_w", a["attn_norm_w"]),
        ("out_t", t(a["attn_out_w"])),
        ("router_w", a["ffn_W_router"]),
        ("router_b", a["ffn_b_router"]),
        ("w1", a["ffn_W1"]),
        ("b1", a["ffn_b1"]),
        ("w2", a["ffn_W2"]),
        ("b2", a["ffn_b2"]),
        ("eye", np.eye(128, dtype=np.float32)),
        ("parity_eye", np.ascontiguousarray(par.reshape(128, blk // 2, blk))),
        ("low_tri", np.ascontiguousarray(tri)),
        ("keep", keep),
    ]
    nc = _bacc.Bacc("TRN2", target_bir_lowering=False, num_devices=1)
    arrays, args = {}, []
    for name, v in laid:
        v = np.ascontiguousarray(v)
        arrays[f"in_{name}"] = v
        args.append(nc.dram_tensor(f"in_{name}", v.shape, mybir.dt.from_np(v.dtype), kind="ExternalInput").ap())
    shape = a["attn_hidden_states"].shape
    args.append(nc.dram_tensor("out_0", shape, mybir.dt.float32, kind="ExternalOutput").ap())
    preln_delta_moe_kernel(nc, *args)
    r = _run(nc, [arrays], core_ids=[0])
    return r.results[0]["out_0"]
```
